# Optimizing a Trainium2 kernel written in Bass

```python
import numpy as np
import jax
import jax.numpy as jnp

def _softmax(x, axis=-1):
    return jax.nn.softmax(x, axis=axis)

def _gelu(x):
    return jax.nn.gelu(x, approximate=True)

def _silu(x):
    return jax.nn.silu(x)

def _sigmoid(x):
    return jax.nn.sigmoid(x)

def _layernorm(x, axis=-1, eps=1e-05):
    m = jnp.mean(x, axis=axis, keepdims=True)
    v = jnp.var(x, axis=axis, keepdims=True)
    return (x - m) / jnp.sqrt(v + eps)

def _scatter_add(tgt, idx, src, axis=0):
    return tgt.at[idx].add(src)

def _segment_sum(src, seg, n):
    return jax.ops.segment_sum(src, seg, n)
kernel_name = 'mk_gnn_resnorm_d4_gnn_r32_42fe6f'

def setup_inputs(seed: int=0):
    np.random.seed(seed)
    _w = jnp.asarray

    def _rec_inputs():
        import jax
        import jax.numpy as jnp
        _gk = jax.random.key(seed)
        x = -7.329e-05 + 0.9999 * jax.random.normal(jax.random.fold_in(_gk, 1), (3125, 256), jnp.float32)
        src = jax.random.randint(jax.random.fold_in(_gk, 2), (50000,), 0, 3125, jnp.int32)
        dst = jax.random.randint(jax.random.fold_in(_gk, 3), (50000,), 0, 3125, jnp.int32)
        _o = jnp.argsort(dst, stable=True)
        src = src[_o]
        dst = dst[_o]
        return (x, src, dst)
    x, src, dst = _rec_inputs()

    def _L0_gnn_setup():
        import jax, jax.numpy as jnp
        import numpy as np
        DIM = 256
        HIDDEN = 256
        NUM_ENT = 6250
        NUM_TRI = 6250
        NUM_EDGES = 18750
        key = jax.random.key(seed)
        k1, k2, k3, k4, k5 = jax.random.split(key, 5)
        entity_emb = jax.random.normal(k1, (NUM_ENT, DIM), dtype=jnp.float32)
        src_idx = jax.random.randint(k2, (NUM_EDGES,), 0, NUM_ENT, dtype=jnp.int64)
        dst_idx = jax.random.randint(k3, (NUM_EDGES,), 0, NUM_TRI, dtype=jnp.int64)
        entity_triangle_index = jnp.stack([src_idx, dst_idx], axis=0)
        bound = 1.0 / np.sqrt(DIM)
        W = jax.random.uniform(k4, (HIDDEN, DIM), minval=-bound, maxval=bound, dtype=jnp.float32)
        b = jax.random.uniform(k5, (HIDDEN,), minval=-bound, maxval=bound, dtype=jnp.float32)
        return {'entity_emb': entity_emb, 'entity_triangle_index': entity_triangle_index, 'num_triangles': NUM_TRI, 'W': W, 'b': b}
    _L0_gnn_all = _L0_gnn_setup()
    _L0_gnn_in = {k: v for k, v in _L0_gnn_all.items() if k in ('W', 'b')}
    del _L0_gnn_all

    def _L1_gnn_setup():
        import jax, jax.numpy as jnp
        import numpy as np
        N_NODES = 50000
        N_EDGES = 25000
        D_IN = 256
        D_OUT = 256
        BN_EPS = 1e-05
        L2_EPS = 1e-12
        key = jax.random.key(seed)
        ks = jax.random.split(key, 8)
        x = jax.random.normal(ks[0], (N_NODES, D_IN), dtype=jnp.float32)
        edge_index = jax.random.randint(ks[1], (2, N_EDGES), 0, N_NODES, dtype=jnp.int64)
        s = 1.0 / np.sqrt(D_IN)
        W_l = jax.random.uniform(ks[2], (D_OUT, D_IN), jnp.float32, -s, s)
        b_l = jax.random.uniform(ks[3], (D_OUT,), jnp.float32, -s, s)
        W_r = jax.random.uniform(ks[4], (D_OUT, D_IN), jnp.float32, -s, s)
        gamma = jnp.ones((D_OUT,), jnp.float32)
        beta = jnp.zeros((D_OUT,), jnp.float32)
        return {'x': x, 'edge_index': edge_index, 'W_l': W_l, 'b_l': b_l, 'W_r': W_r, 'gamma': gamma, 'beta': beta}
    _L1_gnn_all = _L1_gnn_setup()
    _L1_gnn_in = {k: v for k, v in _L1_gnn_all.items() if k in ('W_l', 'b_l', 'W_r', 'gamma', 'beta')}
    del _L1_gnn_all

    def _L2_gnn_setup():
        import jax, jax.numpy as jnp
        import numpy as np
        N, E, D, H, DK, DV, L, HUS = (625, 10000, 256, 8, 32, 32, 2, 1024)

        def _layer_norm(x, g, b, eps=1e-05):
            mu = jnp.mean(x, axis=-1, keepdims=True)
            var = jnp.mean((x - mu) ** 2, axis=-1, keepdims=True)
            return (x - mu) * jax.lax.rsqrt(var + eps) * g + b

        def _ga_layer(h, src, dst, Wq, Wk, Wv, Wo, g, b):
            n = h.shape[0]
            q = (h @ Wq).reshape(n, H, DK)
            k = (h @ Wk).reshape(n, H, DK)
            v = (h @ Wv).reshape(n, H, DV)
            e = jnp.sum(q[dst] * k[src], axis=-1) / np.sqrt(DK).astype(np.float32)
            m = jax.ops.segment_max(e, dst, num_segments=n)
            a = jnp.exp(e - m[dst])
            z = jax.ops.segment_sum(a, dst, num_segments=n)
            alpha = a / (z[dst] + 1e-09)
            msg = v[src] * alpha[:, :, None]
            agg = jax.ops.segment_sum(msg, dst, num_segments=n).reshape(n, H * DV)
            out = agg @ Wo
            return _layer_norm(out + h, g, b)
        key = jax.random.key(seed)
        ks = jax.random.split(key, 12)
        s = 0.02
        return {'h': jax.random.normal(ks[0], (N, D), jnp.float32), 'src': jax.random.randint(ks[1], (E,), 0, N, jnp.int32), 'dst': jax.random.randint(ks[2], (E,), 0, N, jnp.int32), 'Wq': jax.random.normal(ks[3], (L, D, H * DK), jnp.float32) * s, 'Wk': jax.random.normal(ks[4], (L, D, H * DK), jnp.float32) * s, 'Wv': jax.random.normal(ks[5], (L, D, H * DV), jnp.float32) * s, 'Wo': jax.random.normal(ks[6], (L, H * DV, D), jnp.float32) * s, 'ln_g': jnp.ones((L, D), jnp.float32), 'ln_b': jnp.zeros((L, D), jnp.float32), 'w1': jax.random.normal(ks[7], (D, HUS), jnp.float32) * s, 'b1': jnp.zeros((HUS,), jnp.float32), 'w2': jax.random.normal(ks[8], (HUS, D), jnp.float32) * s, 'b2': jnp.zeros((D,), jnp.float32)}
    _L2_gnn_all = _L2_gnn_setup()
    _L2_gnn_in = {k: v for k, v in _L2_gnn_all.items() if k in ('Wq', 'Wk', 'Wv', 'Wo', 'ln_g', 'ln_b', 'w1', 'b1', 'w2', 'b2')}
    del _L2_gnn_all

    def _L3_gnn_setup():
        import jax, jax.numpy as jnp
        import numpy as np
        V = 6250
        E = 18750
        INPUT_DIM = 256
        OUTPUT_DIM = 256
        SUPPORT_DIM = 128
        key = jax.random.key(seed)
        k1, k2, k3 = jax.random.split(key, 3)
        verts = jax.random.normal(k1, (V, INPUT_DIM), dtype=jnp.float32)
        edges = jax.random.randint(k2, (E, 2), 0, V, dtype=jnp.int64)
        kw0, kw1 = jax.random.split(k3)
        w0_w = jax.random.normal(kw0, (OUTPUT_DIM, INPUT_DIM), dtype=jnp.float32) * 0.01
        w0_b = jnp.zeros((OUTPUT_DIM,), dtype=jnp.float32)
        w1_w = jax.random.normal(kw1, (SUPPORT_DIM, INPUT_DIM), dtype=jnp.float32) * 0.01
        w1_b = jnp.zeros((SUPPORT_DIM,), dtype=jnp.float32)
        return {'verts': verts, 'edges': edges, 'w0_w': w0_w, 'w0_b': w0_b, 'w1_w': w1_w, 'w1_b': w1_b}
    _L3_gnn_all = _L3_gnn_setup()
    _L3_gnn_in = {k: v for k, v in _L3_gnn_all.items() if k in ('w0_w', 'w0_b', 'w1_w', 'w1_b')}
    del _L3_gnn_all
    return {'x': x, 'src': src, 'dst': dst, 'L0_gnn_W': _L0_gnn_in['W'], 'L0_gnn_b': _L0_gnn_in['b'], 'L1_gnn_W_l': _L1_gnn_in['W_l'], 'L1_gnn_b_l': _L1_gnn_in['b_l'], 'L1_gnn_W_r': _L1_gnn_in['W_r'], 'L1_gnn_gamma': _L1_gnn_in['gamma'], 'L1_gnn_beta': _L1_gnn_in['beta'], 'L2_gnn_Wq': _L2_gnn_in['Wq'], 'L2_gnn_Wk': _L2_gnn_in['Wk'], 'L2_gnn_Wv': _L2_gnn_in['Wv'], 'L2_gnn_Wo': _L2_gnn_in['Wo'], 'L2_gnn_ln_g': _L2_gnn_in['ln_g'], 'L2_gnn_ln_b': _L2_gnn_in['ln_b'], 'L2_gnn_w1': _L2_gnn_in['w1'], 'L2_gnn_b1': _L2_gnn_in['b1'], 'L2_gnn_w2': _L2_gnn_in['w2'], 'L2_gnn_b2': _L2_gnn_in['b2'], 'L3_gnn_w0_w': _L3_gnn_in['w0_w'], 'L3_gnn_w0_b': _L3_gnn_in['w0_b'], 'L3_gnn_w1_w': _L3_gnn_in['w1_w'], 'L3_gnn_w1_b': _L3_gnn_in['w1_b']}

def reference(x, src, dst, L0_gnn_W, L0_gnn_b, L1_gnn_W_l, L1_gnn_b_l, L1_gnn_W_r, L1_gnn_gamma, L1_gnn_beta, L2_gnn_Wq, L2_gnn_Wk, L2_gnn_Wv, L2_gnn_Wo, L2_gnn_ln_g, L2_gnn_ln_b, L2_gnn_w1, L2_gnn_b1, L2_gnn_w2, L2_gnn_b2, L3_gnn_w0_w, L3_gnn_w0_b, L3_gnn_w1_w, L3_gnn_w1_b):
    import jax
    import jax.numpy as jnp

    def _L0_gnn_ref(entity_emb, entity_triangle_index, num_triangles, W, b):
        import jax, jax.numpy as jnp
        import numpy as np
        DIM = 256
        HIDDEN = 256
        NUM_ENT = 6250
        NUM_TRI = 6250
        NUM_EDGES = 18750
        src_idx = entity_triangle_index[0]
        dst_idx = entity_triangle_index[1]
        msgs = entity_emb[src_idx]
        agg = jax.ops.segment_sum(msgs, dst_idx, num_segments=num_triangles)
        counts = jax.ops.segment_sum(jnp.ones((src_idx.shape[0],), dtype=entity_emb.dtype), dst_idx, num_segments=num_triangles)
        agg = jnp.where(counts[:, None] > 0, agg / jnp.maximum(counts, 1.0)[:, None], agg)
        tri_out = jax.nn.relu(agg @ W.T + b)
        return tri_out

    def _L1_gnn_ref(x, edge_index, W_l, b_l, W_r, gamma, beta):
        import jax, jax.numpy as jnp
        import numpy as np
        N_NODES = 50000
        N_EDGES = 25000
        D_IN = 256
        D_OUT = 256
        BN_EPS = 1e-05
        L2_EPS = 1e-12
        N = x.shape[0]
        src = edge_index[0]
        dst = edge_index[1]
        agg = jax.ops.segment_sum(x[src], dst, num_segments=N)
        deg = jax.ops.segment_sum(jnp.ones_like(src, dtype=x.dtype), dst, num_segments=N)
        mean = agg / jnp.maximum(deg, 1.0)[:, None]
        out = mean @ W_l.T + b_l + x @ W_r.T
        nrm = jnp.sqrt(jnp.sum(out * out, axis=-1, keepdims=True))
        out = out / jnp.maximum(nrm, L2_EPS)
        mu = jnp.mean(out, axis=0)
        var = jnp.mean((out - mu) ** 2, axis=0)
        out = (out - mu) / jnp.sqrt(var + BN_EPS) * gamma + beta
        return jax.nn.relu(out)

    def _L2_gnn_ref(h, src, dst, Wq, Wk, Wv, Wo, ln_g, ln_b, w1, b1, w2, b2):
        import jax, jax.numpy as jnp
        import numpy as np
        N, E, D, H, DK, DV, L, HUS = (625, 10000, 256, 8, 32, 32, 2, 1024)

        def _layer_norm(x, g, b, eps=1e-05):
            mu = jnp.mean(x, axis=-1, keepdims=True)
            var = jnp.mean((x - mu) ** 2, axis=-1, keepdims=True)
            return (x - mu) * jax.lax.rsqrt(var + eps) * g + b

        def _ga_layer(h, src, dst, Wq, Wk, Wv, Wo, g, b):
            n = h.shape[0]
            q = (h @ Wq).reshape(n, H, DK)
            k = (h @ Wk).reshape(n, H, DK)
            v = (h @ Wv).reshape(n, H, DV)
            e = jnp.sum(q[dst] * k[src], axis=-1) / np.sqrt(DK).astype(np.float32)
            m = jax.ops.segment_max(e, dst, num_segments=n)
            a = jnp.exp(e - m[dst])
            z = jax.ops.segment_sum(a, dst, num_segments=n)
            alpha = a / (z[dst] + 1e-09)
            msg = v[src] * alpha[:, :, None]
            agg = jax.ops.segment_sum(msg, dst, num_segments=n).reshape(n, H * DV)
            out = agg @ Wo
            return _layer_norm(out + h, g, b)
        for l in range(Wq.shape[0]):
            h = _ga_layer(h, src, dst, Wq[l], Wk[l], Wv[l], Wo[l], ln_g[l], ln_b[l])
        return jax.nn.relu(h @ w1 + b1) @ w2 + b2

    def _L3_gnn_ref(verts, edges, w0_w, w0_b, w1_w, w1_b):
        import jax, jax.numpy as jnp
        import numpy as np
        V = 6250
        E = 18750
        INPUT_DIM = 256
        OUTPUT_DIM = 256
        SUPPORT_DIM = 128
        verts_w0 = verts @ w0_w.T + w0_b
        verts_w1 = verts @ w1_w.T + w1_b
        src = jnp.concatenate([edges[:, 1], edges[:, 0]])
        dst = jnp.concatenate([edges[:, 0], edges[:, 1]])
        neighbor_sums = jax.ops.segment_sum(verts_w1[src], dst, num_segments=verts.shape[0])
        pad = verts_w0.shape[1] - neighbor_sums.shape[1]
        out = verts_w0 + jnp.pad(neighbor_sums, ((0, 0), (0, pad)))
        return out
    edge_index = jnp.stack([src, dst])
    edge_index_t = jnp.stack([src, dst], axis=1)
    x = _layernorm(x + _L0_gnn_ref(x, edge_index, 3125, L0_gnn_W, L0_gnn_b), axis=-1)
    x = _layernorm(x + _L1_gnn_ref(x, edge_index, L1_gnn_W_l, L1_gnn_b_l, L1_gnn_W_r, L1_gnn_gamma, L1_gnn_beta), axis=-1)
    x = _layernorm(x + _L2_gnn_ref(x, src, dst, L2_gnn_Wq, L2_gnn_Wk, L2_gnn_Wv, L2_gnn_Wo, L2_gnn_ln_g, L2_gnn_ln_b, L2_gnn_w1, L2_gnn_b1, L2_gnn_w2, L2_gnn_b2), axis=-1)
    x = _layernorm(x + _L3_gnn_ref(x, edge_index_t, L3_gnn_w0_w, L3_gnn_w0_b, L3_gnn_w1_w, L3_gnn_w1_b), axis=-1)
    return x

_drawn_inputs = setup_inputs


def setup_inputs(seed=0):
    import zlib

    import numpy as np

    out = dict(_drawn_inputs(seed))
    spreads = {'L1_gnn_gamma': (1.0, 0.2),
     'L1_gnn_beta': (0.0, 0.1),
     'L2_gnn_ln_g': (1.0, 0.6),
     'L2_gnn_ln_b': (0.0, 0.405),
     'L2_gnn_b1': (0.0, 0.1),
     'L2_gnn_b2': (0.0, 0.1),
     'L3_gnn_w0_b': (0.0, 0.1),
     'L3_gnn_w1_b': (0.0, 0.1)}
    factors = {'L1_gnn_b_l': 27.398,
     'L2_gnn_Wq': 8.0,
     'L2_gnn_Wk': 8.0,
     'L2_gnn_Wv': 8.0,
     'L2_gnn_Wo': 8.0}
    for name, (base, spread) in spreads.items():
        noise = np.random.default_rng([zlib.crc32(name.encode()), seed]).standard_normal(out[name].shape)
        drawn = base * np.exp(spread * noise) if base else spread * noise
        out[name] = jnp.asarray(drawn.astype(out[name].dtype))
    for name, factor in factors.items():
        out[name] = (out[name] * factor).astype(out[name].dtype)
    return out
```

```python
from contextlib import ExitStack

import concourse.bass as bass
from concourse import mybir

F32 = mybir.dt.float32
I32 = mybir.dt.int32
ALU = mybir.AluOpType
ACT = mybir.ActivationFunctionType
AX_X = mybir.AxisListType.X

P = 128
N = 3125
E = 50000
D = 256
H, DK = 8, 32
HZ = DK + 1
W = H * HZ
KV = W + D
SCALE = DK ** -0.5
HID = 1024
SUP = 128
NB = -(-N // P)
NP = NB * P
NT = -(-E // P)
CH = -(-NT // P)
EC = CH * P * P
G = 8
SLOTS = 4
NBATCH = -(-(NT + NB - 1) // (G * SLOTS)) * SLOTS
K = NBATCH * G
LAST = N - (NB - 1) * P
BIG = 1e30
LN_EPS = 1e-5
COPIES = 4


class Named:
    pass


def over_batches(eng, step, lag=0):
    for i in range(SLOTS):
        step(i, i)
    with eng.Fori(1, NBATCH // SLOTS) as n:
        for slot in range(SLOTS):
            step(n * SLOTS + slot, slot)
    for i in range(NBATCH, NBATCH + lag):
        step(i, i % SLOTS)


def over_bins(eng, step, lag=0):
    for b in range(4):
        step(b, b % 2)
    with eng.Fori(2, (NB - 1) // 2) as n:
        for parity in range(2):
            step(n * 2 + parity, parity)
    for b in range((NB - 1) // 2 * 2, NB + lag):
        step(b, b % 2)


def runs(b):
    return not isinstance(b, int) or 0 <= b < NB


def sem_maker(nc, ctx, phase):
    made = []

    def sem(name):
        made.append(nc.alloc_semaphore(f"{phase}_{name}"))
        return made[-1]

    def clear():
        nc.clear_and_free_semaphores(made)
        nc.all_engine_barrier()

    ctx.callback(clear)
    return sem


def load_edges(nc, t, d):
    with ExitStack() as ctx:
        sem = sem_maker(nc, ctx, "le")
        falls = ctx.enter_context(nc.sbuf_tensor("falls", [P, CH, P], F32))
        fall_count = ctx.enter_context(nc.sbuf_tensor("fall_count", [P, 1], F32))
        loaded = sem("loaded")
        compared = sem("compared")
        counted = sem("counted")
        summed = sem("summed")
        ones_ready = sem("ones_ready")
        block = ctx.enter_context(nc.Block())

        @block.sync
        def _(sp):
            for tile, flat in ((t.dst_i, d.dst[1:1 + EC]), (t.prev_i, d.dst[0:EC]), (t.src_now, d.src)):
                sp.dma_start(tile[:, :, :], flat.rearrange("(c p e) -> p c e", c=CH, p=P)).then_inc(loaded, 16)
            sp.wait_ge(loaded, 48)

        @block.vector
        def _(dve):
            dve.memset(t.ones[:, :], 1.0).then_inc(ones_ready, 1)
            dve.wait_ge(loaded, 48)
            dve.tensor_tensor(falls[:, :, :], t.dst_i[:, :, :], t.prev_i[:, :, :], ALU.is_lt).then_inc(compared, 1)
            dve.wait_ge(compared, 1)
            dve.tensor_reduce(fall_count[:, :], falls[:, :, :], mybir.AxisListType.XY, ALU.add).then_inc(counted, 1)
            dve.wait_ge(summed, 1)
            dve.tensor_copy(t.unsorted[:, :], t.ps[0][0:1, 0:1])

        @block.tensor
        def _(pe):
            pe.wait_ge(ones_ready, 1)
            pe.wait_ge(counted, 1)
            pe.matmul(t.ps[0][:, 0:1], t.ones[:, :], fall_count[:, :], start=True, stop=True).then_inc(summed, 1)


def sort_edges(nc, t, d):
    CUT = 8
    PIECE = NT * P // CUT
    with ExitStack() as ctx:
        sem = sem_maker(nc, ctx, "sort")

        def sb(name, shape, dt=F32):
            return ctx.enter_context(nc.sbuf_tensor(name, shape, dt))

        records = sb("records", [P, CH, P, 2], I32)
        keys = sb("keys", [P, CH * P])
        rank = sb("rank", [P, CH * P])
        count = sb("count", [P, 1])
        tile_no = sb("key_tile_no", [P, CH])
        position = sb("position", [P, P])
        equal = sb("equal_keys", [P, P])
        lower = sb("equal_before", [P, P])
        head = sb("head", [1, 2], I32)
        place = sb("place", [P, 1], I32)
        record = sb("record", [P, 2], I32)
        flat = t.rows[:, :, :, :].rearrange("p a b c -> p (a b c)")
        piece = flat[:, 0:PIECE]
        smaller = flat[:, PIECE:2 * PIECE]

        numbered = sem("numbered")
        filled = sem("filled")
        keys_ready = sem("keys_ready")
        kept = sem("kept")
        piece_loaded = sem("piece_loaded")
        compared = sem("compared")
        ranked = sem("ranked")
        tied = sem("tied")
        staged = sem("staged")
        taken = sem("taken")
        sent = sem("sent")
        reloaded = sem("reloaded")
        split = sem("split")
        block = ctx.enter_context(nc.Block())

        @block.gpsimd
        def _(pool):
            f = dict(allow_small_or_imprecise_dtypes=True)
            pool.iota(tile_no[:, :], [[P, CH]], base=0, channel_multiplier=1, **f).then_inc(numbered, 1)
            pool.iota(position[:, :], [[1, P]], base=0, channel_multiplier=0, **f).then_inc(numbered, 1)
            unsorted = pool.value_load(t.unsorted[0:1, 0:1])
            with pool.If(unsorted > 0):
                pool.wait_ge(kept, 48)
                for c in range(CH):
                    tiles = min(P, NT - c * P)
                    with pool.Fori(0, P) as e:
                        pool.wait_ge(staged, (e + c * P) + 1)
                        pool.sem_inc(taken, 1)
                        pool.indirect_dma_start(d.records, bass.IndirectOffsetOnAxis(place[0:tiles, :], 0),
                                                record[0:tiles, :], None).then_inc(sent, 16)

        @block.sync
        def _(sp):
            unsorted = sp.value_load(t.unsorted[0:1, 0:1])
            with sp.If(unsorted > 0):
                sp.wait_ge(filled, 3)
                sp.dma_start(d.records[1:1 + EC, :].rearrange("(c p e) r -> p c (e r)", c=CH, p=P),
                             records[:, :, :, :].rearrange("p c e r -> p c (e r)")).then_inc(kept, 16)
                sp.dma_start(d.records[0:1, :], head[:, :]).then_inc(kept, 16)
                sp.wait_ge(keys_ready, 1)
                sp.dma_start(d.keys.rearrange("(c p e) -> p c e", c=CH, p=P),
                             keys[:, :].rearrange("p (c e) -> p c e", c=CH)).then_inc(kept, 16)
                sp.wait_ge(kept, 48)
                for q in range(CUT):
                    if q >= 1:
                        sp.wait_ge(compared, q * CH * P)
                    sp.dma_start(piece, d.keys[q * PIECE:(q + 1) * PIECE].partition_broadcast(P)
                                 ).then_inc(piece_loaded, 16)
                sp.wait_ge(sent, 16 * CH * P)
                for n, tile in enumerate((1, 0)):
                    if n:
                        sp.wait_ge(split, 2)
                    sp.dma_start(records[:, :, :, :].rearrange("p c e r -> p c (e r)"),
                                 d.records[tile:tile + EC, :].rearrange("(c p e) r -> p c (e r)", c=CH, p=P)
                                 ).then_inc(reloaded, 16)
                sp.wait_ge(reloaded, 32)

        @block.vector
        def _(dve):
            dve.wait_ge(numbered, 2)
            unsorted = dve.value_load(t.unsorted[0:1, 0:1])
            with dve.If(unsorted > 0):
                dve.tensor_copy(records[:, :, :, 0], t.dst_i[:, :, :]).then_inc(filled, 1)
                dve.tensor_copy(records[:, :, :, 1], t.src_now[:, :, :]).then_inc(filled, 1)
                dve.memset(head[:, :], -1).then_inc(filled, 1)
                dve.memset(rank[:, :], 1.0)
                for c in range(CH):
                    ins = dve.tensor_scalar(keys[:, c * P:(c + 1) * P], t.dst_i[:, c, :], float(CH * P),
                                            tile_no[:, c:c + 1], ALU.mult, ALU.add)
                ins.then_inc(keys_ready, 1)
                dve.wait_ge(keys_ready, 1)
                for q in range(CUT):
                    dve.wait_ge(piece_loaded, 16 * (q + 1))
                    with dve.Fori(0, CH * P) as e:
                        at = e + q * CH * P
                        dve.wait_ge(ranked, at)
                        dve.tensor_scalar(smaller, piece, keys[:, bass.ds(e, 1)], 0.0, ALU.is_lt, ALU.add,
                                          accum_out=count[:, :]).then_inc(compared, 1)
                        dve.wait_ge(compared, at + 1)
                        dve.tensor_tensor(rank[:, bass.ds(e, 1)], rank[:, bass.ds(e, 1)], count[:, :], ALU.add
                                          ).then_inc(ranked, 1)
                for c in range(CH):
                    with dve.Fori(0, P) as e:
                        at = e + c * P
                        dve.wait_ge(ranked, at + CUT * CH * P)
                        dve.tensor_scalar(equal[:, :], keys[:, c * P:(c + 1) * P], keys[:, bass.ds(at, 1)], None,
                                          ALU.is_equal).then_inc(tied, 1)
                        dve.wait_ge(tied, at * 2 + 1)
                        dve.scalar_tensor_tensor(out=lower[:, :], in0=position[:, :], scalar=position[:, bass.ds(e, 1)],
                                                 in1=equal[:, :], op0=ALU.is_lt, op1=ALU.mult,
                                                 accum_out=count[:, :]).then_inc(tied, 1)
                        dve.wait_ge(tied, at * 2 + 2)
                        dve.tensor_tensor(rank[:, bass.ds(at, 1)], rank[:, bass.ds(at, 1)], count[:, :], ALU.add
                                          ).then_inc(ranked, 1)
                dve.wait_ge(ranked, (CUT + 1) * CH * P)
                for c in range(CH):
                    with dve.Fori(0, P) as e:
                        at = e + c * P
                        dve.wait_ge(sent, at * 16)
                        dve.tensor_scalar(place[:, :], rank[:, bass.ds(at, 1)], 1.0, None, ALU.mult)
                        dve.tensor_scalar(record[:, 0:1], t.dst_i[:, c, bass.ds(e, 1)], 1.0, None, ALU.mult)
                        dve.tensor_scalar(record[:, 1:2], t.src_now[:, c, bass.ds(e, 1)], 1.0, None, ALU.mult
                                          ).then_inc(staged, 1)
                dve.wait_ge(reloaded, 16)
                dve.tensor_copy(t.dst_i[:, :, :], records[:, :, :, 0]).then_inc(split, 1)
                dve.tensor_copy(t.src_now[:, :, :], records[:, :, :, 1]).then_inc(split, 1)
                dve.wait_ge(reloaded, 32)
                dve.tensor_copy(t.prev_i[:, :, :], records[:, :, :, 0])


def build_tables(nc, t, d):
    with ExitStack() as ctx:
        sem = sem_maker(nc, ctx, "tab")

        def sb(name, shape, dt=F32):
            return ctx.enter_context(nc.sbuf_tensor(name, shape, dt))

        dst_f = sb("dst_f", [P, CH, P])
        src_f = sb("src_f", [P, CH, P])
        seg_start = sb("seg_start", [P, CH, P])
        ends_i = sb("ends_i", [P, 2, CH], I32)
        first = sb("first", [P, CH])
        last = sb("last", [P, CH])
        real_tile = sb("real_tile", [P, CH])
        pairs = sb("pairs", [P, CH])
        pairs_before = sb("pairs_before", [P, CH])
        begin = sb("begin", [P, CH])
        end = sb("end", [P, CH])
        shift = sb("shift", [P, CH])
        iota_k = sb("iota_k", [P, K])
        tile_no = sb("tile_no", [P, CH])
        upper = sb("upper", [P, P])
        at_or_after = sb("at_or_after", [P, CH, K])
        sel = sb("sel", [P, CH, K])
        bin_f = sb("bin_f", [P, K])
        no_pair = sb("no_pair", [P, K])
        base = sb("base", [P, K])
        bias_rows = sb("bias_rows", [P, CH, P])
        zeros = sb("zeros", [P, 2048])

        xloaded = sem("x_loaded")
        consts = sem("consts")
        chain = sem("vector_chain")
        pairs_ready = sem("pairs_ready")
        begin_ready = sem("begin_ready")
        sel_ready = sem("sel_ready")
        bins_done = sem("bins_done")
        tables_done = sem("tables_done")
        bias_done = sem("bias_done")
        bias_copied = sem("bias_copied")
        zeroed = sem("zeroed")
        stored = sem("stored")
        block = ctx.enter_context(nc.Block())

        @block.sync
        def _(sp):
            sp.dma_start(t.x[:, :].rearrange("p (b f) -> p b f", b=NB),
                         d.x.rearrange("(b p) f -> p b f", p=P)).then_inc(xloaded, 16)
            sp.wait_ge(zeroed, 1)
            for r in range(COPIES):
                for at in range(0, NP + P, 2048):
                    rows = min(2048, NP + P - at)
                    sp.dma_start(d.reversed[r][at:at + rows, :].rearrange("(p a) n -> p (a n)", p=P),
                                 zeros[:, 0:rows * SUP // P]).then_inc(stored, 16)
            sp.wait_ge(bias_copied, CH)
            for c in range(CH):
                n = min(P, K - c * P)
                sp.dma_start(d.bias[c * P * P:(c * P + n) * P].rearrange("(k e) -> k e", e=P),
                             bias_rows[0:n, c, :]).then_inc(stored, 16)
            sp.wait_ge(xloaded, 16)
            sp.wait_ge(stored, (COPIES * 2 + CH) * 16)

        @block.gpsimd
        def _(pool):
            f = dict(allow_small_or_imprecise_dtypes=True)
            pool.memset(t.ident[:, :], 0.0).then_inc(consts, 1)
            pool.iota(t.node[:, :], [[1, P]], base=0, channel_multiplier=0, **f).then_inc(consts, 1)
            pool.iota(iota_k[:, :], [[1, K]], base=0, channel_multiplier=0, **f).then_inc(consts, 1)
            pool.iota(tile_no[:, :], [[P, CH]], base=0, channel_multiplier=1, **f).then_inc(consts, 1)
            pool.iota(t.spare[:, :], [[0, 1]], base=NP, channel_multiplier=1, **f).then_inc(consts, 1)
            pool.wait_ge(consts, 5)
            pool.affine_select(out=t.ident[:, :], in_=t.ident[:, :], compare_op=ALU.not_equal, fill=1.0,
                               base=0, pattern=[[-1, P]], channel_multiplier=1).then_inc(consts, 1)
            pool.affine_select(out=upper[:, :], in_=t.ones[:, :], compare_op=ALU.is_gt, fill=0.0,
                               base=0, pattern=[[1, P]], channel_multiplier=-1).then_inc(consts, 1)
            pool.affine_select(out=t.lower[:, :], in_=t.ones[:, :], compare_op=ALU.is_gt, fill=0.0,
                               base=0, pattern=[[-1, P]], channel_multiplier=1).then_inc(consts, 1)
            pool.memset(t.real[:, 0, :], 1.0).then_inc(consts, 1)
            pool.affine_select(out=t.real[:, 1, :], in_=t.ones[:, :], compare_op=ALU.is_gt, fill=0.0,
                               base=LAST, pattern=[[0, P]], channel_multiplier=-1).then_inc(consts, 1)

        @block.vector
        def _(dve):
            n = [0]

            def done(ins):
                n[0] += 1
                ins.then_inc(chain, 1)
                dve.wait_ge(chain, n[0])

            dve.memset(zeros[:, :], 0.0).then_inc(zeroed, 1)
            dve.memset(t.eps[:, :], LN_EPS)
            for slot in range(SLOTS):
                for j in range(G):
                    dve.memset(t.rows[:, slot, j, D:D + 1], 1.0)
            dve.memset(t.acc[:, :], 0.0)
            dve.wait_ge(consts, 10)
            dve.tensor_copy(src_f[:, :, :], t.src_now[:, :, :])
            dve.tensor_copy(dst_f[:, :, :], t.dst_i[:, :, :])
            dve.tensor_tensor(seg_start[:, :, :], t.dst_i[:, :, :], t.prev_i[:, :, :], ALU.not_equal)
            dve.tensor_scalar(ends_i[:, 0, :], t.dst_i[:, :, 0], 7, None, ALU.arith_shift_right)
            done(dve.tensor_scalar(ends_i[:, 1, :], t.dst_i[:, :, P - 1], 7, None, ALU.arith_shift_right))
            dve.tensor_copy(first[:, :], ends_i[:, 0, :])
            dve.tensor_scalar(real_tile[:, :], tile_no[:, :], float(NT), None, ALU.is_lt)
            done(dve.tensor_scalar(last[:, :], ends_i[:, 1, :], 1.0, None, ALU.add))
            done(dve.tensor_tensor(pairs[:, :], last[:, :], first[:, :], ALU.subtract))
            done(dve.tensor_tensor(pairs[:, :], pairs[:, :], real_tile[:, :], ALU.mult))
            done(dve.memset(pairs_before[:, 0:1], 0.0))
            for c in range(1, CH):
                done(dve.tensor_tensor(pairs_before[:, c:c + 1], pairs_before[:, c - 1:c], pairs[:, c - 1:c], ALU.add))
            dve.tensor_copy(end[:, :], pairs[:, :]).then_inc(pairs_ready, 1)
            dve.wait_ge(begin_ready, 1)
            done(dve.tensor_copy(begin[:, :], t.ps[0][:, 0:CH]))
            dve.tensor_tensor(shift[:, :], first[:, :], begin[:, :], ALU.subtract)
            done(dve.tensor_tensor(end[:, :], begin[:, :], pairs[:, :], ALU.add))
            for c in range(CH):
                done(dve.tensor_scalar(at_or_after[:, c, :], iota_k[:, :], begin[:, c:c + 1], None, ALU.is_ge))
            for c in range(CH):
                dve.scalar_tensor_tensor(out=sel[:, c, :], in0=iota_k[:, :], scalar=end[:, c:c + 1],
                                         in1=at_or_after[:, c, :], op0=ALU.is_lt, op1=ALU.mult).then_inc(sel_ready, 1)
            dve.wait_ge(bins_done, 1)
            done(dve.tensor_tensor(base[:, :], t.ps[2][:, 0:K], iota_k[:, :], ALU.mult))
            done(dve.tensor_tensor(bin_f[:, :], t.ps[1][:, 0:K], base[:, :], ALU.add))
            dve.tensor_copy(t.bins[:, :], bin_f[0:1, :])
            dve.tensor_scalar(no_pair[:, :], t.ps[2][:, 0:K], -1.0, 1e6, ALU.add, ALU.mult)
            done(dve.tensor_scalar(base[:, :], bin_f[:, :], float(-P), None, ALU.mult))
            done(dve.tensor_tensor(base[:, :], base[:, :], no_pair[:, :], ALU.add))
            dve.wait_ge(tables_done, 1)
            dve.tensor_tensor(t.dst_at[:, :], t.ps[4][:, 0:K], base[:, :], ALU.add)
            dve.tensor_copy(t.src_i[:, :], t.ps[3][:, 0:K])
            dve.tensor_copy(t.src_at[:, :], t.ps[3][:, 0:K])
            for c in range(CH):
                m = min(P, K - c * P)
                dve.wait_ge(bias_done, c + 1)
                dve.tensor_scalar(bias_rows[0:m, c, :], t.ps[5 + c % 2][0:m, 0:P], -BIG, None,
                                  ALU.mult).then_inc(bias_copied, 1)

        @block.tensor
        def _(pe):
            pe.wait_ge(consts, 10)
            pe.wait_ge(pairs_ready, 1)
            pe.matmul(t.ps[0][:, 0:CH], upper[:, :], pairs[:, :], start=True, stop=False)
            pe.matmul(t.ps[0][:, 0:CH], t.ones[:, :], pairs_before[:, :], start=False, stop=True).then_inc(begin_ready, 1)
            pe.wait_ge(sel_ready, CH)
            for c in range(CH):
                pe.matmul(t.ps[1][:, 0:K], shift[:, c:c + 1].to_broadcast([P, P]), sel[:, c, :],
                          start=c == 0, stop=c == CH - 1)
            for c in range(CH):
                mm = pe.matmul(t.ps[2][:, 0:K], t.ones[:, :], sel[:, c, :], start=c == 0, stop=c == CH - 1)
            mm.then_inc(bins_done, 1)
            for out, table in ((t.ps[3], src_f), (t.ps[4], dst_f)):
                for c in range(CH):
                    mm = pe.matmul(out[:, 0:K], table[:, c, :], sel[:, c, :], start=c == 0, stop=c == CH - 1)
            mm.then_inc(tables_done, 1)
            for kc in range(CH):
                m = min(P, K - kc * P)
                if kc >= 2:
                    pe.wait_ge(bias_copied, kc - 1)
                for c in range(CH):
                    mm = pe.matmul(t.ps[5 + kc % 2][0:m, 0:P], sel[:, c, kc * P:kc * P + m], seg_start[:, c, :],
                                   start=c == 0, stop=c == CH - 1)
                mm.then_inc(bias_done, 1)


def aggregate(nc, t, d, phase, table, width, ones_column, find_twins=False):
    cols = width + ones_column
    with ExitStack() as ctx:
        sem = sem_maker(nc, ctx, phase)
        index_copied = sem("index_copied")
        index_taken = sem("index_taken")
        gathered = [sem(f"gathered{s}") for s in range(SLOTS)]
        onehot_ready = sem("onehot_ready")
        part_done = sem("part_done")
        added = sem("added")
        column_ready = sem("column_ready")
        row_ready = sem("row_ready")
        twins_counted = sem("twins_counted")
        twins_kept = sem("twins_kept")
        block = ctx.enter_context(nc.Block())

        @block.gpsimd
        def _(pool):
            def step(i, slot):
                if not isinstance(i, int) or i >= SLOTS:
                    pool.wait_ge(part_done, (i - SLOTS + 1) * G)
                pool.tensor_copy(t.index[:, slot, :], t.src_i[:, bass.ds(i * G, G)]).then_inc(index_copied, 1)
                pool.wait_ge(index_copied, i + 1)
                pool.sem_inc(index_taken, 1)
                for j in range(G):
                    pool.indirect_dma_start(t.rows[:, slot, j, 0:width], None, table,
                                            bass.IndirectOffsetOnAxis(t.index[:, slot, j:j + 1], 0)
                                            ).then_inc(gathered[slot], 16)
            over_batches(pool, step)

        @block.tensor
        def _(pe):
            def step(i, slot):
                pe.wait_ge(gathered[slot], (i - slot) * (16 * G // SLOTS) + 16 * G)
                for j in range(G):
                    k = i * G + j
                    pe.wait_ge(onehot_ready, k + 1)
                    two_back(pe, added, k)
                    pe.matmul(t.ps[j % 2][:, 0:cols], t.onehot[:, j % 4, :], t.rows[:, slot, j, 0:cols],
                              start=True, stop=True).then_inc(part_done, 1)
                    if find_twins:
                        pe.wait_ge(column_ready, i + 1)
                        two_back(pe, twins_counted, k)
                        pe.matmul(t.ps[2 + j % 2][:, 0:P], t.column[:, slot % 2, j:j + 1].to_broadcast([P, P]),
                                  t.ident[:, :], start=True, stop=True).then_inc(row_ready, 1)
            over_batches(pe, step)

        @block.vector
        def _(dve):
            def add(k, j):
                b = dve.value_load(t.bins[0:1, bass.ds(k, 1)], min_val=0, max_val=NB - 1)
                dve.wait_ge(part_done, k + 1)
                acc = t.acc[:, bass.ds(b * W, cols)]
                if not isinstance(k, int) or k >= 1:
                    dve.wait_ge(added, k)
                dve.tensor_tensor(acc, t.ps[j % 2][:, 0:cols], acc, ALU.add).then_inc(added, 1)

            def count_twins(i, slot, j, k):
                dve.wait_ge(row_ready, k + 1)
                dve.scalar_tensor_tensor(out=t.work[:, j % 2, 0:P], in0=t.ps[2 + j % 2][:, 0:P],
                                         scalar=t.column[:, slot % 2, j:j + 1], in1=t.lower[:, :],
                                         op0=ALU.is_equal, op1=ALU.mult,
                                         accum_out=t.twin_count[:, slot % 2, j:j + 1]).then_inc(twins_counted, 1)

            def step(i, slot):
                if find_twins:
                    if not isinstance(i, int) or i >= 1:
                        dve.wait_ge(twins_counted, i * G)
                        dve.tensor_copy(t.twins[:, bass.ds((i - 1) * G, G)],
                                        t.twin_count[:, (slot - 1) % 2, :]).then_inc(twins_kept, 1)
                        dve.wait_ge(twins_kept, i)
                    dve.tensor_copy(t.column[:, slot % 2, :], t.src_at[:, bass.ds(i * G, G)]).then_inc(column_ready, 1)
                for j in range(G):
                    k = i * G + j
                    if not isinstance(k, int) or k >= 4:
                        dve.wait_ge(part_done, k - 3)
                    dve.tensor_scalar(t.onehot[:, j % 4, :], t.node[:, :], t.dst_at[:, bass.ds(k, 1)], None,
                                      ALU.is_equal).then_inc(onehot_ready, 1)
                    if not isinstance(k, int) or k >= 2:
                        add(k - 2, j)
                    if find_twins and j >= 1:
                        count_twins(i, slot, j - 1, k - 1)
                if find_twins:
                    count_twins(i, slot, G - 1, i * G + G - 1)
            over_batches(dve, step)
            add(K - 2, 0)
            add(K - 1, 1)
            if find_twins:
                dve.wait_ge(twins_counted, K)
                dve.tensor_copy(t.twins[:, K - G:K], t.twin_count[:, (SLOTS - 1) % 2, :])


def weights(nc, ctx, name, dram):
    tile = ctx.enter_context(nc.sbuf_tensor(f"sb_{name}", [P, dram.shape[0] // P, dram.shape[1]], F32))
    return tile, tile[:, :, :], dram.rearrange("(c p) n -> p c n", p=P)


def vector(nc, ctx, name, dram):
    tile = ctx.enter_context(nc.sbuf_tensor(f"sb_{name}", [P, dram.shape[0]], F32))
    return tile, tile[:, :], dram.partition_broadcast(P)


def load(sp, loads, loaded):
    for _, tile, dram in loads:
        sp.dma_start(tile, dram).then_inc(loaded, 16)


def started(b, lag=0):
    return not isinstance(b, int) or 0 <= b - lag < NB


def two_back(eng, signal, b):
    if not isinstance(b, int) or b >= 2:
        eng.wait_ge(signal, b - 1)


def norm_sems(sem):
    norm = Named()
    norm.summed, norm.waited, norm.stats, norm.moments = sem("summed"), sem("waited"), sem("stats"), sem("moments")
    norm.std, norm.rstd, norm.normed = sem("std"), sem("rstd"), sem("normed")
    return norm


def norm_moments(dve, t, s, b, par):
    dve.wait_ge(s.summed, b + 1)
    dve.bn_stats(t.stats[:, par, :], t.s2[:, par, :]).then_inc(s.stats, 1)
    dve.wait_ge(s.stats, b + 1)
    dve.sem_inc(s.waited, 1)
    dve.bn_aggr(t.mv[:, par, :], t.stats[:, par, :]).then_inc(s.moments, 1)


def norm_std(act, t, s, b, par):
    act.wait_ge(s.moments, b + 1)
    act.activation(t.std[:, par, :], t.mv[:, par, 1:2], ACT.Sqrt, bias=t.eps[:, :]).then_inc(s.std, 1)


def norm_apply(dve, t, s, b, par, out):
    dve.wait_ge(s.std, b + 1)
    dve.reciprocal(t.rstd[:, par, :], t.std[:, par, :]).then_inc(s.rstd, 1)
    dve.wait_ge(s.rstd, b + 1)
    dve.tensor_scalar(out, t.s2[:, par, :], t.mv[:, par, 0:1], t.rstd[:, par, :],
                      ALU.subtract, ALU.mult).then_inc(s.normed, 1)


def turn(pe, t, src, par, signal, blocks=2):
    for c in range(blocks):
        mm = pe.transpose(t.ps[par][:, c * P:(c + 1) * P], src[:, c * P:(c + 1) * P], t.ident[:, :])
    mm.then_inc(signal, 1)


def store_bins(sp, t, src, stride, width, dram, ready, stored):
    def step(b, par):
        sp.wait_ge(ready, b + 1)
        sp.dma_start(dram[bass.ds(b * P, P), :], src[:, bass.ds(b * stride, width)]).then_inc(stored, 16)
    over_bins(sp, step)
    sp.wait_ge(stored, 16 * NB)


def dense0(nc, t, d):
    with ExitStack() as ctx:
        sem = sem_maker(nc, ctx, "d0")
        loads = [weights(nc, ctx, "W0", d.W0T), vector(nc, ctx, "b0", d.L0_gnn_b)]
        W0, b0 = (x[0] for x in loads)
        loaded = sem("loaded")
        degree = sem("degree")
        inverse = sem("inverse")
        mean_ready = sem("mean_ready")
        turned = sem("turned")
        turned_copied = sem("turned_copied")
        product_done = sem("product_done")
        biased = sem("biased")
        norm = norm_sems(sem)
        stored = sem("stored")
        block = ctx.enter_context(nc.Block())

        @block.vector
        def _(dve):
            dve.wait_ge(loaded, 32)

            def step(b, par):
                if started(b):
                    two_back(dve, turned, b)
                    dve.tensor_scalar(t.degree[:, par, :], t.acc[:, bass.ds(b * W + D, 1)], 1.0, None,
                                      ALU.max).then_inc(degree, 1)
                    dve.wait_ge(degree, b + 1)
                    dve.reciprocal(t.inv_deg[:, bass.ds(b, 1)], t.degree[:, par, :]).then_inc(inverse, 1)
                    dve.wait_ge(inverse, b + 1)
                    dve.tensor_scalar(t.work[:, par, 0:D], t.acc[:, bass.ds(b * W, D)], t.inv_deg[:, bass.ds(b, 1)],
                                      None, ALU.mult).then_inc(mean_ready, 1)
                if started(b, 1):
                    o, q = b - 1, 1 - par
                    dve.wait_ge(product_done, o + 1)
                    dve.tensor_tensor(t.s1[:, q, :], t.ps[2 + q][:, 0:D], b0[:, :], ALU.add).then_inc(biased, 1)
                    dve.wait_ge(biased, o + 1)
                    dve.scalar_tensor_tensor(out=t.s2[:, q, :], in0=t.s1[:, q, :], scalar=0.0,
                                             in1=t.x[:, bass.ds(o * D, D)], op0=ALU.max, op1=ALU.add
                                             ).then_inc(norm.summed, 1)
                    norm_moments(dve, t, norm, o, q)
                if started(b, 2):
                    norm_apply(dve, t, norm, b - 2, par, t.x[:, bass.ds((b - 2) * D, D)])
            over_bins(dve, step, lag=2)
            dve.memset(t.acc[:, :], 0.0)

        @block.tensor
        def _(pe):
            pe.wait_ge(loaded, 32)

            def step(b, par):
                if started(b):
                    pe.wait_ge(mean_ready, b + 1)
                    two_back(pe, turned_copied, b)
                    turn(pe, t, t.work[:, par, :], par, turned)
                if started(b, 1):
                    o, q = b - 1, 1 - par
                    pe.wait_ge(turned_copied, o + 1)
                    if not isinstance(b, int) or o >= 2:
                        pe.wait_ge(biased, o - 1)
                    for c in range(2):
                        mm = pe.matmul(t.ps[2 + q][:, 0:D], t.turned[:, q, c * P:(c + 1) * P], W0[:, c, :],
                                       start=c == 0, stop=c == 1)
                    mm.then_inc(product_done, 1)
            over_bins(pe, step, lag=1)

        @block.scalar
        def _(act):
            def step(b, par):
                if started(b):
                    act.wait_ge(turned, b + 1)
                    two_back(act, product_done, b)
                    act.copy(t.turned[:, par, 0:D], t.ps[par][:, 0:D]).then_inc(turned_copied, 1)
                if started(b, 1):
                    norm_std(act, t, norm, b - 1, 1 - par)
            over_bins(act, step, lag=1)

        @block.sync
        def _(sp):
            load(sp, loads, loaded)
            store_bins(sp, t, t.x, D, D, d.x1, norm.normed, stored)


def dense1(nc, t, d):
    with ExitStack() as ctx:
        sem = sem_maker(nc, ctx, "d1")
        loads = [weights(nc, ctx, "Wl", d.WlT), weights(nc, ctx, "Wr", d.WrT), vector(nc, ctx, "bl", d.L1_gnn_b_l),
                 vector(nc, ctx, "gamma", d.L1_gnn_gamma), vector(nc, ctx, "beta", d.L1_gnn_beta)]
        Wl, Wr, bl, gamma, beta = (x[0] for x in loads)
        col_mean = ctx.enter_context(nc.sbuf_tensor("col_mean", [P, D], F32))
        col_var = ctx.enter_context(nc.sbuf_tensor("col_var", [P, D], F32))
        loaded = sem("loaded")
        inputs_ready = sem("inputs_ready")
        turned = sem("turned")
        turned_copied = sem("turned_copied")
        product_done = sem("product_done")
        biased = sem("biased")
        squares_ready = sem("squares_ready")
        length_ready = sem("length_ready")
        length_kept = sem("length_kept")
        inverse = sem("inverse")
        unit_ready = sem("unit_ready")
        columns_summed = sem("columns_summed")
        column_mean = sem("column_mean")
        centred = sem("centred")
        squared = sem("squared")
        squares_summed = sem("squares_summed")
        column_var = sem("column_var")
        column_std = sem("column_std")
        gain = sem("gain")
        scaled = sem("scaled")
        shifted = sem("shifted")
        norm = norm_sems(sem)
        stored = sem("stored")
        block = ctx.enter_context(nc.Block())

        def row(b):
            return t.acc[:, bass.ds(b * W, D)]

        def column_sum(pe, bank, rows, b, signal):
            first = isinstance(b, int) and b == 0
            last = isinstance(b, int) and b == NB - 1
            pe.matmul(t.ps[bank][:, 0:D], t.real[:, int(last), :], rows, start=first, stop=last,
                      skip_group_check=True).then_inc(signal, 1)

        @block.vector
        def _(dve):
            dve.wait_ge(loaded, 80)

            def rows(b, par):
                if started(b):
                    two_back(dve, turned, b)
                    dve.tensor_scalar(t.work[:, par, 0:D], row(b), t.inv_deg[:, bass.ds(b, 1)], None, ALU.mult)
                    dve.tensor_scalar(t.work[:, par, D:2 * D], t.x[:, bass.ds(b * D, D)], 1.0, None,
                                      ALU.mult).then_inc(inputs_ready, 1)
                if started(b, 1):
                    o, q = b - 1, 1 - par
                    dve.wait_ge(product_done, o + 1)
                    two_back(dve, unit_ready, o)
                    dve.tensor_tensor(t.s1[:, q, :], t.ps[2 + q][:, 0:D], bl[:, :], ALU.add).then_inc(biased, 1)
                if started(b, 2):
                    o = b - 2
                    dve.wait_ge(length_ready, o + 1)
                    dve.tensor_scalar(t.rstd[:, par, :], t.std[:, par, :], 1e-12, None, ALU.max).then_inc(length_kept, 1)
                    dve.wait_ge(length_kept, o + 1)
                    dve.reciprocal(t.degree[:, par, :], t.rstd[:, par, :]).then_inc(inverse, 1)
                    dve.wait_ge(inverse, o + 1)
                    dve.tensor_scalar(row(o), t.s1[:, par, :], t.degree[:, par, :], None, ALU.mult).then_inc(unit_ready, 1)
            over_bins(dve, rows, lag=2)
            dve.wait_ge(columns_summed, NB)
            dve.tensor_scalar(col_mean[:, :], t.ps[4][:, 0:D], 1.0 / N, None, ALU.mult).then_inc(column_mean, 1)
            dve.wait_ge(column_mean, 1)

            def centre(b, par):
                dve.tensor_tensor(row(b), row(b), col_mean[:, :], ALU.subtract).then_inc(centred, 1)
                dve.wait_ge(centred, b + 1)
                two_back(dve, squares_summed, b)
                dve.tensor_tensor(t.s2[:, par, :], row(b), row(b), ALU.mult).then_inc(squared, 1)
            over_bins(dve, centre)
            dve.wait_ge(squares_summed, NB)
            dve.tensor_scalar(col_var[:, :], t.ps[5][:, 0:D], 1.0 / N, None, ALU.mult).then_inc(column_var, 1)
            dve.wait_ge(column_std, 1)
            dve.reciprocal(col_var[:, :], col_mean[:, :]).then_inc(gain, 1)
            dve.wait_ge(gain, 1)
            dve.tensor_tensor(col_mean[:, :], col_var[:, :], gamma[:, :], ALU.mult).then_inc(gain, 1)
            dve.wait_ge(gain, 2)

            def finish_rows(b, par):
                if started(b):
                    dve.tensor_tensor(t.s1[:, par, :], row(b), col_mean[:, :], ALU.mult).then_inc(scaled, 1)
                    dve.wait_ge(scaled, b + 1)
                    dve.tensor_tensor(t.work[:, par, 0:D], t.s1[:, par, :], beta[:, :], ALU.add).then_inc(shifted, 1)
                    dve.wait_ge(shifted, b + 1)
                    dve.scalar_tensor_tensor(out=t.s2[:, par, :], in0=t.work[:, par, 0:D], scalar=0.0,
                                             in1=t.x[:, bass.ds(b * D, D)], op0=ALU.max, op1=ALU.add
                                             ).then_inc(norm.summed, 1)
                    norm_moments(dve, t, norm, b, par)
                if started(b, 1):
                    norm_apply(dve, t, norm, b - 1, 1 - par, t.x[:, bass.ds((b - 1) * D, D)])
            over_bins(dve, finish_rows, lag=1)
            dve.memset(t.acc[:, :], 0.0)

        @block.tensor
        def _(pe):
            pe.wait_ge(loaded, 80)

            def rows(b, par):
                if started(b):
                    pe.wait_ge(inputs_ready, b + 1)
                    two_back(pe, turned_copied, b)
                    turn(pe, t, t.work[:, par, :], par, turned, 4)
                if started(b, 1):
                    o, q = b - 1, 1 - par
                    pe.wait_ge(turned_copied, o + 1)
                    if not isinstance(b, int) or o >= 2:
                        pe.wait_ge(biased, o - 1)
                    for c in range(4):
                        mm = pe.matmul(t.ps[2 + q][:, 0:D], t.turned[:, q, c * P:(c + 1) * P],
                                       (Wl, Wr)[c // 2][:, c % 2, :], start=c == 0, stop=c == 3)
                    mm.then_inc(product_done, 1)
                if started(b, 3):
                    pe.wait_ge(unit_ready, b - 2)
                    column_sum(pe, 4, row(b - 3), b - 3, columns_summed)
            over_bins(pe, rows, lag=3)

            def squares(b, par):
                pe.wait_ge(squared, b + 1)
                column_sum(pe, 5, t.s2[:, par, :], b, squares_summed)
            over_bins(pe, squares)

        @block.scalar
        def _(act):
            def rows(b, par):
                if started(b):
                    act.wait_ge(turned, b + 1)
                    two_back(act, product_done, b)
                    act.copy(t.turned[:, par, :], t.ps[par][:, 0:2 * D]).then_inc(turned_copied, 1)
                if started(b, 1):
                    o, q = b - 1, 1 - par
                    act.wait_ge(biased, o + 1)
                    act.activation(t.s2[:, q, :], t.s1[:, q, :], ACT.Square,
                                   accum_out=t.squares[:, q, :]).then_inc(squares_ready, 1)
                    act.wait_ge(squares_ready, o + 1)
                    act.sqrt(t.std[:, q, :], t.squares[:, q, :]).then_inc(length_ready, 1)
            over_bins(act, rows, lag=1)
            act.wait_ge(column_var, 1)
            act.activation(col_mean[:, :], col_var[:, :], ACT.Sqrt, bias=t.eps[:, :]).then_inc(column_std, 1)

            def finish_rows(b, par):
                norm_std(act, t, norm, b, par)
            over_bins(act, finish_rows)

        @block.sync
        def _(sp):
            load(sp, loads, loaded)
            store_bins(sp, t, t.x, D, D, d.x2, norm.normed, stored)


def project(nc, t, d, layer):
    with ExitStack() as ctx:
        sem = sem_maker(nc, ctx, f"p{layer}")
        loads = [weights(nc, ctx, f"{w}{layer}", dram[layer])
                 for w, dram in (("wq", d.L2_gnn_Wq), ("wk", d.L2_gnn_Wk), ("wv", d.L2_gnn_Wv))]
        wq, wk, wv = (x[0] for x in loads)
        kv = ctx.enter_context(nc.sbuf_tensor(f"kv_out{layer}", [P, 2, KV], F32))
        loaded = sem("weights_loaded")
        gap_ready = sem("gap_ready")
        input_ready = sem("input_ready")
        turned = sem("turned")
        turned_copied = sem("turned_copied")
        query_done = sem("query_done")
        kv_done = sem("kv_done")
        query_kept = sem("query_kept")
        kv_copied = sem("kv_copied")
        stored = [sem(f"stored{p}") for p in range(2)]
        block = ctx.enter_context(nc.Block())

        @block.vector
        def _(dve):
            dve.memset(kv[:, :, D:W], 0.0).then_inc(gap_ready, 1)

            def step(b, par):
                if started(b):
                    two_back(dve, turned, b)
                    dve.tensor_scalar(t.work[:, par, 0:D], t.x[:, bass.ds(b * D, D)], 1.0, None,
                                      ALU.mult).then_inc(input_ready, 1)
                if started(b, 1):
                    o, q = b - 1, 1 - par
                    dve.wait_ge(query_done, o + 1)
                    dve.tensor_scalar(t.q[:, bass.ds(o * D, D)], t.ps[2 + q][:, 0:D], 1.0, None,
                                      ALU.mult).then_inc(query_kept, 1)
            over_bins(dve, step, lag=1)

        @block.tensor
        def _(pe):
            pe.wait_ge(loaded, 48)

            def step(b, par):
                if started(b):
                    pe.wait_ge(input_ready, b + 1)
                    two_back(pe, turned_copied, b)
                    turn(pe, t, t.work[:, par, :], par, turned)
                if started(b, 1):
                    o, q = b - 1, 1 - par
                    pe.wait_ge(turned_copied, o + 1)
                    two_back(pe, query_kept, o)
                    for c in range(2):
                        mm = pe.matmul(t.ps[2 + q][:, 0:D], t.turned[:, q, c * P:(c + 1) * P], wq[:, c, :],
                                       start=c == 0, stop=c == 1)
                    mm.then_inc(query_done, 1)
                    two_back(pe, kv_copied, o)
                    for n, w in enumerate((wk, wv)):
                        for c in range(2):
                            mm = pe.matmul(t.ps[4 + q][:, n * D:(n + 1) * D], t.turned[:, q, c * P:(c + 1) * P],
                                           w[:, c, :], start=c == 0, stop=c == 1)
                    mm.then_inc(kv_done, 1)
            over_bins(pe, step, lag=1)

        @block.scalar
        def _(act):
            act.wait_ge(gap_ready, 1)

            def step(b, par):
                if started(b):
                    act.wait_ge(turned, b + 1)
                    two_back(act, kv_done, b)
                    act.copy(t.turned[:, par, 0:D], t.ps[par][:, 0:D]).then_inc(turned_copied, 1)
                if started(b, 1):
                    o, q = b - 1, 1 - par
                    act.wait_ge(kv_done, o + 1)
                    if not isinstance(o, int) or o >= 2:
                        act.wait_ge(stored[q], (o - q) * 8)
                    act.copy(kv[:, q, 0:D], t.ps[4 + q][:, 0:D])
                    act.copy(kv[:, q, W:KV], t.ps[4 + q][:, D:2 * D]).then_inc(kv_copied, 1)
            over_bins(act, step, lag=1)

        @block.sync
        def _(sp):
            load(sp, loads, loaded)

            def step(b, par):
                sp.wait_ge(kv_copied, b + 1)
                sp.dma_start(d.kv[bass.ds(b * P, P), :], kv[:, par, :]).then_inc(stored[par], 16)
            over_bins(sp, step)
            sp.wait_ge(stored[0], 16 * (NB - NB // 2))
            sp.wait_ge(stored[1], 16 * (NB // 2))


def attend(nc, t, d, layer):
    with ExitStack() as ctx:
        sem = sem_maker(nc, ctx, f"at{layer}")

        def sb(name, shape):
            return ctx.enter_context(nc.sbuf_tensor(f"{name}{layer}", shape, F32))

        onehot = sb("edge_node", [P, 2, G, P])
        onehot_t = sb("node_edge", [P, 2, G // 2, P])
        product = sb("product", [P, 2, D])
        scores = sb("scores", [P, 2, G * H])
        below = sb("below", [P, 2, G * H])
        fresh = sb("fresh", [H, 2, G * P + 1])
        run_max = sb("run_max", [H, 2, G * P])
        seg_max = sb("seg_max", [H, G * P])
        first_max = sb("first_max", [1, H])
        drop = sb("drop", [1, H])
        shrink = sb("shrink", [1, H])
        shrink_less_1 = sb("shrink_less_1", [1, H])

        index_copied = sem("index_copied")
        index_taken = sem("index_taken")
        gathered = [sem(f"gathered{s}") for s in range(SLOTS)]
        fresh_loaded = [sem(f"fresh_loaded{p}") for p in range(2)]
        onehot_ready = sem("onehot_ready")
        onehot_turned = sem("onehot_turned")
        onehot_t_copied = sem("onehot_t_copied")
        query_done = sem("query_done")
        product_ready = sem("product_ready")
        score_ready = sem("score_ready")
        score_turned = sem("score_turned")
        run_max_ready = sem("run_max_ready")
        seg_max_ready = sem("seg_max_ready")
        max_turned = sem("max_turned")
        below_ready = sem("below_ready")
        weight_ready = sem("weight_ready")
        weight_placed = sem("weight_placed")
        first_kept = sem("first_kept")
        drop_ready = sem("drop_ready")
        shrink_ready = sem("shrink_ready")
        shrink_used = sem("shrink_used")
        spread_done = sem("spread_done")
        message_ready = sem("message_ready")
        rescaled = sem("rescaled")
        waited = sem("waited")
        part_done = sem("part_done")
        added = sem("added")
        block = ctx.enter_context(nc.Block())

        turned_bank = t.ps[0]
        HG = G // 2
        max_cols = t.ps[7][:, 0:G * H]
        old_max = t.ps[7][0:1, G * H:G * H + H]
        weight = t.ps[7][:, 128:128 + G * H]
        spread = t.ps[7][:, 256:256 + H]

        def in_loop(i):
            return not isinstance(i, int)

        @block.sync
        def _(sp):
            def step(i, slot):
                if in_loop(i) or i >= 2:
                    sp.wait_ge(seg_max_ready, i - 1)
                sp.dma_start(fresh[:, slot % 2, 0:G * P],
                             d.bias[bass.ds(i * G * P, G * P)].partition_broadcast(H)
                             ).then_inc(fresh_loaded[slot % 2], 16)
            over_batches(sp, step)

        @block.gpsimd
        def _(pool):
            def step(i, slot):
                if in_loop(i) or i >= SLOTS:
                    pool.wait_ge(part_done, (i - SLOTS + 1) * G)
                pool.tensor_copy(t.index[:, slot, :], t.src_i[:, bass.ds(i * G, G)]).then_inc(index_copied, 1)
                pool.wait_ge(index_copied, i + 1)
                pool.sem_inc(index_taken, 1)
                for j in range(G):
                    pool.indirect_dma_start(t.rows[:, slot, j, :], None, d.kv,
                                            bass.IndirectOffsetOnAxis(t.index[:, slot, j:j + 1], 0)
                                            ).then_inc(gathered[slot], 16)
            over_batches(pool, step)

        @block.tensor
        def _(pe):
            def turn_onehot(i, k, par, j):
                pe.wait_ge(onehot_ready, k + 1)
                if j == HG or j == 0 and (in_loop(k) or k >= G):
                    pe.wait_ge(onehot_t_copied, 2 * i + j // HG)
                pe.transpose(turned_bank[:, (j % HG) * P:(j % HG + 1) * P], onehot[:, par, j, :],
                             t.ident[:, :]).then_inc(onehot_turned, 1)

            def query(i, k, j):
                b = pe.value_load(t.bins[0:1, bass.ds(k, 1)], min_val=0, max_val=NB - 1)
                pe.wait_ge(onehot_t_copied, 2 * i + j // HG + 1)
                two_back(pe, product_ready, k)
                pe.matmul(t.ps[1 + j % 2][:, 0:D], onehot_t[:, j // HG, j % HG, :], t.q[:, bass.ds(b * D, D)],
                          start=True, stop=True).then_inc(query_done, 1)

            def turn_scores(i, k, par, j):
                pe.wait_ge(score_ready, k + 1)
                if j == 0 and (in_loop(i) or i >= 1):
                    pe.wait_ge(run_max_ready, i * 2)
                pe.transpose(t.ps[5 + j // HG][0:H, (j % HG) * P:(j % HG + 1) * P], scores[:, par, j * H:(j + 1) * H],
                             t.ident[:, :]).then_inc(score_turned, 1)

            def part(k, slot, par, j):
                pe.wait_ge(message_ready, k + 1)
                two_back(pe, added, k)
                pe.matmul(t.ps[3 + j % 2][:, 0:W], onehot[:, par, j, :], t.rows[:, slot, j, 0:W],
                          start=True, stop=True).then_inc(part_done, 1)

            def turn_max(i, par):
                pe.wait_ge(seg_max_ready, i + 1)
                if in_loop(i) or i >= 1:
                    pe.wait_ge(below_ready, i)
                    pe.wait_ge(message_ready, i * G)
                pe.sem_inc(waited, 1)
                for j in range(G):
                    mm = pe.transpose(max_cols[:, j * H:(j + 1) * H], seg_max[:, j * P:(j + 1) * P],
                                      t.ident[0:H, 0:H])
                if in_loop(i) or i >= 1:
                    mm = pe.transpose(old_max, run_max[:, 1 - par, G * P - 1:G * P], t.ident[0:H, 0:H])
                mm.then_inc(max_turned, 1)

            def spread_shrink(i, par):
                pe.wait_ge(shrink_used, i)
                pe.matmul(spread, onehot[0:1, par, 0, :], shrink_less_1[:, :], start=True,
                          stop=True).then_inc(spread_done, 1)

            def step(i, slot):
                par = slot % 2
                now = in_loop(i) or i < NBATCH
                before = in_loop(i) or i >= 1
                for j in range(G + HG + 2):
                    if now and j < G:
                        turn_onehot(i, i * G + j, par, j)
                    if now and 0 <= j - HG - 1 < G:
                        query(i, i * G + j - HG - 1, j - HG - 1)
                    if before and 1 <= j <= G:
                        part((i - 1) * G + j - 1, (slot - 1) % SLOTS, 1 - par, j - 1)
                    if now and j >= HG + 2:
                        turn_scores(i, i * G + j - HG - 2, par, j - HG - 2)
                if now:
                    turn_max(i, par)
                    if before:
                        spread_shrink(i, par)

            over_batches(pe, step, lag=1)

        @block.scalar
        def _(act):
            def step(i, slot):
                par = slot % 2
                for half in range(2):
                    act.wait_ge(onehot_turned, i * G + (half + 1) * HG)
                    if in_loop(i) or i >= 1:
                        act.wait_ge(query_done, (i - 1) * G + (half + 1) * HG)
                    act.copy(onehot_t[:, half, :, :], turned_bank[:, :].rearrange("p (j n) -> p j n", j=HG)
                             ).then_inc(onehot_t_copied, 1)
                act.wait_ge(below_ready, i + 1)
                if in_loop(i) or i >= 1:
                    act.wait_ge(drop_ready, i)
                act.activation(weight, below[:, par, :], ACT.Exp, scale=SCALE).then_inc(weight_ready, 1)
                z = t.rows[:, slot, :, 0:W].rearrange("p j (h e) -> p j h e", h=H)[:, :, :, DK]
                act.activation(z, below[:, par, :].rearrange("p (j h) -> p j h", j=G), ACT.Exp,
                               scale=SCALE).then_inc(weight_placed, 1)
                if in_loop(i) or i >= 1:
                    if in_loop(i) or i >= 2:
                        act.wait_ge(shrink_used, i - 1)
                    act.activation(shrink[:, :], drop[:, :], ACT.Exp, scale=SCALE).then_inc(shrink_ready, 1)
            over_batches(act, step)

        @block.vector
        def _(dve):
            for par in range(2):
                dve.memset(fresh[:, par, G * P:G * P + 1], 0.0)

            def find_onehot(k, par, j):
                if in_loop(k) or k >= 2 * G:
                    dve.wait_ge(part_done, k - 2 * G + 1)
                dve.tensor_scalar(onehot[:, par, j, :], t.node[:, :], t.dst_at[:, bass.ds(k, 1)], None,
                                  ALU.is_equal).then_inc(onehot_ready, 1)

            def score(i, k, slot, par, j):
                if j == 0:
                    dve.wait_ge(gathered[slot], (i - slot) * (16 * G // SLOTS) + 16 * G)
                dve.wait_ge(query_done, k + 1)
                two_back(dve, score_ready, k)
                dve.tensor_tensor(product[:, j % 2, :], t.ps[1 + j % 2][:, 0:D], t.rows[:, slot, j, 0:D],
                                  ALU.mult).then_inc(product_ready, 1)
                dve.wait_ge(product_ready, k + 1)
                if j == 0 and (in_loop(i) or i >= 2):
                    dve.wait_ge(below_ready, i - 1)
                dve.tensor_reduce(scores[:, par, j * H:(j + 1) * H],
                                  product[:, j % 2, :].rearrange("p (h e) -> p h e", h=H), AX_X, ALU.add
                                  ).then_inc(score_ready, 1)

            def message(i, k, slot, par, j):
                if j == 0:
                    dve.wait_ge(weight_placed, i + 1)
                out = t.rows[:, slot, j, 0:W].rearrange("p (h e) -> p h e", h=H)[:, :, 0:DK]
                w = weight[:, j * H:(j + 1) * H].unsqueeze(2).to_broadcast([P, H, DK])
                dve.tensor_tensor(out, t.rows[:, slot, j, W:KV].rearrange("p (h e) -> p h e", h=H), w,
                                  ALU.mult).then_inc(message_ready, 1)

            def add(k, j):
                b = dve.value_load(t.bins[0:1, bass.ds(k, 1)], min_val=0, max_val=NB - 1)
                dve.wait_ge(part_done, k + 1)
                acc = t.acc[:, bass.ds(b * W, W)]
                if in_loop(k) or k >= 1:
                    dve.wait_ge(added, k)
                dve.tensor_tensor(acc, t.ps[3 + j % 2][:, 0:W], acc, ALU.add).then_inc(added, 1)

            def maxima(i, slot, par):
                dve.wait_ge(fresh_loaded[par], (i - par) * 8 + 16)
                dve.wait_ge(score_turned, (i + 1) * G)
                if in_loop(i) or i >= 1:
                    dve.wait_ge(max_turned, i)
                start = run_max[:, 1 - par, G * P - 1:G * P] if in_loop(i) or i >= 1 else -BIG
                half = G * P // 2
                dve.tensor_tensor_scan(run_max[:, par, 0:half], fresh[:, par, 0:half], t.ps[5][0:H, :], start,
                                       ALU.add, ALU.max).then_inc(run_max_ready, 1)
                dve.wait_ge(run_max_ready, i * 2 + 1)
                dve.tensor_tensor_scan(run_max[:, par, half:2 * half], fresh[:, par, half:2 * half], t.ps[6][0:H, :],
                                       run_max[:, par, half - 1:half], ALU.add, ALU.max).then_inc(run_max_ready, 1)
                dve.wait_ge(run_max_ready, i * 2 + 2)
                dve.tensor_tensor_scan(seg_max[:, ::-1], fresh[:, par, 1:G * P + 1][:, ::-1],
                                       run_max[:, par, ::-1], -BIG, ALU.add, ALU.max).then_inc(seg_max_ready, 1)
                dve.wait_ge(max_turned, i + 1)
                if in_loop(i) or i >= 2:
                    dve.wait_ge(weight_placed, i - 1)
                dve.tensor_tensor(below[:, par, :], scores[:, par, :], max_cols, ALU.subtract).then_inc(below_ready, 1)

            def rescale(i):
                b = dve.value_load(t.bins[0:1, bass.ds(i * G, 1)], min_val=0, max_val=NB - 1)
                if in_loop(i) or i >= 2:
                    dve.wait_ge(drop_ready, i - 1)
                dve.tensor_copy(first_max[:, :], max_cols[0:1, 0:H]).then_inc(first_kept, 1)
                dve.wait_ge(first_kept, i)
                if in_loop(i) or i >= 2:
                    dve.wait_ge(shrink_ready, i - 1)
                dve.tensor_tensor(drop[:, :], old_max, first_max[:, :], ALU.subtract).then_inc(drop_ready, 1)
                dve.wait_ge(shrink_ready, i)
                if in_loop(i) or i >= 2:
                    dve.wait_ge(spread_done, i - 1)
                dve.tensor_scalar(shrink_less_1[:, :], shrink[:, :], 1.0, -1.0, ALU.min, ALU.add).then_inc(shrink_used, 1)
                dve.wait_ge(spread_done, i)
                acc = t.acc[:, bass.ds(b * W, W)].rearrange("p (h e) -> p h e", h=H)
                dve.wait_ge(added, i * G)
                dve.scalar_tensor_tensor(out=acc, in0=spread.unsqueeze(2).to_broadcast([P, H, HZ]), scalar=1.0,
                                         in1=acc, op0=ALU.add, op1=ALU.mult).then_inc(rescaled, 1)
                dve.wait_ge(rescaled, i)

            def step(i, slot):
                par = slot % 2
                now = in_loop(i) or i < NBATCH
                before = in_loop(i) or i >= 1
                for j in range(G + HG + 1):
                    if now and j < G:
                        find_onehot(i * G + j, par, j)
                    if before and j < G:
                        message(i - 1, (i - 1) * G + j, (slot - 1) % SLOTS, 1 - par, j)
                    if now and j > HG:
                        score(i, i * G + j - HG - 1, slot, par, j - HG - 1)
                    if before and 1 <= j <= G:
                        add((i - 1) * G + j - 1, j - 1)
                if now:
                    maxima(i, slot, par)
                    if before:
                        rescale(i)
            over_batches(dve, step, lag=1)


def after_attention(nc, t, d, layer):
    with ExitStack() as ctx:
        sem = sem_maker(nc, ctx, f"o{layer}")
        loads = [weights(nc, ctx, f"wo{layer}", d.L2_gnn_Wo[layer]), vector(nc, ctx, f"ln_g{layer}", d.L2_gnn_ln_g[layer]),
                 vector(nc, ctx, f"ln_b{layer}", d.L2_gnn_ln_b[layer])]
        wo, g, bb = (x[0] for x in loads)

        def sb(name, shape):
            return ctx.enter_context(nc.sbuf_tensor(f"{name}{layer}", shape, F32))

        total = sb("total", [P, 2, H])
        share = sb("share", [P, 2, H])
        loaded = sem("loaded")
        total_ready = sem("total_ready")
        share_ready = sem("share_ready")
        mean_ready = sem("mean_ready")
        turned = sem("turned")
        turned_copied = sem("turned_copied")
        product_done = sem("product_done")
        norm = norm_sems(sem)
        scaled = sem("scaled")
        finished = sem("finished")
        block = ctx.enter_context(nc.Block())

        @block.vector
        def _(dve):
            dve.wait_ge(loaded, 48)

            def step(b, par):
                if started(b):
                    acc = t.acc[:, bass.ds(b * W, W)].rearrange("p (h e) -> p h e", h=H)
                    two_back(dve, share_ready, b)
                    dve.tensor_scalar(total[:, par, :], acc[:, :, DK], 1e-9, None, ALU.add).then_inc(total_ready, 1)
                    dve.wait_ge(total_ready, b + 1)
                    two_back(dve, mean_ready, b)
                    dve.reciprocal(share[:, par, :], total[:, par, :]).then_inc(share_ready, 1)
                    dve.wait_ge(share_ready, b + 1)
                    two_back(dve, turned, b)
                    dve.tensor_tensor(t.work[:, par, 0:D].rearrange("p (h e) -> p h e", h=H), acc[:, :, 0:DK],
                                      share[:, par, :].unsqueeze(2).to_broadcast([P, H, DK]), ALU.mult
                                      ).then_inc(mean_ready, 1)
                if started(b, 1):
                    o, q = b - 1, 1 - par
                    dve.wait_ge(product_done, o + 1)
                    two_back(dve, norm.normed, o)
                    dve.tensor_tensor(t.s2[:, q, :], t.ps[2 + q][:, 0:D], t.x[:, bass.ds(o * D, D)], ALU.add
                                      ).then_inc(norm.summed, 1)
                    norm_moments(dve, t, norm, o, q)
                if started(b, 2):
                    o = b - 2
                    two_back(dve, scaled, o)
                    norm_apply(dve, t, norm, o, par, t.s1[:, par, :])
                    dve.wait_ge(norm.normed, o + 1)
                    two_back(dve, finished, o)
                    dve.tensor_tensor(t.work[:, par, D:2 * D], t.s1[:, par, :], g[:, :], ALU.mult).then_inc(scaled, 1)
                    dve.wait_ge(scaled, o + 1)
                    dve.tensor_tensor(t.x[:, bass.ds(o * D, D)], t.work[:, par, D:2 * D], bb[:, :], ALU.add
                                      ).then_inc(finished, 1)
            over_bins(dve, step, lag=2)
            dve.memset(t.acc[:, :], 0.0)

        @block.tensor
        def _(pe):
            pe.wait_ge(loaded, 48)

            def step(b, par):
                if started(b):
                    pe.wait_ge(mean_ready, b + 1)
                    two_back(pe, turned_copied, b)
                    turn(pe, t, t.work[:, par, :], par, turned)
                if started(b, 1):
                    o, q = b - 1, 1 - par
                    pe.wait_ge(turned_copied, o + 1)
                    two_back(pe, norm.summed, o)
                    for c in range(2):
                        mm = pe.matmul(t.ps[2 + q][:, 0:D], t.turned[:, q, c * P:(c + 1) * P], wo[:, c, :],
                                       start=c == 0, stop=c == 1)
                    mm.then_inc(product_done, 1)
            over_bins(pe, step, lag=1)

        @block.scalar
        def _(act):
            def step(b, par):
                if started(b):
                    act.wait_ge(turned, b + 1)
                    two_back(act, product_done, b)
                    act.copy(t.turned[:, par, 0:D], t.ps[par][:, 0:D]).then_inc(turned_copied, 1)
                if started(b, 1):
                    norm_std(act, t, norm, b - 1, 1 - par)
            over_bins(act, step, lag=1)

        @block.sync
        def _(sp):
            load(sp, loads, loaded)


def mlp(nc, t, d):
    HC = HID // P
    with ExitStack() as ctx:
        sem = sem_maker(nc, ctx, "mlp")
        loads = [weights(nc, ctx, "mlp_w1", d.L2_gnn_w1), weights(nc, ctx, "mlp_w2", d.L2_gnn_w2),
                 vector(nc, ctx, "mlp_b2", d.L2_gnn_b2)]
        w1, w2, b2 = (x[0] for x in loads)
        b1 = ctx.enter_context(nc.sbuf_tensor("mlp_b1", [P, HC], F32))
        hidden = ctx.enter_context(nc.sbuf_tensor("hidden", [P, 2, HC, P], F32))
        before = ctx.enter_context(nc.sbuf_tensor("x_before", [P, 2, D], F32))
        loaded = sem("loaded")
        before_loaded = [sem(f"before_loaded{p}") for p in range(2)]
        input_ready = sem("input_ready")
        turned = sem("turned")
        turned_copied = sem("turned_copied")
        hidden_done = sem("hidden_done")
        hidden_ready = sem("hidden_ready")
        product_done = sem("product_done")
        biased = sem("biased")
        norm = norm_sems(sem)
        block = ctx.enter_context(nc.Block())

        @block.vector
        def _(dve):
            dve.wait_ge(loaded, 64)

            def step(b, par):
                if started(b):
                    two_back(dve, turned, b)
                    dve.tensor_scalar(t.work[:, par, 0:D], t.x[:, bass.ds(b * D, D)], 1.0, None,
                                      ALU.mult).then_inc(input_ready, 1)
                if started(b, 2):
                    o = b - 2
                    dve.wait_ge(product_done, o + 1)
                    two_back(dve, norm.summed, o)
                    dve.tensor_tensor(t.s1[:, par, :], t.ps[6 + par][:, 0:D], b2[:, :], ALU.add).then_inc(biased, 1)
                    dve.wait_ge(biased, o + 1)
                    dve.wait_ge(before_loaded[par], (o - par) * 8 + 16)
                    two_back(dve, norm.normed, o)
                    dve.tensor_tensor(t.s2[:, par, :], t.s1[:, par, :], before[:, par, :], ALU.add
                                      ).then_inc(norm.summed, 1)
                    norm_moments(dve, t, norm, o, par)
                if started(b, 3):
                    norm_apply(dve, t, norm, b - 3, 1 - par, t.x[:, bass.ds((b - 3) * D, D)])
            over_bins(dve, step, lag=3)

        @block.tensor
        def _(pe):
            pe.wait_ge(loaded, 64)

            def step(b, par):
                if started(b):
                    pe.wait_ge(input_ready, b + 1)
                    two_back(pe, turned_copied, b)
                    turn(pe, t, t.work[:, par, :], par, turned)
                if started(b, 1):
                    o, q = b - 1, 1 - par
                    pe.wait_ge(turned_copied, o + 1)
                    two_back(pe, hidden_ready, o)
                    for j in range(HC):
                        for c in range(2):
                            mm = pe.matmul(t.ps[2 + 2 * q + j // 4][:, (j % 4) * P:(j % 4 + 1) * P],
                                           w1[:, c, j * P:(j + 1) * P], t.turned[:, q, c * P:(c + 1) * P],
                                           start=c == 0, stop=c == 1)
                    mm.then_inc(hidden_done, 1)
                if started(b, 2):
                    o = b - 2
                    pe.wait_ge(hidden_ready, o + 1)
                    two_back(pe, biased, o)
                    for j in range(HC):
                        mm = pe.matmul(t.ps[6 + par][:, 0:D], hidden[:, par, j, :], w2[:, j, :],
                                       start=j == 0, stop=j == HC - 1)
                    mm.then_inc(product_done, 1)
            over_bins(pe, step, lag=2)

        @block.scalar
        def _(act):
            act.wait_ge(loaded, 64)

            def step(b, par):
                if started(b):
                    act.wait_ge(turned, b + 1)
                    two_back(act, hidden_done, b)
                    act.copy(t.turned[:, par, 0:D], t.ps[par][:, 0:D]).then_inc(turned_copied, 1)
                if started(b, 1):
                    o, q = b - 1, 1 - par
                    act.wait_ge(hidden_done, o + 1)
                    two_back(act, product_done, o)
                    for j in range(HC):
                        ins = act.activation(hidden[:, q, j, :], t.ps[2 + 2 * q + j // 4][:, (j % 4) * P:(j % 4 + 1) * P],
                                             ACT.Relu, bias=b1[:, j:j + 1])
                    ins.then_inc(hidden_ready, 1)
                if started(b, 2):
                    norm_std(act, t, norm, b - 2, par)
            over_bins(act, step, lag=2)

        @block.sync
        def _(sp):
            load(sp, loads, loaded)
            sp.dma_start(b1[:, :], d.b1T).then_inc(loaded, 16)

            def step(b, par):
                two_back(sp, norm.summed, b)
                sp.dma_start(before[:, par, :], d.x2[bass.ds(b * P, P), :]).then_inc(before_loaded[par], 16)
            over_bins(sp, step)


def project3(nc, t, d):
    with ExitStack() as ctx:
        sem = sem_maker(nc, ctx, "p3")
        loads = [weights(nc, ctx, "w1", d.w1T), vector(nc, ctx, "w1_b", d.L3_gnn_w1_b)]
        w1, b1 = (x[0] for x in loads)
        is_twin = ctx.enter_context(nc.sbuf_tensor("is_twin", [P, K], F32))
        detour = ctx.enter_context(nc.sbuf_tensor("detour", [P, K], F32))
        loaded = sem("loaded")
        input_ready = sem("input_ready")
        turned = sem("turned")
        turned_copied = sem("turned_copied")
        product_done = sem("product_done")
        kept = sem("kept")
        stored = sem("stored")
        chain = sem("target_chain")
        block = ctx.enter_context(nc.Block())

        @block.vector
        def _(dve):
            dve.wait_ge(loaded, 32)
            dve.tensor_scalar(is_twin[:, :], t.twins[:, :], 1.0, None, ALU.min)
            dve.tensor_scalar(detour[:, :], t.src_at[:, :], -1.0, t.spare[:, :], ALU.mult, ALU.add).then_inc(chain, 1)
            dve.wait_ge(chain, 1)
            dve.tensor_tensor(detour[:, :], detour[:, :], is_twin[:, :], ALU.mult).then_inc(chain, 1)
            dve.wait_ge(chain, 2)
            dve.tensor_tensor(t.target_i[:, :], detour[:, :], t.src_at[:, :], ALU.add)

            def step(b, par):
                if started(b):
                    two_back(dve, turned, b)
                    dve.tensor_scalar(t.work[:, par, 0:D], t.x[:, bass.ds(b * D, D)], 1.0, None,
                                      ALU.mult).then_inc(input_ready, 1)
                if started(b, 1):
                    o, q = b - 1, 1 - par
                    dve.wait_ge(product_done, o + 1)
                    dve.tensor_tensor(t.z[:, bass.ds(o * SUP, SUP)], t.ps[2 + q][:, 0:SUP], b1[:, :], ALU.add
                                      ).then_inc(kept, 1)
            over_bins(dve, step, lag=1)

        @block.tensor
        def _(pe):
            pe.wait_ge(loaded, 32)

            def step(b, par):
                if started(b):
                    pe.wait_ge(input_ready, b + 1)
                    two_back(pe, turned_copied, b)
                    turn(pe, t, t.work[:, par, :], par, turned)
                if started(b, 1):
                    o, q = b - 1, 1 - par
                    pe.wait_ge(turned_copied, o + 1)
                    two_back(pe, kept, o)
                    for c in range(2):
                        mm = pe.matmul(t.ps[2 + q][:, 0:SUP], t.turned[:, q, c * P:(c + 1) * P], w1[:, c, :],
                                       start=c == 0, stop=c == 1)
                    mm.then_inc(product_done, 1)
            over_bins(pe, step, lag=1)

        @block.scalar
        def _(act):
            def step(b, par):
                act.wait_ge(turned, b + 1)
                two_back(act, product_done, b)
                act.copy(t.turned[:, par, 0:D], t.ps[par][:, 0:D]).then_inc(turned_copied, 1)
            over_bins(act, step)

        @block.sync
        def _(sp):
            load(sp, loads, loaded)
            store_bins(sp, t, t.z, SUP, SUP, d.z, kept, stored)


def neighbour_sums(nc, t, d):
    with ExitStack() as ctx:
        sem = sem_maker(nc, ctx, "a3")

        def sb(name, shape):
            return ctx.enter_context(nc.sbuf_tensor(name, shape, F32))

        onehot_t = sb("node_edge", [P, 2, P])
        same = sb("same_source", [P, 2, P])
        ends = sb("z_at_destination", [P, 2, SUP])
        outgoing = sb("outgoing", [P, COPIES, SUP])
        column = sb("source_column", [P, 2, G])
        target = ctx.enter_context(nc.sbuf_tensor("target_now", [P, SLOTS, G], I32))
        index_copied = sem("index_copied")
        index_taken = sem("index_taken")
        gathered = [sem(f"gathered{s}") for s in range(SLOTS)]
        sent = [sem(f"sent{r}") for r in range(COPIES)]
        column_ready = sem("column_ready")
        onehot_ready = sem("onehot_ready")
        turned = sem("turned")
        turned_copied = sem("turned_copied")
        row_ready = sem("row_ready")
        same_ready = sem("same_ready")
        ends_done = sem("ends_done")
        ends_copied = sem("ends_copied")
        merged = sem("merged")
        outgoing_ready = sem("outgoing_ready")
        part_done = sem("part_done")
        added = sem("added")
        block = ctx.enter_context(nc.Block())

        def in_loop(i):
            return not isinstance(i, int)

        LAG = G + G // 2
        assert LAG % COPIES == 0

        @block.gpsimd
        def _(pool):
            def step(i, slot):
                if in_loop(i) or i < NBATCH:
                    if in_loop(i) or i >= SLOTS:
                        pool.wait_ge(part_done, (i - SLOTS + 1) * G)
                    pool.tensor_copy(t.index[:, slot, :], t.src_i[:, bass.ds(i * G, G)])
                    if in_loop(i) or i >= SLOTS:
                        for r in range(COPIES):
                            pool.wait_ge(sent[r], (i - SLOTS + 1) * (16 * G // COPIES))
                        pool.sem_inc(index_taken, 1)
                    pool.tensor_copy(target[:, slot, :], t.target_i[:, bass.ds(i * G, G)]).then_inc(index_copied, 1)
                    pool.wait_ge(index_copied, i + 1)
                    pool.sem_inc(index_taken, 1)
                for j in range(G):
                    if in_loop(i) or i < NBATCH:
                        pool.indirect_dma_start(t.rows[:, slot, j, 0:SUP], None, d.z,
                                                bass.IndirectOffsetOnAxis(t.index[:, slot, j:j + 1], 0)
                                                ).then_inc(gathered[slot], 16)
                    k = i * G + j - LAG
                    if in_loop(k) or 0 <= k < K:
                        r = j % COPIES
                        pool.wait_ge(outgoing_ready, k + 1)
                        pool.sem_inc(index_taken, 1)
                        if in_loop(k) or k >= COPIES:
                            pool.wait_ge(sent[r], i * (16 * G // COPIES) + 16 * ((j - LAG - r) // COPIES))
                            pool.sem_inc(index_taken, 1)
                        pool.indirect_dma_start(d.reversed[r], bass.IndirectOffsetOnAxis(
                            target[:, (slot * G + j - LAG) // G % SLOTS, (j - LAG) % G:(j - LAG) % G + 1], 0),
                            outgoing[:, r, :], None, compute_op=ALU.add).then_inc(sent[r], 16)
            over_batches(pool, step, lag=2)
            for r in range(COPIES):
                pool.wait_ge(sent[r], 16 * K // COPIES)

        @block.tensor
        def _(pe):
            def turn_both(i, k, slot, j):
                pe.wait_ge(onehot_ready, k + 1)
                two_back(pe, ends_copied, k)
                pe.transpose(t.ps[2 + j % 2][:, 0:P], t.onehot[:, j % 4, :], t.ident[:, :]).then_inc(turned, 1)
                pe.wait_ge(column_ready, i + 1)
                two_back(pe, same_ready, k)
                pe.matmul(t.ps[4 + j % 2][:, 0:P], column[:, slot % 2, j:j + 1].to_broadcast([P, P]),
                          t.ident[:, :], start=True, stop=True).then_inc(row_ready, 1)

            def take_ends(k, j):
                b = pe.value_load(t.bins[0:1, bass.ds(k, 1)], min_val=0, max_val=NB - 1)
                pe.wait_ge(turned_copied, k + 1)
                pe.matmul(t.ps[2 + j % 2][:, P:P + SUP], onehot_t[:, j % 2, :], t.z[:, bass.ds(b * SUP, SUP)],
                          start=True, stop=True).then_inc(ends_done, 1)

            def merge(k, j):
                pe.wait_ge(ends_copied, k + 1)
                pe.wait_ge(same_ready, k + 1)
                two_back(pe, outgoing_ready, k)
                pe.matmul(t.ps[6 + j % 2][:, 0:SUP], same[:, j % 2, :], ends[:, j % 2, :],
                          start=True, stop=True).then_inc(merged, 1)

            def part(k, slot, j):
                two_back(pe, added, k)
                pe.matmul(t.ps[j % 2][:, 0:SUP], t.onehot[:, j % 4, :], t.rows[:, slot, j, 0:SUP],
                          start=True, stop=True).then_inc(part_done, 1)

            def step(i, slot):
                if in_loop(i) or i < NBATCH:
                    pe.wait_ge(gathered[slot], (i - slot) * (16 * G // SLOTS) + 16 * G)
                for j in range(G):
                    k = i * G + j
                    if in_loop(i) or i < NBATCH:
                        turn_both(i, k, slot, j)
                        part(k, slot, j)
                    if in_loop(k) or 1 <= k <= K:
                        take_ends(k - 1, (j - 1) % G)
                    if in_loop(k) or 2 <= k <= K + 1:
                        merge(k - 2, (j - 2) % G)
            over_batches(pe, step, lag=1)

        @block.scalar
        def _(act):
            def step(i, slot):
                for j in range(G):
                    k = i * G + j
                    if in_loop(i) or i < NBATCH:
                        act.wait_ge(turned, k + 1)
                        two_back(act, ends_done, k)
                        act.copy(onehot_t[:, j % 2, :], t.ps[2 + j % 2][:, 0:P]).then_inc(turned_copied, 1)
                    if in_loop(k) or 1 <= k <= K:
                        act.wait_ge(ends_done, k)
                        two_back(act, merged, k - 1)
                        act.copy(ends[:, (j - 1) % 2, :], t.ps[2 + (j - 1) % 2][:, P:P + SUP]).then_inc(ends_copied, 1)
                    if in_loop(k) or 2 <= k <= K + 1:
                        act.wait_ge(merged, k - 1)
                        r = (j - 2) % COPIES
                        if in_loop(k) or k - 2 >= COPIES:
                            last = k - 2 - COPIES
                            act.wait_ge(sent[r], (last - r) * (16 // COPIES) + 16)
                        act.copy(outgoing[:, r, :], t.ps[6 + (j - 2) % 2][:, 0:SUP]).then_inc(outgoing_ready, 1)
            over_batches(act, step, lag=1)

        @block.vector
        def _(dve):
            def add(k, j):
                b = dve.value_load(t.bins[0:1, bass.ds(k, 1)], min_val=0, max_val=NB - 1)
                dve.wait_ge(part_done, k + 1)
                acc = t.acc[:, bass.ds(b * W, SUP)]
                if in_loop(k) or k >= 1:
                    dve.wait_ge(added, k)
                dve.tensor_tensor(acc, t.ps[j % 2][:, 0:SUP], acc, ALU.add).then_inc(added, 1)

            def step(i, slot):
                if in_loop(i) or i >= 2:
                    dve.wait_ge(same_ready, (i - 1) * G)
                dve.tensor_copy(column[:, slot % 2, :], t.src_at[:, bass.ds(i * G, G)]).then_inc(column_ready, 1)
                dve.wait_ge(column_ready, i + 1)
                for j in range(G):
                    k = i * G + j
                    if in_loop(k) or k >= 4:
                        dve.wait_ge(part_done, k - 3)
                        dve.wait_ge(turned, k - 3)
                    dve.tensor_scalar(t.onehot[:, j % 4, :], t.node[:, :], t.dst_at[:, bass.ds(k, 1)], None,
                                      ALU.is_equal).then_inc(onehot_ready, 1)
                    dve.wait_ge(row_ready, k + 1)
                    two_back(dve, merged, k)
                    dve.tensor_scalar(same[:, j % 2, :], t.ps[4 + j % 2][:, 0:P], column[:, slot % 2, j:j + 1], None,
                                      ALU.is_equal).then_inc(same_ready, 1)
                    if in_loop(k) or k >= 1:
                        add(k - 1, (j - 1) % G)
            over_batches(dve, step)
            add(K - 1, G - 1)


def dense3(nc, t, d):
    with ExitStack() as ctx:
        sem = sem_maker(nc, ctx, "d3")
        loads = [weights(nc, ctx, "w0", d.w0T), vector(nc, ctx, "w0_b", d.L3_gnn_w0_b)]
        w0, b0 = (x[0] for x in loads)
        back = ctx.enter_context(nc.sbuf_tensor("back", [P, 2, COPIES, SUP], F32))
        loaded = sem("loaded")
        back_loaded = [sem(f"back_loaded{p}") for p in range(2)]
        input_ready = sem("input_ready")
        turned = sem("turned")
        turned_copied = sem("turned_copied")
        product_done = sem("product_done")
        gathered = sem("sums_added")
        biased = sem("biased")
        joined = sem("joined")
        norm = norm_sems(sem)
        stored = sem("stored")
        block = ctx.enter_context(nc.Block())

        @block.vector
        def _(dve):
            dve.wait_ge(loaded, 32)

            def step(b, par):
                if started(b):
                    two_back(dve, turned, b)
                    dve.tensor_scalar(t.work[:, par, 0:D], t.x[:, bass.ds(b * D, D)], 1.0, None,
                                      ALU.mult).then_inc(input_ready, 1)
                    acc = t.acc[:, bass.ds(b * W, SUP)]
                    dve.wait_ge(back_loaded[par], (b - par) * (16 * COPIES // 2) + 16 * COPIES)
                    for r in range(COPIES):
                        dve.tensor_tensor(acc, acc, back[:, par, r, :], ALU.add).then_inc(gathered, 1)
                        dve.wait_ge(gathered, b * COPIES + r + 1)
                if started(b, 1):
                    o, q = b - 1, 1 - par
                    dve.wait_ge(product_done, o + 1)
                    two_back(dve, norm.summed, o)
                    dve.tensor_tensor(t.s1[:, q, :], t.ps[2 + q][:, 0:D], b0[:, :], ALU.add).then_inc(biased, 1)
                    dve.wait_ge(biased, o + 1)
                    dve.tensor_tensor(t.s1[:, q, 0:SUP], t.s1[:, q, 0:SUP], t.acc[:, bass.ds(o * W, SUP)],
                                      ALU.add).then_inc(joined, 1)
                    dve.wait_ge(joined, o + 1)
                    two_back(dve, norm.normed, o)
                    dve.tensor_tensor(t.s2[:, q, :], t.s1[:, q, :], t.x[:, bass.ds(o * D, D)], ALU.add
                                      ).then_inc(norm.summed, 1)
                    norm_moments(dve, t, norm, o, q)
                if started(b, 2):
                    norm_apply(dve, t, norm, b - 2, par, t.x[:, bass.ds((b - 2) * D, D)])
            over_bins(dve, step, lag=2)

        @block.tensor
        def _(pe):
            pe.wait_ge(loaded, 32)

            def step(b, par):
                if started(b):
                    pe.wait_ge(input_ready, b + 1)
                    two_back(pe, turned_copied, b)
                    turn(pe, t, t.work[:, par, :], par, turned)
                if started(b, 1):
                    o, q = b - 1, 1 - par
                    pe.wait_ge(turned_copied, o + 1)
                    two_back(pe, biased, o)
                    for c in range(2):
                        mm = pe.matmul(t.ps[2 + q][:, 0:D], t.turned[:, q, c * P:(c + 1) * P], w0[:, c, :],
                                       start=c == 0, stop=c == 1)
                    mm.then_inc(product_done, 1)
            over_bins(pe, step, lag=1)

        @block.scalar
        def _(act):
            def step(b, par):
                if started(b):
                    act.wait_ge(turned, b + 1)
                    two_back(act, product_done, b)
                    act.copy(t.turned[:, par, 0:D], t.ps[par][:, 0:D]).then_inc(turned_copied, 1)
                if started(b, 1):
                    norm_std(act, t, norm, b - 1, 1 - par)
            over_bins(act, step, lag=1)

        @block.sync
        def _(sp):
            load(sp, loads, loaded)

            def step(b, par):
                if started(b):
                    if not isinstance(b, int) or b >= 2:
                        sp.wait_ge(gathered, (b - 1) * COPIES)
                    for r in range(COPIES):
                        sp.dma_start(back[:, par, r, :], d.reversed[r][bass.ds(b * P, P), :]
                                     ).then_inc(back_loaded[par], 16)
                if started(b, 2):
                    o = b - 2
                    sp.wait_ge(norm.normed, o + 1)
                    rows = LAST if isinstance(b, int) and o == NB - 1 else P
                    sp.dma_start(d.out[bass.ds(o * P, rows), :], t.x[0:rows, bass.ds(o * D, D)]).then_inc(stored, 16)
            over_bins(sp, step, lag=2)
            sp.wait_ge(stored, 16 * NB)


def program(nc, d):
    with ExitStack() as ctx:
        t = Named()

        t.ps = [ctx.enter_context(nc.psum_tensor(f"bank{i}", [P, 512], F32)) for i in range(8)]

        def sb(name, shape, dt=F32):
            return ctx.enter_context(nc.sbuf_tensor(name, shape, dt))

        t.x = sb("x", [P, NB * D])
        t.acc = sb("acc", [P, NB * W])
        t.rows = sb("rows", [P, SLOTS, G, KV])
        t.onehot = sb("onehot", [P, 4, P])
        t.ident = sb("ident", [P, P])
        t.lower = sb("lower", [P, P])
        t.node = sb("node", [P, P])
        t.real = sb("real", [P, 2, P])
        t.eps = sb("eps", [P, 1])
        t.spare = sb("spare", [P, 1])
        t.dst_at = sb("dst_at", [P, K])
        t.src_at = sb("src_at", [P, K])
        t.src_i = sb("src_idx", [P, K], I32)
        t.bins = sb("bins", [1, K], I32)
        t.index = sb("index", [P, SLOTS, G], I32)
        t.degree = sb("degree", [P, 2, 1])
        t.inv_deg = sb("inv_deg", [P, NB])
        t.work = sb("work", [P, 2, 2 * D])
        t.turned = sb("turned", [P, 2, 2 * D])
        t.squares = sb("squares", [P, 2, 1])
        t.column = sb("column", [P, 2, G])
        t.twin_count = sb("twin_count", [P, 2, G])
        t.twins = sb("twins", [P, K])
        t.s1 = sb("s1", [P, 2, D])
        t.s2 = sb("s2", [P, 2, D])
        t.stats = sb("stats", [P, 2, 6])
        t.mv = sb("mv", [P, 2, 2])
        t.std = sb("std", [P, 2, 1])
        t.rstd = sb("rstd", [P, 2, 1])

        with ExitStack() as edges:
            t.dst_i, t.prev_i, t.src_now = (edges.enter_context(nc.sbuf_tensor(name, [P, CH, P], I32))
                                            for name in ("dst_now", "dst_before", "src_now"))
            t.ones = edges.enter_context(nc.sbuf_tensor("ones", [P, P], F32))
            t.unsorted = edges.enter_context(nc.sbuf_tensor("unsorted", [1, 1], I32))
            load_edges(nc, t, d)
            sort_edges(nc, t, d)
            build_tables(nc, t, d)
        aggregate(nc, t, d, "a0", d.x, D, 1)
        dense0(nc, t, d)
        aggregate(nc, t, d, "a1", d.x1, D, 0, find_twins=True)
        dense1(nc, t, d)
        with nc.sbuf_tensor("queries", [P, NB * D], F32) as t.q:
            for layer in range(2):
                project(nc, t, d, layer)
                attend(nc, t, d, layer)
                after_attention(nc, t, d, layer)
        mlp(nc, t, d)
        with nc.sbuf_tensor("supports", [P, NB * SUP], F32) as t.z, nc.sbuf_tensor("target", [P, K], I32) as t.target_i:
            project3(nc, t, d)
            neighbour_sums(nc, t, d)
        dense3(nc, t, d)


def kernel(**inputs):
    import numpy as np
    import concourse.bacc as bacc
    from concourse.bass_utils import run_bass_kernel_spmd as run

    nc = bacc.Bacc("TRN2", target_bir_lowering=False, num_devices=1)
    v = {name: np.asarray(a) for name, a in inputs.items()}
    arrays = {name: a for name, a in v.items()
              if name != "L2_gnn_b1" and (name.startswith("L2") or a.ndim == 1 and name[0] == "L")}
    arrays["x"] = np.concatenate([v["x"], np.zeros((NP - N, D), v["x"].dtype)])
    arrays["src"] = np.concatenate([v["src"], np.full(EC - E, NP - 1, v["src"].dtype)])
    arrays["dst"] = np.concatenate([np.full(1, -1, v["dst"].dtype), v["dst"], np.full(EC - E, NP - 1, v["dst"].dtype)])
    for name, w in (("W0T", "L0_gnn_W"), ("WlT", "L1_gnn_W_l"), ("WrT", "L1_gnn_W_r"), ("w0T", "L3_gnn_w0_w"),
                    ("w1T", "L3_gnn_w1_w")):
        arrays[name] = np.ascontiguousarray(v[w].T)
    arrays["b1T"] = np.ascontiguousarray(v["L2_gnn_b1"].reshape(-1, P).T)
    d = Named()

    def given(name):
        a = arrays[name]
        return nc.dram_tensor(f"in_{name}", a.shape, mybir.dt.from_np(a.dtype), kind="ExternalInput").ap()

    d.x, d.src, d.dst = given("x"), given("src"), given("dst")
    d.W0T, d.L0_gnn_b = given("W0T"), given("L0_gnn_b")
    d.WlT, d.WrT, d.L1_gnn_b_l = given("WlT"), given("WrT"), given("L1_gnn_b_l")
    d.L1_gnn_gamma, d.L1_gnn_beta = given("L1_gnn_gamma"), given("L1_gnn_beta")
    d.L2_gnn_Wq, d.L2_gnn_Wk, d.L2_gnn_Wv = given("L2_gnn_Wq"), given("L2_gnn_Wk"), given("L2_gnn_Wv")
    d.L2_gnn_Wo, d.L2_gnn_ln_g, d.L2_gnn_ln_b = given("L2_gnn_Wo"), given("L2_gnn_ln_g"), given("L2_gnn_ln_b")
    d.L2_gnn_w1, d.b1T, d.L2_gnn_w2, d.L2_gnn_b2 = given("L2_gnn_w1"), given("b1T"), given("L2_gnn_w2"), given("L2_gnn_b2")
    d.w0T, d.L3_gnn_w0_b, d.w1T, d.L3_gnn_w1_b = given("w0T"), given("L3_gnn_w0_b"), given("w1T"), given("L3_gnn_w1_b")

    def scratch(name, shape, dt=F32):
        return nc.dram_tensor(f"dram_{name}", shape, dt).ap()

    d.records = scratch("records", (1 + EC, 2), I32)
    d.keys = scratch("keys", (EC,))
    d.bias = scratch("segment_bias", (K * P,))
    d.reversed = [scratch(f"reversed{r}", (NP + P, SUP)) for r in range(COPIES)]
    d.x1 = scratch("x1", (NP, D))
    d.x2 = scratch("x2", (NP, D))
    d.kv = scratch("kv", (NP, KV))
    d.z = scratch("z", (NP, SUP))
    d.out = nc.dram_tensor("out", (N, D), F32, kind="ExternalOutput").ap()
    program(nc, d)
    got = run(nc, [{f"in_{name}": a for name, a in arrays.items()}], core_ids=[0])
    return got.results[0]["out"]
```

```python
from contextlib import ExitStack

import concourse.bass as bass
from concourse import mybir

F32 = mybir.dt.float32
I32 = mybir.dt.int32
ALU = mybir.AluOpType
ACT = mybir.ActivationFunctionType
AX_X = mybir.AxisListType.X

P = 128
N = 3125
E = 50000
D = 256
H, DK = 8, 32
HZ = DK + 1
W = H * HZ
KV = W + D
SCALE = DK ** -0.5
HID = 1024
SUP = 128
NB = -(-N // P)
NP = NB * P
NT = -(-E // P)
CH = -(-NT // P)
EC = CH * P * P
G = 8
SLOTS = 4
NBATCH = -(-(NT + NB - 1) // (G * SLOTS)) * SLOTS
K = NBATCH * G
LAST = N - (NB - 1) * P
BIG = 1e30
LN_EPS = 1e-5
COPIES = 4


class Named:
    pass


def over_batches(eng, step, lag=0):
    for i in range(SLOTS):
        step(i, i)
    with eng.Fori(1, NBATCH // SLOTS) as n:
        for slot in range(SLOTS):
            step(n * SLOTS + slot, slot)
    for i in range(NBATCH, NBATCH + lag):
        step(i, i % SLOTS)


def over_bins(eng, step, lag=0):
    for b in range(4):
        step(b, b % 2)
    with eng.Fori(2, (NB - 1) // 2) as n:
        for parity in range(2):
            step(n * 2 + parity, parity)
    for b in range((NB - 1) // 2 * 2, NB + lag):
        step(b, b % 2)


def runs(b):
    return not isinstance(b, int) or 0 <= b < NB


def sem_maker(nc, ctx, phase):
    made = []

    def sem(name):
        made.append(nc.alloc_semaphore(f"{phase}_{name}"))
        return made[-1]

    def clear():
        nc.clear_and_free_semaphores(made)
        nc.all_engine_barrier()

    ctx.callback(clear)
    return sem


def load_edges(nc, t, d):
    with ExitStack() as ctx:
        sem = sem_maker(nc, ctx, "le")
        falls = ctx.enter_context(nc.sbuf_tensor("falls", [P, CH, P], F32))
        fall_count = ctx.enter_context(nc.sbuf_tensor("fall_count", [P, 1], F32))
        loaded = sem("loaded")
        compared = sem("compared")
        counted = sem("counted")
        summed = sem("summed")
        ones_ready = sem("ones_ready")
        block = ctx.enter_context(nc.Block())

        @block.sync
        def _(sp):
            for tile, flat in ((t.dst_i, d.dst[1:1 + EC]), (t.prev_i, d.dst[0:EC]), (t.src_now, d.src)):
                sp.dma_start(tile[:, :, :], flat.rearrange("(c p e) -> p c e", c=CH, p=P)).then_inc(loaded, 16)
            sp.wait_ge(loaded, 48)

        @block.vector
        def _(dve):
            dve.memset(t.ones[:, :], 1.0).then_inc(ones_ready, 1)
            dve.wait_ge(loaded, 48)
            dve.tensor_tensor(falls[:, :, :], t.dst_i[:, :, :], t.prev_i[:, :, :], ALU.is_lt).then_inc(compared, 1)
            dve.wait_ge(compared, 1)
            dve.tensor_reduce(fall_count[:, :], falls[:, :, :], mybir.AxisListType.XY, ALU.add).then_inc(counted, 1)
            dve.wait_ge(summed, 1)
            dve.tensor_copy(t.unsorted[:, :], t.ps[0][0:1, 0:1])

        @block.tensor
        def _(pe):
            pe.wait_ge(ones_ready, 1)
            pe.wait_ge(counted, 1)
            pe.matmul(t.ps[0][:, 0:1], t.ones[:, :], fall_count[:, :], start=True, stop=True).then_inc(summed, 1)


def sort_edges(nc, t, d):
    CUT = 8
    PIECE = NT * P // CUT
    with ExitStack() as ctx:
        sem = sem_maker(nc, ctx, "sort")

        def sb(name, shape, dt=F32):
            return ctx.enter_context(nc.sbuf_tensor(name, shape, dt))

        records = sb("records", [P, CH, P, 2], I32)
        keys = sb("keys", [P, CH * P])
        rank = sb("rank", [P, CH * P])
        count = sb("count", [P, 1])
        tile_no = sb("key_tile_no", [P, CH])
        position = sb("position", [P, P])
        equal = sb("equal_keys", [P, P])
        lower = sb("equal_before", [P, P])
        head = sb("head", [1, 2], I32)
        place = sb("place", [P, 1], I32)
        record = sb("record", [P, 2], I32)
        flat = t.rows[:, :, :, :].rearrange("p a b c -> p (a b c)")
        piece = flat[:, 0:PIECE]
        smaller = flat[:, PIECE:2 * PIECE]

        numbered = sem("numbered")
        filled = sem("filled")
        keys_ready = sem("keys_ready")
        kept = sem("kept")
        piece_loaded = sem("piece_loaded")
        compared = sem("compared")
        ranked = sem("ranked")
        tied = sem("tied")
        staged = sem("staged")
        taken = sem("taken")
        sent = sem("sent")
        reloaded = sem("reloaded")
        split = sem("split")
        block = ctx.enter_context(nc.Block())

        @block.gpsimd
        def _(pool):
            f = dict(allow_small_or_imprecise_dtypes=True)
            pool.iota(tile_no[:, :], [[P, CH]], base=0, channel_multiplier=1, **f).then_inc(numbered, 1)
            pool.iota(position[:, :], [[1, P]], base=0, channel_multiplier=0, **f).then_inc(numbered, 1)
            unsorted = pool.value_load(t.unsorted[0:1, 0:1])
            with pool.If(unsorted > 0):
                pool.wait_ge(kept, 48)
                for c in range(CH):
                    tiles = min(P, NT - c * P)
                    with pool.Fori(0, P) as e:
                        pool.wait_ge(staged, (e + c * P) + 1)
                        pool.sem_inc(taken, 1)
                        pool.indirect_dma_start(d.records, bass.IndirectOffsetOnAxis(place[0:tiles, :], 0),
                                                record[0:tiles, :], None).then_inc(sent, 16)

        @block.sync
        def _(sp):
            unsorted = sp.value_load(t.unsorted[0:1, 0:1])
            with sp.If(unsorted > 0):
                sp.wait_ge(filled, 3)
                sp.dma_start(d.records[1:1 + EC, :].rearrange("(c p e) r -> p c (e r)", c=CH, p=P),
                             records[:, :, :, :].rearrange("p c e r -> p c (e r)")).then_inc(kept, 16)
                sp.dma_start(d.records[0:1, :], head[:, :]).then_inc(kept, 16)
                sp.wait_ge(keys_ready, 1)
                sp.dma_start(d.keys.rearrange("(c p e) -> p c e", c=CH, p=P),
                             keys[:, :].rearrange("p (c e) -> p c e", c=CH)).then_inc(kept, 16)
                sp.wait_ge(kept, 48)
                for q in range(CUT):
                    if q >= 1:
                        sp.wait_ge(compared, q * CH * P)
                    sp.dma_start(piece, d.keys[q * PIECE:(q + 1) * PIECE].partition_broadcast(P)
                                 ).then_inc(piece_loaded, 16)
                sp.wait_ge(sent, 16 * CH * P)
                for n, tile in enumerate((1, 0)):
                    if n:
                        sp.wait_ge(split, 2)
                    sp.dma_start(records[:, :, :, :].rearrange("p c e r -> p c (e r)"),
                                 d.records[tile:tile + EC, :].rearrange("(c p e) r -> p c (e r)", c=CH, p=P)
                                 ).then_inc(reloaded, 16)
                sp.wait_ge(reloaded, 32)

        @block.vector
        def _(dve):
            dve.wait_ge(numbered, 2)
            unsorted = dve.value_load(t.unsorted[0:1, 0:1])
            with dve.If(unsorted > 0):
                dve.tensor_copy(records[:, :, :, 0], t.dst_i[:, :, :]).then_inc(filled, 1)
                dve.tensor_copy(records[:, :, :, 1], t.src_now[:, :, :]).then_inc(filled, 1)
                dve.memset(head[:, :], -1).then_inc(filled, 1)
                dve.memset(rank[:, :], 1.0)
                for c in range(CH):
                    ins = dve.tensor_scalar(keys[:, c * P:(c + 1) * P], t.dst_i[:, c, :], float(CH * P),
                                            tile_no[:, c:c + 1], ALU.mult, ALU.add)
                ins.then_inc(keys_ready, 1)
                dve.wait_ge(keys_ready, 1)
                for q in range(CUT):
                    dve.wait_ge(piece_loaded, 16 * (q + 1))
                    with dve.Fori(0, CH * P) as e:
                        at = e + q * CH * P
                        dve.wait_ge(ranked, at)
                        dve.tensor_scalar(smaller, piece, keys[:, bass.ds(e, 1)], 0.0, ALU.is_lt, ALU.add,
                                          accum_out=count[:, :]).then_inc(compared, 1)
                        dve.wait_ge(compared, at + 1)
                        dve.tensor_tensor(rank[:, bass.ds(e, 1)], rank[:, bass.ds(e, 1)], count[:, :], ALU.add
                                          ).then_inc(ranked, 1)
                for c in range(CH):
                    with dve.Fori(0, P) as e:
                        at = e + c * P
                        dve.wait_ge(ranked, at + CUT * CH * P)
                        dve.tensor_scalar(equal[:, :], keys[:, c * P:(c + 1) * P], keys[:, bass.ds(at, 1)], None,
                                          ALU.is_equal).then_inc(tied, 1)
                        dve.wait_ge(tied, at * 2 + 1)
                        dve.scalar_tensor_tensor(out=lower[:, :], in0=position[:, :], scalar=position[:, bass.ds(e, 1)],
                                                 in1=equal[:, :], op0=ALU.is_lt, op1=ALU.mult,
                                                 accum_out=count[:, :]).then_inc(tied, 1)
                        dve.wait_ge(tied, at * 2 + 2)
                        dve.tensor_tensor(rank[:, bass.ds(at, 1)], rank[:, bass.ds(at, 1)], count[:, :], ALU.add
                                          ).then_inc(ranked, 1)
                dve.wait_ge(ranked, (CUT + 1) * CH * P)
                for c in range(CH):
                    with dve.Fori(0, P) as e:
                        at = e + c * P
                        dve.wait_ge(sent, at * 16)
                        dve.tensor_scalar(place[:, :], rank[:, bass.ds(at, 1)], 1.0, None, ALU.mult)
                        dve.tensor_scalar(record[:, 0:1], t.dst_i[:, c, bass.ds(e, 1)], 1.0, None, ALU.mult)
                        dve.tensor_scalar(record[:, 1:2], t.src_now[:, c, bass.ds(e, 1)], 1.0, None, ALU.mult
                                          ).then_inc(staged, 1)
                dve.wait_ge(reloaded, 16)
                dve.tensor_copy(t.dst_i[:, :, :], records[:, :, :, 0]).then_inc(split, 1)
                dve.tensor_copy(t.src_now[:, :, :], records[:, :, :, 1]).then_inc(split, 1)
                dve.wait_ge(reloaded, 32)
                dve.tensor_copy(t.prev_i[:, :, :], records[:, :, :, 0])


def build_tables(nc, t, d):
    with ExitStack() as ctx:
        sem = sem_maker(nc, ctx, "tab")

        def sb(name, shape, dt=F32):
            return ctx.enter_context(nc.sbuf_tensor(name, shape, dt))

        dst_f = sb("dst_f", [P, CH, P])
        src_f = sb("src_f", [P, CH, P])
        seg_start = sb("seg_start", [P, CH, P])
        ends_i = sb("ends_i", [P, 2, CH], I32)
        first = sb("first", [P, CH])
        last = sb("last", [P, CH])
        real_tile = sb("real_tile", [P, CH])
        pairs = sb("pairs", [P, CH])
        pairs_before = sb("pairs_before", [P, CH])
        begin = sb("begin", [P, CH])
        end = sb("end", [P, CH])
        shift = sb("shift", [P, CH])
        iota_k = sb("iota_k", [P, K])
        tile_no = sb("tile_no", [P, CH])
        upper = sb("upper", [P, P])
        at_or_after = sb("at_or_after", [P, CH, K])
        sel = sb("sel", [P, CH, K])
        bin_f = sb("bin_f", [P, K])
        no_pair = sb("no_pair", [P, K])
        base = sb("base", [P, K])
        bias_rows = sb("bias_rows", [P, CH, P])
        zeros = sb("zeros", [P, 2048])

        xloaded = sem("x_loaded")
        consts = sem("consts")
        chain = sem("vector_chain")
        pairs_ready = sem("pairs_ready")
        begin_ready = sem("begin_ready")
        sel_ready = sem("sel_ready")
        bins_done = sem("bins_done")
        tables_done = sem("tables_done")
        bias_done = sem("bias_done")
        bias_copied = sem("bias_copied")
        zeroed = sem("zeroed")
        stored = sem("stored")
        block = ctx.enter_context(nc.Block())

        @block.sync
        def _(sp):
            sp.dma_start(t.x[:, :].rearrange("p (b f) -> p b f", b=NB),
                         d.x.rearrange("(b p) f -> p b f", p=P)).then_inc(xloaded, 16)
            sp.wait_ge(zeroed, 1)
            for r in range(COPIES):
                for at in range(0, NP + P, 2048):
                    rows = min(2048, NP + P - at)
                    sp.dma_start(d.reversed[r][at:at + rows, :].rearrange("(p a) n -> p (a n)", p=P),
                                 zeros[:, 0:rows * SUP // P]).then_inc(stored, 16)
            sp.wait_ge(bias_copied, CH)
            for c in range(CH):
                n = min(P, K - c * P)
                sp.dma_start(d.bias[c * P * P:(c * P + n) * P].rearrange("(k e) -> k e", e=P),
                             bias_rows[0:n, c, :]).then_inc(stored, 16)
            sp.wait_ge(xloaded, 16)
            sp.wait_ge(stored, (COPIES * 2 + CH) * 16)

        @block.gpsimd
        def _(pool):
            f = dict(allow_small_or_imprecise_dtypes=True)
            pool.memset(t.ident[:, :], 0.0).then_inc(consts, 1)
            pool.iota(t.node[:, :], [[1, P]], base=0, channel_multiplier=0, **f).then_inc(consts, 1)
            pool.iota(iota_k[:, :], [[1, K]], base=0, channel_multiplier=0, **f).then_inc(consts, 1)
            pool.iota(tile_no[:, :], [[P, CH]], base=0, channel_multiplier=1, **f).then_inc(consts, 1)
            pool.iota(t.spare[:, :], [[0, 1]], base=NP, channel_multiplier=1, **f).then_inc(consts, 1)
            pool.wait_ge(consts, 5)
            pool.affine_select(out=t.ident[:, :], in_=t.ident[:, :], compare_op=ALU.not_equal, fill=1.0,
                               base=0, pattern=[[-1, P]], channel_multiplier=1).then_inc(consts, 1)
            pool.affine_select(out=upper[:, :], in_=t.ones[:, :], compare_op=ALU.is_gt, fill=0.0,
                               base=0, pattern=[[1, P]], channel_multiplier=-1).then_inc(consts, 1)
            pool.affine_select(out=t.lower[:, :], in_=t.ones[:, :], compare_op=ALU.is_gt, fill=0.0,
                               base=0, pattern=[[-1, P]], channel_multiplier=1).then_inc(consts, 1)
            pool.memset(t.real[:, 0, :], 1.0).then_inc(consts, 1)
            pool.affine_select(out=t.real[:, 1, :], in_=t.ones[:, :], compare_op=ALU.is_gt, fill=0.0,
                               base=LAST, pattern=[[0, P]], channel_multiplier=-1).then_inc(consts, 1)

        @block.vector
        def _(dve):
            n = [0]

            def done(ins):
                n[0] += 1
                ins.then_inc(chain, 1)
                dve.wait_ge(chain, n[0])

            dve.memset(zeros[:, :], 0.0).then_inc(zeroed, 1)
            dve.memset(t.eps[:, :], LN_EPS)
            for slot in range(SLOTS):
                for j in range(G):
                    dve.memset(t.rows[:, slot, j, D:D + 1], 1.0)
            dve.memset(t.acc[:, :], 0.0)
            dve.wait_ge(consts, 10)
            dve.tensor_copy(src_f[:, :, :], t.src_now[:, :, :])
            dve.tensor_copy(dst_f[:, :, :], t.dst_i[:, :, :])
            dve.tensor_tensor(seg_start[:, :, :], t.dst_i[:, :, :], t.prev_i[:, :, :], ALU.not_equal)
            dve.tensor_scalar(ends_i[:, 0, :], t.dst_i[:, :, 0], 7, None, ALU.arith_shift_right)
            done(dve.tensor_scalar(ends_i[:, 1, :], t.dst_i[:, :, P - 1], 7, None, ALU.arith_shift_right))
            dve.tensor_copy(first[:, :], ends_i[:, 0, :])
            dve.tensor_scalar(real_tile[:, :], tile_no[:, :], float(NT), None, ALU.is_lt)
            done(dve.tensor_scalar(last[:, :], ends_i[:, 1, :], 1.0, None, ALU.add))
            done(dve.tensor_tensor(pairs[:, :], last[:, :], first[:, :], ALU.subtract))
            done(dve.tensor_tensor(pairs[:, :], pairs[:, :], real_tile[:, :], ALU.mult))
            done(dve.memset(pairs_before[:, 0:1], 0.0))
            for c in range(1, CH):
                done(dve.tensor_tensor(pairs_before[:, c:c + 1], pairs_before[:, c - 1:c], pairs[:, c - 1:c], ALU.add))
            dve.tensor_copy(end[:, :], pairs[:, :]).then_inc(pairs_ready, 1)
            dve.wait_ge(begin_ready, 1)
            done(dve.tensor_copy(begin[:, :], t.ps[0][:, 0:CH]))
            dve.tensor_tensor(shift[:, :], first[:, :], begin[:, :], ALU.subtract)
            done(dve.tensor_tensor(end[:, :], begin[:, :], pairs[:, :], ALU.add))
            for c in range(CH):
                done(dve.tensor_scalar(at_or_after[:, c, :], iota_k[:, :], begin[:, c:c + 1], None, ALU.is_ge))
            for c in range(CH):
                dve.scalar_tensor_tensor(out=sel[:, c, :], in0=iota_k[:, :], scalar=end[:, c:c + 1],
                                         in1=at_or_after[:, c, :], op0=ALU.is_lt, op1=ALU.mult).then_inc(sel_ready, 1)
            dve.wait_ge(bins_done, 1)
            done(dve.tensor_tensor(base[:, :], t.ps[2][:, 0:K], iota_k[:, :], ALU.mult))
            done(dve.tensor_tensor(bin_f[:, :], t.ps[1][:, 0:K], base[:, :], ALU.add))
            dve.tensor_copy(t.bins[:, :], bin_f[0:1, :])
            dve.tensor_scalar(no_pair[:, :], t.ps[2][:, 0:K], -1.0, 1e6, ALU.add, ALU.mult)
            done(dve.tensor_scalar(base[:, :], bin_f[:, :], float(-P), None, ALU.mult))
            done(dve.tensor_tensor(base[:, :], base[:, :], no_pair[:, :], ALU.add))
            dve.wait_ge(tables_done, 1)
            dve.tensor_tensor(t.dst_at[:, :], t.ps[4][:, 0:K], base[:, :], ALU.add)
            dve.tensor_copy(t.src_i[:, :], t.ps[3][:, 0:K])
            dve.tensor_copy(t.src_at[:, :], t.ps[3][:, 0:K])
            for c in range(CH):
                m = min(P, K - c * P)
                dve.wait_ge(bias_done, c + 1)
                dve.tensor_scalar(bias_rows[0:m, c, :], t.ps[5 + c % 2][0:m, 0:P], -BIG, None,
                                  ALU.mult).then_inc(bias_copied, 1)

        @block.tensor
        def _(pe):
            pe.wait_ge(consts, 10)
            pe.wait_ge(pairs_ready, 1)
            pe.matmul(t.ps[0][:, 0:CH], upper[:, :], pairs[:, :], start=True, stop=False)
            pe.matmul(t.ps[0][:, 0:CH], t.ones[:, :], pairs_before[:, :], start=False, stop=True).then_inc(begin_ready, 1)
            pe.wait_ge(sel_ready, CH)
            for c in range(CH):
                pe.matmul(t.ps[1][:, 0:K], shift[:, c:c + 1].to_broadcast([P, P]), sel[:, c, :],
                          start=c == 0, stop=c == CH - 1)
            for c in range(CH):
                mm = pe.matmul(t.ps[2][:, 0:K], t.ones[:, :], sel[:, c, :], start=c == 0, stop=c == CH - 1)
            mm.then_inc(bins_done, 1)
            for out, table in ((t.ps[3], src_f), (t.ps[4], dst_f)):
                for c in range(CH):
                    mm = pe.matmul(out[:, 0:K], table[:, c, :], sel[:, c, :], start=c == 0, stop=c == CH - 1)
            mm.then_inc(tables_done, 1)
            for kc in range(CH):
                m = min(P, K - kc * P)
                if kc >= 2:
                    pe.wait_ge(bias_copied, kc - 1)
                for c in range(CH):
                    mm = pe.matmul(t.ps[5 + kc % 2][0:m, 0:P], sel[:, c, kc * P:kc * P + m], seg_start[:, c, :],
                                   start=c == 0, stop=c == CH - 1)
                mm.then_inc(bias_done, 1)


def aggregate(nc, t, d, phase, table, width, ones_column, find_twins=False):
    cols = width + ones_column
    with ExitStack() as ctx:
        sem = sem_maker(nc, ctx, phase)
        index_copied = sem("index_copied")
        index_taken = sem("index_taken")
        gathered = [sem(f"gathered{s}") for s in range(SLOTS)]
        onehot_ready = sem("onehot_ready")
        part_done = sem("part_done")
        added = sem("added")
        column_ready = sem("column_ready")
        row_ready = sem("row_ready")
        twins_counted = sem("twins_counted")
        twins_kept = sem("twins_kept")
        block = ctx.enter_context(nc.Block())

        @block.gpsimd
        def _(pool):
            def step(i, slot):
                if not isinstance(i, int) or i >= SLOTS:
                    pool.wait_ge(part_done, (i - SLOTS + 1) * G)
                pool.tensor_copy(t.index[:, slot, :], t.src_i[:, bass.ds(i * G, G)]).then_inc(index_copied, 1)
                pool.wait_ge(index_copied, i + 1)
                pool.sem_inc(index_taken, 1)
                for j in range(G):
                    pool.indirect_dma_start(t.rows[:, slot, j, 0:width], None, table,
                                            bass.IndirectOffsetOnAxis(t.index[:, slot, j:j + 1], 0)
                                            ).then_inc(gathered[slot], 16)
            over_batches(pool, step)

        @block.tensor
        def _(pe):
            def step(i, slot):
                pe.wait_ge(gathered[slot], (i - slot) * (16 * G // SLOTS) + 16 * G)
                for j in range(G):
                    k = i * G + j
                    pe.wait_ge(onehot_ready, k + 1)
                    two_back(pe, added, k)
                    pe.matmul(t.ps[j % 2][:, 0:cols], t.onehot[:, j % 4, :], t.rows[:, slot, j, 0:cols],
                              start=True, stop=True).then_inc(part_done, 1)
                    if find_twins:
                        pe.wait_ge(column_ready, i + 1)
                        two_back(pe, twins_counted, k)
                        pe.matmul(t.ps[2 + j % 2][:, 0:P], t.column[:, slot % 2, j:j + 1].to_broadcast([P, P]),
                                  t.ident[:, :], start=True, stop=True).then_inc(row_ready, 1)
            over_batches(pe, step)

        @block.vector
        def _(dve):
            def add(k, j):
                b = dve.value_load(t.bins[0:1, bass.ds(k, 1)], min_val=0, max_val=NB - 1)
                dve.wait_ge(part_done, k + 1)
                acc = t.acc[:, bass.ds(b * W, cols)]
                if not isinstance(k, int) or k >= 1:
                    dve.wait_ge(added, k)
                dve.tensor_tensor(acc, t.ps[j % 2][:, 0:cols], acc, ALU.add).then_inc(added, 1)

            def count_twins(i, slot, j, k):
                dve.wait_ge(row_ready, k + 1)
                dve.scalar_tensor_tensor(out=t.work[:, j % 2, 0:P], in0=t.ps[2 + j % 2][:, 0:P],
                                         scalar=t.column[:, slot % 2, j:j + 1], in1=t.lower[:, :],
                                         op0=ALU.is_equal, op1=ALU.mult,
                                         accum_out=t.twin_count[:, slot % 2, j:j + 1]).then_inc(twins_counted, 1)

            def step(i, slot):
                if find_twins:
                    if not isinstance(i, int) or i >= 1:
                        dve.wait_ge(twins_counted, i * G)
                        dve.tensor_copy(t.twins[:, bass.ds((i - 1) * G, G)],
                                        t.twin_count[:, (slot - 1) % 2, :]).then_inc(twins_kept, 1)
                        dve.wait_ge(twins_kept, i)
                    dve.tensor_copy(t.column[:, slot % 2, :], t.src_at[:, bass.ds(i * G, G)]).then_inc(column_ready, 1)
                for j in range(G):
                    k = i * G + j
                    if not isinstance(k, int) or k >= 4:
                        dve.wait_ge(part_done, k - 3)
                    dve.tensor_scalar(t.onehot[:, j % 4, :], t.node[:, :], t.dst_at[:, bass.ds(k, 1)], None,
                                      ALU.is_equal).then_inc(onehot_ready, 1)
                    if not isinstance(k, int) or k >= 2:
                        add(k - 2, j)
                    if find_twins and j >= 1:
                        count_twins(i, slot, j - 1, k - 1)
                if find_twins:
                    count_twins(i, slot, G - 1, i * G + G - 1)
            over_batches(dve, step)
            add(K - 2, 0)
            add(K - 1, 1)
            if find_twins:
                dve.wait_ge(twins_counted, K)
                dve.tensor_copy(t.twins[:, K - G:K], t.twin_count[:, (SLOTS - 1) % 2, :])


def weights(nc, ctx, name, dram):
    tile = ctx.enter_context(nc.sbuf_tensor(f"sb_{name}", [P, dram.shape[0] // P, dram.shape[1]], F32))
    return tile, tile[:, :, :], dram.rearrange("(c p) n -> p c n", p=P)


def vector(nc, ctx, name, dram):
    tile = ctx.enter_context(nc.sbuf_tensor(f"sb_{name}", [P, dram.shape[0]], F32))
    return tile, tile[:, :], dram.partition_broadcast(P)


def load(sp, loads, loaded):
    for _, tile, dram in loads:
        sp.dma_start(tile, dram).then_inc(loaded, 16)


def started(b, lag=0):
    return not isinstance(b, int) or 0 <= b - lag < NB


def two_back(eng, signal, b):
    if not isinstance(b, int) or b >= 2:
        eng.wait_ge(signal, b - 1)


def norm_sems(sem):
    norm = Named()
    norm.summed, norm.waited, norm.stats, norm.moments = sem("summed"), sem("waited"), sem("stats"), sem("moments")
    norm.std, norm.rstd, norm.normed = sem("std"), sem("rstd"), sem("normed")
    return norm


def norm_moments(dve, t, s, b, par):
    dve.wait_ge(s.summed, b + 1)
    dve.bn_stats(t.stats[:, par, :], t.s2[:, par, :]).then_inc(s.stats, 1)
    dve.wait_ge(s.stats, b + 1)
    dve.sem_inc(s.waited, 1)
    dve.bn_aggr(t.mv[:, par, :], t.stats[:, par, :]).then_inc(s.moments, 1)


def norm_std(act, t, s, b, par):
    act.wait_ge(s.moments, b + 1)
    act.activation(t.std[:, par, :], t.mv[:, par, 1:2], ACT.Sqrt, bias=t.eps[:, :]).then_inc(s.std, 1)


def norm_apply(dve, t, s, b, par, out):
    dve.wait_ge(s.std, b + 1)
    dve.reciprocal(t.rstd[:, par, :], t.std[:, par, :]).then_inc(s.rstd, 1)
    dve.wait_ge(s.rstd, b + 1)
    dve.tensor_scalar(out, t.s2[:, par, :], t.mv[:, par, 0:1], t.rstd[:, par, :],
                      ALU.subtract, ALU.mult).then_inc(s.normed, 1)


def turn(pe, t, src, par, signal, blocks=2):
    for c in range(blocks):
        mm = pe.transpose(t.ps[par][:, c * P:(c + 1) * P], src[:, c * P:(c + 1) * P], t.ident[:, :])
    mm.then_inc(signal, 1)


def store_bins(sp, t, src, stride, width, dram, ready, stored):
    def step(b, par):
        sp.wait_ge(ready, b + 1)
        sp.dma_start(dram[bass.ds(b * P, P), :], src[:, bass.ds(b * stride, width)]).then_inc(stored, 16)
    over_bins(sp, step)
    sp.wait_ge(stored, 16 * NB)


def dense0(nc, t, d):
    with ExitStack() as ctx:
        sem = sem_maker(nc, ctx, "d0")
        loads = [weights(nc, ctx, "W0", d.W0T), vector(nc, ctx, "b0", d.L0_gnn_b)]
        W0, b0 = (x[0] for x in loads)
        loaded = sem("loaded")
        degree = sem("degree")
        inverse = sem("inverse")
        mean_ready = sem("mean_ready")
        turned = sem("turned")
        turned_copied = sem("turned_copied")
        product_done = sem("product_done")
        biased = sem("biased")
        norm = norm_sems(sem)
        stored = sem("stored")
        block = ctx.enter_context(nc.Block())

        @block.vector
        def _(dve):
            dve.wait_ge(loaded, 32)

            def step(b, par):
                if started(b):
                    two_back(dve, turned, b)
                    dve.tensor_scalar(t.degree[:, par, :], t.acc[:, bass.ds(b * W + D, 1)], 1.0, None,
                                      ALU.max).then_inc(degree, 1)
                    dve.wait_ge(degree, b + 1)
                    dve.reciprocal(t.inv_deg[:, bass.ds(b, 1)], t.degree[:, par, :]).then_inc(inverse, 1)
                    dve.wait_ge(inverse, b + 1)
                    dve.tensor_scalar(t.work[:, par, 0:D], t.acc[:, bass.ds(b * W, D)], t.inv_deg[:, bass.ds(b, 1)],
                                      None, ALU.mult).then_inc(mean_ready, 1)
                if started(b, 1):
                    o, q = b - 1, 1 - par
                    dve.wait_ge(product_done, o + 1)
                    dve.tensor_tensor(t.s1[:, q, :], t.ps[2 + q][:, 0:D], b0[:, :], ALU.add).then_inc(biased, 1)
                    dve.wait_ge(biased, o + 1)
                    dve.scalar_tensor_tensor(out=t.s2[:, q, :], in0=t.s1[:, q, :], scalar=0.0,
                                             in1=t.x[:, bass.ds(o * D, D)], op0=ALU.max, op1=ALU.add
                                             ).then_inc(norm.summed, 1)
                    norm_moments(dve, t, norm, o, q)
                if started(b, 2):
                    norm_apply(dve, t, norm, b - 2, par, t.x[:, bass.ds((b - 2) * D, D)])
            over_bins(dve, step, lag=2)
            dve.memset(t.acc[:, :], 0.0)

        @block.tensor
        def _(pe):
            pe.wait_ge(loaded, 32)

            def step(b, par):
                if started(b):
                    pe.wait_ge(mean_ready, b + 1)
                    two_back(pe, turned_copied, b)
                    turn(pe, t, t.work[:, par, :], par, turned)
                if started(b, 1):
                    o, q = b - 1, 1 - par
                    pe.wait_ge(turned_copied, o + 1)
                    if not isinstance(b, int) or o >= 2:
                        pe.wait_ge(biased, o - 1)
                    for c in range(2):
                        mm = pe.matmul(t.ps[2 + q][:, 0:D], t.turned[:, q, c * P:(c + 1) * P], W0[:, c, :],
                                       start=c == 0, stop=c == 1)
                    mm.then_inc(product_done, 1)
            over_bins(pe, step, lag=1)

        @block.scalar
        def _(act):
            def step(b, par):
                if started(b):
                    act.wait_ge(turned, b + 1)
                    two_back(act, product_done, b)
                    act.copy(t.turned[:, par, 0:D], t.ps[par][:, 0:D]).then_inc(turned_copied, 1)
                if started(b, 1):
                    norm_std(act, t, norm, b - 1, 1 - par)
            over_bins(act, step, lag=1)

        @block.sync
        def _(sp):
            load(sp, loads, loaded)
            store_bins(sp, t, t.x, D, D, d.x1, norm.normed, stored)


def dense1(nc, t, d):
    with ExitStack() as ctx:
        sem = sem_maker(nc, ctx, "d1")
        loads = [weights(nc, ctx, "Wl", d.WlT), weights(nc, ctx, "Wr", d.WrT), vector(nc, ctx, "bl", d.L1_gnn_b_l),
                 vector(nc, ctx, "gamma", d.L1_gnn_gamma), vector(nc, ctx, "beta", d.L1_gnn_beta)]
        Wl, Wr, bl, gamma, beta = (x[0] for x in loads)
        col_mean = ctx.enter_context(nc.sbuf_tensor("col_mean", [P, D], F32))
        col_var = ctx.enter_context(nc.sbuf_tensor("col_var", [P, D], F32))
        loaded = sem("loaded")
        inputs_ready = sem("inputs_ready")
        turned = sem("turned")
        turned_copied = sem("turned_copied")
        product_done = sem("product_done")
        biased = sem("biased")
        squares_ready = sem("squares_ready")
        length_ready = sem("length_ready")
        length_kept = sem("length_kept")
        inverse = sem("inverse")
        unit_ready = sem("unit_ready")
        columns_summed = sem("columns_summed")
        column_mean = sem("column_mean")
        centred = sem("centred")
        squared = sem("squared")
        squares_summed = sem("squares_summed")
        column_var = sem("column_var")
        column_std = sem("column_std")
        gain = sem("gain")
        scaled = sem("scaled")
        shifted = sem("shifted")
        norm = norm_sems(sem)
        stored = sem("stored")
        block = ctx.enter_context(nc.Block())

        def row(b):
            return t.acc[:, bass.ds(b * W, D)]

        def column_sum(pe, bank, rows, b, signal):
            first = isinstance(b, int) and b == 0
            last = isinstance(b, int) and b == NB - 1
            pe.matmul(t.ps[bank][:, 0:D], t.real[:, int(last), :], rows, start=first, stop=last,
                      skip_group_check=True).then_inc(signal, 1)

        @block.vector
        def _(dve):
            dve.wait_ge(loaded, 80)

            def rows(b, par):
                if started(b):
                    two_back(dve, turned, b)
                    dve.tensor_scalar(t.work[:, par, 0:D], row(b), t.inv_deg[:, bass.ds(b, 1)], None, ALU.mult)
                    dve.tensor_scalar(t.work[:, par, D:2 * D], t.x[:, bass.ds(b * D, D)], 1.0, None,
                                      ALU.mult).then_inc(inputs_ready, 1)
                if started(b, 1):
                    o, q = b - 1, 1 - par
                    dve.wait_ge(product_done, o + 1)
                    two_back(dve, unit_ready, o)
                    dve.tensor_tensor(t.s1[:, q, :], t.ps[2 + q][:, 0:D], bl[:, :], ALU.add).then_inc(biased, 1)
                if started(b, 2):
                    o = b - 2
                    dve.wait_ge(length_ready, o + 1)
                    dve.tensor_scalar(t.rstd[:, par, :], t.std[:, par, :], 1e-12, None, ALU.max).then_inc(length_kept, 1)
                    dve.wait_ge(length_kept, o + 1)
                    dve.reciprocal(t.degree[:, par, :], t.rstd[:, par, :]).then_inc(inverse, 1)
                    dve.wait_ge(inverse, o + 1)
                    dve.tensor_scalar(row(o), t.s1[:, par, :], t.degree[:, par, :], None, ALU.mult).then_inc(unit_ready, 1)
            over_bins(dve, rows, lag=2)
            dve.wait_ge(columns_summed, NB)
            dve.tensor_scalar(col_mean[:, :], t.ps[4][:, 0:D], 1.0 / N, None, ALU.mult).then_inc(column_mean, 1)
            dve.wait_ge(column_mean, 1)

            def centre(b, par):
                dve.tensor_tensor(row(b), row(b), col_mean[:, :], ALU.subtract).then_inc(centred, 1)
                dve.wait_ge(centred, b + 1)
                two_back(dve, squares_summed, b)
                dve.tensor_tensor(t.s2[:, par, :], row(b), row(b), ALU.mult).then_inc(squared, 1)
            over_bins(dve, centre)
            dve.wait_ge(squares_summed, NB)
            dve.tensor_scalar(col_var[:, :], t.ps[5][:, 0:D], 1.0 / N, None, ALU.mult).then_inc(column_var, 1)
            dve.wait_ge(column_std, 1)
            dve.reciprocal(col_var[:, :], col_mean[:, :]).then_inc(gain, 1)
            dve.wait_ge(gain, 1)
            dve.tensor_tensor(col_mean[:, :], col_var[:, :], gamma[:, :], ALU.mult).then_inc(gain, 1)
            dve.wait_ge(gain, 2)

            def finish_rows(b, par):
                if started(b):
                    dve.tensor_tensor(t.s1[:, par, :], row(b), col_mean[:, :], ALU.mult).then_inc(scaled, 1)
                    dve.wait_ge(scaled, b + 1)
                    dve.tensor_tensor(t.work[:, par, 0:D], t.s1[:, par, :], beta[:, :], ALU.add).then_inc(shifted, 1)
                    dve.wait_ge(shifted, b + 1)
                    dve.scalar_tensor_tensor(out=t.s2[:, par, :], in0=t.work[:, par, 0:D], scalar=0.0,
                                             in1=t.x[:, bass.ds(b * D, D)], op0=ALU.max, op1=ALU.add
                                             ).then_inc(norm.summed, 1)
                    norm_moments(dve, t, norm, b, par)
                if started(b, 1):
                    norm_apply(dve, t, norm, b - 1, 1 - par, t.x[:, bass.ds((b - 1) * D, D)])
            over_bins(dve, finish_rows, lag=1)
            dve.memset(t.acc[:, :], 0.0)

        @block.tensor
        def _(pe):
            pe.wait_ge(loaded, 80)

            def rows(b, par):
                if started(b):
                    pe.wait_ge(inputs_ready, b + 1)
                    two_back(pe, turned_copied, b)
                    turn(pe, t, t.work[:, par, :], par, turned, 4)
                if started(b, 1):
                    o, q = b - 1, 1 - par
                    pe.wait_ge(turned_copied, o + 1)
                    if not isinstance(b, int) or o >= 2:
                        pe.wait_ge(biased, o - 1)
                    for c in range(4):
                        mm = pe.matmul(t.ps[2 + q][:, 0:D], t.turned[:, q, c * P:(c + 1) * P],
                                       (Wl, Wr)[c // 2][:, c % 2, :], start=c == 0, stop=c == 3)
                    mm.then_inc(product_done, 1)
                if started(b, 3):
                    pe.wait_ge(unit_ready, b - 2)
                    column_sum(pe, 4, row(b - 3), b - 3, columns_summed)
            over_bins(pe, rows, lag=3)

            def squares(b, par):
                pe.wait_ge(squared, b + 1)
                column_sum(pe, 5, t.s2[:, par, :], b, squares_summed)
            over_bins(pe, squares)

        @block.scalar
        def _(act):
            def rows(b, par):
                if started(b):
                    act.wait_ge(turned, b + 1)
                    two_back(act, product_done, b)
                    act.copy(t.turned[:, par, :], t.ps[par][:, 0:2 * D]).then_inc(turned_copied, 1)
                if started(b, 1):
                    o, q = b - 1, 1 - par
                    act.wait_ge(biased, o + 1)
                    act.activation(t.s2[:, q, :], t.s1[:, q, :], ACT.Square,
                                   accum_out=t.squares[:, q, :]).then_inc(squares_ready, 1)
                    act.wait_ge(squares_ready, o + 1)
                    act.sqrt(t.std[:, q, :], t.squares[:, q, :]).then_inc(length_ready, 1)
            over_bins(act, rows, lag=1)
            act.wait_ge(column_var, 1)
            act.activation(col_mean[:, :], col_var[:, :], ACT.Sqrt, bias=t.eps[:, :]).then_inc(column_std, 1)

            def finish_rows(b, par):
                norm_std(act, t, norm, b, par)
            over_bins(act, finish_rows)

        @block.sync
        def _(sp):
            load(sp, loads, loaded)
            store_bins(sp, t, t.x, D, D, d.x2, norm.normed, stored)


def project(nc, t, d, layer):
    with ExitStack() as ctx:
        sem = sem_maker(nc, ctx, f"p{layer}")
        loads = [weights(nc, ctx, f"{w}{layer}", dram[layer])
                 for w, dram in (("wq", d.L2_gnn_Wq), ("wk", d.L2_gnn_Wk), ("wv", d.L2_gnn_Wv))]
        wq, wk, wv = (x[0] for x in loads)
        kv = ctx.enter_context(nc.sbuf_tensor(f"kv_out{layer}", [P, 2, KV], F32))
        loaded = sem("weights_loaded")
        gap_ready = sem("gap_ready")
        input_ready = sem("input_ready")
        turned = sem("turned")
        turned_copied = sem("turned_copied")
        query_done = sem("query_done")
        kv_done = sem("kv_done")
        query_kept = sem("query_kept")
        kv_copied = sem("kv_copied")
        stored = [sem(f"stored{p}") for p in range(2)]
        block = ctx.enter_context(nc.Block())

        @block.vector
        def _(dve):
            dve.memset(kv[:, :, D:W], 0.0).then_inc(gap_ready, 1)

            def step(b, par):
                if started(b):
                    two_back(dve, turned, b)
                    dve.tensor_scalar(t.work[:, par, 0:D], t.x[:, bass.ds(b * D, D)], 1.0, None,
                                      ALU.mult).then_inc(input_ready, 1)
                if started(b, 1):
                    o, q = b - 1, 1 - par
                    dve.wait_ge(query_done, o + 1)
                    dve.tensor_scalar(t.q[:, bass.ds(o * D, D)], t.ps[2 + q][:, 0:D], 1.0, None,
                                      ALU.mult).then_inc(query_kept, 1)
            over_bins(dve, step, lag=1)

        @block.tensor
        def _(pe):
            pe.wait_ge(loaded, 48)

            def step(b, par):
                if started(b):
                    pe.wait_ge(input_ready, b + 1)
                    two_back(pe, turned_copied, b)
                    turn(pe, t, t.work[:, par, :], par, turned)
                if started(b, 1):
                    o, q = b - 1, 1 - par
                    pe.wait_ge(turned_copied, o + 1)
                    two_back(pe, query_kept, o)
                    for c in range(2):
                        mm = pe.matmul(t.ps[2 + q][:, 0:D], t.turned[:, q, c * P:(c + 1) * P], wq[:, c, :],
                                       start=c == 0, stop=c == 1)
                    mm.then_inc(query_done, 1)
                    two_back(pe, kv_copied, o)
                    for n, w in enumerate((wk, wv)):
                        for c in range(2):
                            mm = pe.matmul(t.ps[4 + q][:, n * D:(n + 1) * D], t.turned[:, q, c * P:(c + 1) * P],
                                           w[:, c, :], start=c == 0, stop=c == 1)
                    mm.then_inc(kv_done, 1)
            over_bins(pe, step, lag=1)

        @block.scalar
        def _(act):
            act.wait_ge(gap_ready, 1)

            def step(b, par):
                if started(b):
                    act.wait_ge(turned, b + 1)
                    two_back(act, kv_done, b)
                    act.copy(t.turned[:, par, 0:D], t.ps[par][:, 0:D]).then_inc(turned_copied, 1)
                if started(b, 1):
                    o, q = b - 1, 1 - par
                    act.wait_ge(kv_done, o + 1)
                    if not isinstance(o, int) or o >= 2:
                        act.wait_ge(stored[q], (o - q) * 8)
                    act.copy(kv[:, q, 0:D], t.ps[4 + q][:, 0:D])
                    act.copy(kv[:, q, W:KV], t.ps[4 + q][:, D:2 * D]).then_inc(kv_copied, 1)
            over_bins(act, step, lag=1)

        @block.sync
        def _(sp):
            load(sp, loads, loaded)

            def step(b, par):
                sp.wait_ge(kv_copied, b + 1)
                sp.dma_start(d.kv[bass.ds(b * P, P), :], kv[:, par, :]).then_inc(stored[par], 16)
            over_bins(sp, step)
            sp.wait_ge(stored[0], 16 * (NB - NB // 2))
            sp.wait_ge(stored[1], 16 * (NB // 2))


def attend(nc, t, d, layer):
    QUERY, SCORE, MESSAGE, PART, SUM = G, G + 1, 2 * G + 5, 2 * G + 6, 2 * G + 7
    HG = G // 2
    with ExitStack() as ctx:
        sem = sem_maker(nc, ctx, f"at{layer}")

        def sb(name, shape):
            return ctx.enter_context(nc.sbuf_tensor(f"{name}{layer}", shape, F32))

        onehot = sb("edge_node", [P, SLOTS, G, P])
        onehot_t = sb("node_edge", [P, 2, HG, P])
        product = t.s1
        scores = sb("scores", [P, 2, G * H])
        below = sb("below", [P, 2, G * H])
        fresh = sb("fresh", [H, 2, G * P + 1])
        run_max = sb("run_max", [H, 2, G * P])
        seg_max = t.work[0:H, :, :].rearrange("p a b -> p (a b)")
        first_max = sb("first_max", [1, H])
        drop = sb("drop", [1, H])
        shrink = sb("shrink", [1, H])
        shrink_less_1 = sb("shrink_less_1", [1, H])

        index_copied = sem("index_copied")
        index_taken = sem("index_taken")
        gathered = [sem(f"gathered{s}") for s in range(SLOTS)]
        fresh_loaded = [sem(f"fresh_loaded{p}") for p in range(2)]
        distance_ready = sem("distance_ready")
        distance_free = sem("distance_free")
        onehot_ready = sem("onehot_ready")
        onehot_turned = sem("onehot_turned")
        onehot_t_copied = sem("onehot_t_copied")
        query_done = sem("query_done")
        product_ready = sem("product_ready")
        score_ready = sem("score_ready")
        score_turned = sem("score_turned")
        run_max_ready = sem("run_max_ready")
        seg_max_ready = sem("seg_max_ready")
        max_turned = sem("max_turned")
        below_ready = sem("below_ready")
        weight_ready = sem("weight_ready")
        first_kept = sem("first_kept")
        drop_ready = sem("drop_ready")
        shrink_ready = sem("shrink_ready")
        shrink_used = sem("shrink_used")
        spread_done = sem("spread_done")
        message_ready = sem("message_ready")
        rescaled = sem("rescaled")
        waited = sem("waited")
        part_done = sem("part_done")
        added = sem("added")
        block = ctx.enter_context(nc.Block())

        turned_bank = t.ps[0]
        score_bank = t.ps[5]
        weight = t.ps[6][:, 0:G * H]
        max_cols = t.ps[7][:, 0:G * H]
        old_max = t.ps[7][0:1, G * H:G * H + H]
        spread = t.ps[7][:, 256:256 + H]

        def in_loop(i):
            return not isinstance(i, int)

        def has_pair(k):
            return in_loop(k) or 0 <= k < K

        def has_batch(b):
            return in_loop(b) or 0 <= b < NBATCH

        def place(slot, j, lag):
            n = (slot * G + j - lag) % (SLOTS * G)
            return n // G, n % G

        @block.sync
        def _(sp):
            def step(i, slot):
                if in_loop(i) or i >= 2:
                    sp.wait_ge(seg_max_ready, i - 1)
                sp.dma_start(fresh[:, slot % 2, 0:G * P],
                             d.bias[bass.ds(i * G * P, G * P)].partition_broadcast(H)
                             ).then_inc(fresh_loaded[slot % 2], 16)
            over_batches(sp, step)

        @block.gpsimd
        def _(pool):
            def step(i, slot):
                if in_loop(i) or i >= SLOTS:
                    pool.wait_ge(part_done, (i - SLOTS + 1) * G)
                pool.tensor_copy(t.index[:, slot, :], t.src_i[:, bass.ds(i * G, G)]).then_inc(index_copied, 1)
                pool.wait_ge(index_copied, i + 1)
                pool.sem_inc(index_taken, 1)
                for j in range(G):
                    pool.indirect_dma_start(t.rows[:, slot, j, :], None, d.kv,
                                            bass.IndirectOffsetOnAxis(t.index[:, slot, j:j + 1], 0)
                                            ).then_inc(gathered[slot], 16)
            over_batches(pool, step)

        @block.tensor
        def _(pe):
            def turn_onehots(b, slot, half):
                pe.wait_ge(onehot_ready, 2 * b + half + 1)
                if in_loop(b) or 2 * b + half >= 1:
                    pe.wait_ge(onehot_t_copied, 2 * b + half)
                for j in range(HG):
                    mm = pe.transpose(turned_bank[:, j * P:(j + 1) * P], onehot[:, slot, half * HG + j, :],
                                      t.ident[:, :])
                mm.then_inc(onehot_turned, 1)

            def query(b, k, j):
                bin_ = pe.value_load(t.bins[0:1, bass.ds(k, 1)], min_val=0, max_val=NB - 1)
                if j % HG == 0:
                    pe.wait_ge(onehot_t_copied, 2 * b + j // HG + 1)
                two_back(pe, product_ready, k)
                pe.matmul(t.ps[1 + j % 2][:, 0:D], onehot_t[:, j // HG, j % HG, :], t.q[:, bass.ds(bin_ * D, D)],
                          start=True, stop=True).then_inc(query_done, 1)

            def turn_scores(b, par, half):
                pe.wait_ge(score_ready, b * G + (half + 1) * HG)
                if in_loop(b) or 2 * b + half >= 1:
                    pe.wait_ge(run_max_ready, 2 * b + half)
                for j in range(HG):
                    col = (half * HG + j) * H
                    mm = pe.transpose(score_bank[0:H, j * P:(j + 1) * P], scores[:, par, col:col + H], t.ident[:, :])
                mm.then_inc(score_turned, 1)

            def turn_max(b, par):
                pe.wait_ge(seg_max_ready, b + 1)
                if in_loop(b) or b >= 1:
                    pe.wait_ge(below_ready, b)
                if in_loop(b) or b >= 2:
                    pe.wait_ge(rescaled, b - 1)
                pe.sem_inc(waited, 1)
                for j in range(G):
                    mm = pe.transpose(max_cols[:, j * H:(j + 1) * H], seg_max[:, j * P:(j + 1) * P],
                                      t.ident[0:H, 0:H])
                if in_loop(b) or b >= 1:
                    mm = pe.transpose(old_max, run_max[:, 1 - par, G * P - 1:G * P], t.ident[0:H, 0:H])
                mm.then_inc(max_turned, 1)

            def spread_shrink(b, slot):
                pe.wait_ge(shrink_used, b)
                pe.matmul(spread, onehot[0:1, slot, 0, :], shrink_less_1[:, :], start=True,
                          stop=True).then_inc(spread_done, 1)

            def part(k, slot, j):
                pe.wait_ge(message_ready, k + 1)
                two_back(pe, added, k)
                pe.matmul(t.ps[3 + j % 2][:, 0:W], onehot[:, slot, j, :], t.rows[:, slot, j, 0:W],
                          start=True, stop=True).then_inc(part_done, 1)

            def step(i, slot):
                for j in range(G):
                    s = i * G + j
                    if j == 0 and has_batch(i - 1):
                        turn_onehots(i - 1, (slot - 1) % SLOTS, 1)
                    if j == HG and has_batch(i):
                        turn_onehots(i, slot, 0)
                    if has_pair(s - QUERY):
                        query(i - 1, s - QUERY, j)
                    if j == 1 and has_batch(i - 2):
                        turn_scores(i - 2, slot % 2, 1)
                    if j == HG + 1 and has_batch(i - 1):
                        turn_scores(i - 1, 1 - slot % 2, 0)
                    if j == 3 and has_batch(i - 2):
                        turn_max(i - 2, slot % 2)
                    if j == 6 and has_batch(i - 2) and (in_loop(i) or i >= 3):
                        spread_shrink(i - 2, (slot - 2) % SLOTS)
                    if has_pair(s - PART):
                        part(s - PART, *place(slot, j, PART))
            over_batches(pe, step, lag=3)

        @block.scalar
        def _(act):
            def find_onehot(i, k, slot, j):
                half = j // HG
                if j % HG == 0 and (in_loop(i) or i >= SLOTS):
                    act.wait_ge(part_done, k + HG - SLOTS * G)
                    act.sem_inc(distance_free, 1)
                act.activation(onehot[:, slot, j, :], t.node[:, :], ACT.Abs, scale=-1.0,
                               bias=t.dst_at[:, bass.ds(k, 1)]).then_inc(distance_ready, 1)
                if j % HG == HG - 1:
                    act.wait_ge(distance_ready, k + 1)
                    four = onehot[:, slot, half * HG:(half + 1) * HG, :]
                    act.activation(four, four, ACT.Relu, scale=-1.0, bias=1.0).then_inc(onehot_ready, 1)

            def copy_turned(b, half):
                act.wait_ge(onehot_turned, 2 * b + half + 1)
                if in_loop(b) or b >= 1:
                    act.wait_ge(query_done, (b - 1) * G + (half + 1) * HG)
                act.copy(onehot_t[:, half, :, :], turned_bank[:, :].rearrange("p (j n) -> p j n", j=HG)
                         ).then_inc(onehot_t_copied, 1)

            def find_weights(b, slot):
                par = slot % 2
                act.wait_ge(below_ready, b + 1)
                if in_loop(b) or b >= 1:
                    act.wait_ge(message_ready, b * G)
                act.activation(weight, below[:, par, :], ACT.Exp, scale=SCALE).then_inc(weight_ready, 1)
                z = t.rows[:, slot, :, 0:W].rearrange("p j (h e) -> p j h e", h=H)[:, :, :, DK]
                act.activation(z, below[:, par, :].rearrange("p (j h) -> p j h", j=G), ACT.Exp,
                               scale=SCALE).then_inc(weight_ready, 1)
                if in_loop(b) or b >= 1:
                    act.wait_ge(drop_ready, b)
                    if in_loop(b) or b >= 2:
                        act.wait_ge(shrink_used, b - 1)
                    act.activation(shrink[:, :], drop[:, :], ACT.Exp, scale=SCALE).then_inc(shrink_ready, 1)

            def step(i, slot):
                for j in range(G):
                    if j == 1 and has_batch(i - 1):
                        copy_turned(i - 1, 1)
                    if j == HG + 1 and has_batch(i):
                        copy_turned(i, 0)
                    if j == 4 and has_batch(i - 2):
                        find_weights(i - 2, (slot - 2) % SLOTS)
                    if has_batch(i):
                        find_onehot(i, i * G + j, slot, j)
            over_batches(act, step, lag=3)

        @block.vector
        def _(dve):
            for par in range(2):
                dve.memset(fresh[:, par, G * P:G * P + 1], 0.0)

            def multiply(b, k, slot, j):
                if j == 0:
                    dve.wait_ge(gathered[slot], (b - slot) * (16 * G // SLOTS) + 16 * G)
                dve.wait_ge(query_done, k + 1)
                two_back(dve, score_ready, k)
                dve.tensor_tensor(product[:, j % 2, :], t.ps[1 + j % 2][:, 0:D], t.rows[:, slot, j, 0:D],
                                  ALU.mult).then_inc(product_ready, 1)

            def score(b, k, slot, j):
                dve.wait_ge(product_ready, k + 1)
                if j == 0 and (in_loop(b) or b >= 2):
                    dve.wait_ge(below_ready, b - 1)
                dve.tensor_reduce(scores[:, slot % 2, j * H:(j + 1) * H],
                                  product[:, j % 2, :].rearrange("p (h e) -> p h e", h=H), AX_X, ALU.add
                                  ).then_inc(score_ready, 1)

            half = G * P // 2

            def first_scan(b, par):
                dve.wait_ge(fresh_loaded[par], (b - par) * 8 + 16)
                dve.wait_ge(score_turned, 2 * b + 1)
                if in_loop(b) or b >= 1:
                    dve.wait_ge(max_turned, b)
                    dve.wait_ge(seg_max_ready, b)
                start = run_max[:, 1 - par, G * P - 1:G * P] if in_loop(b) or b >= 1 else -BIG
                dve.tensor_tensor_scan(run_max[:, par, 0:half], fresh[:, par, 0:half], score_bank[0:H, :], start,
                                       ALU.add, ALU.max).then_inc(run_max_ready, 1)

            def scans(b, par):
                dve.wait_ge(score_turned, 2 * b + 2)
                dve.wait_ge(run_max_ready, b * 2 + 1)
                dve.tensor_tensor_scan(run_max[:, par, half:2 * half], fresh[:, par, half:2 * half], score_bank[0:H, :],
                                       run_max[:, par, half - 1:half], ALU.add, ALU.max).then_inc(run_max_ready, 1)
                dve.wait_ge(run_max_ready, b * 2 + 2)
                dve.tensor_tensor_scan(seg_max[:, ::-1], fresh[:, par, 1:G * P + 1][:, ::-1],
                                       run_max[:, par, ::-1], -BIG, ALU.add, ALU.max).then_inc(seg_max_ready, 1)

            def compare(b, par):
                dve.wait_ge(max_turned, b + 1)
                if in_loop(b) or b >= 2:
                    dve.wait_ge(weight_ready, 2 * (b - 1))
                dve.tensor_tensor(below[:, par, :], scores[:, par, :], max_cols, ALU.subtract).then_inc(below_ready, 1)
                if in_loop(b) or b >= 1:
                    if in_loop(b) or b >= 2:
                        dve.wait_ge(drop_ready, b - 1)
                    dve.tensor_copy(first_max[:, :], max_cols[0:1, 0:H]).then_inc(first_kept, 1)

            def find_drop(b):
                dve.wait_ge(first_kept, b)
                if in_loop(b) or b >= 2:
                    dve.wait_ge(shrink_ready, b - 1)
                dve.tensor_tensor(drop[:, :], old_max, first_max[:, :], ALU.subtract).then_inc(drop_ready, 1)

            def less_1(b):
                dve.wait_ge(shrink_ready, b)
                if in_loop(b) or b >= 2:
                    dve.wait_ge(spread_done, b - 1)
                dve.tensor_scalar(shrink_less_1[:, :], shrink[:, :], 1.0, -1.0, ALU.min, ALU.add).then_inc(shrink_used, 1)

            def message(b, k, slot, j):
                if j == 0:
                    dve.wait_ge(weight_ready, 2 * (b + 1))
                out = t.rows[:, slot, j, 0:W].rearrange("p (h e) -> p h e", h=H)[:, :, 0:DK]
                w = weight[:, j * H:(j + 1) * H].unsqueeze(2).to_broadcast([P, H, DK])
                dve.tensor_tensor(out, t.rows[:, slot, j, W:KV].rearrange("p (h e) -> p h e", h=H), w,
                                  ALU.mult).then_inc(message_ready, 1)

            def add(b, k, j):
                bin_ = dve.value_load(t.bins[0:1, bass.ds(k, 1)], min_val=0, max_val=NB - 1)
                acc = t.acc[:, bass.ds(bin_ * W, W)]
                if in_loop(k) or k >= 1:
                    dve.wait_ge(added, k)
                if j == 0 and (in_loop(b) or b >= 1):
                    dve.wait_ge(spread_done, b)
                    heads = acc.rearrange("p (h e) -> p h e", h=H)
                    dve.scalar_tensor_tensor(out=heads, in0=spread.unsqueeze(2).to_broadcast([P, H, HZ]), scalar=1.0,
                                             in1=heads, op0=ALU.add, op1=ALU.mult).then_inc(rescaled, 1)
                    dve.wait_ge(rescaled, b)
                dve.wait_ge(part_done, k + 1)
                dve.tensor_tensor(acc, t.ps[3 + j % 2][:, 0:W], acc, ALU.add).then_inc(added, 1)

            def step(i, slot):
                for j in range(G):
                    s = i * G + j
                    if j == HG + 2 and has_batch(i - 1):
                        first_scan(i - 1, 1 - slot % 2)
                    if j == 2 and has_batch(i - 2):
                        scans(i - 2, slot % 2)
                    if j == 4 and has_batch(i - 2):
                        compare(i - 2, slot % 2)
                    its_slot, its_j = place(slot, j, SCORE)
                    if has_pair(s - SCORE):
                        multiply(i - (SCORE - j + G - 1) // G, s - SCORE, its_slot, its_j)
                    if j == 4 and has_batch(i - 2) and (in_loop(i) or i >= 3):
                        find_drop(i - 2)
                    if has_pair(s - MESSAGE):
                        message(i - (MESSAGE - j + G - 1) // G, s - MESSAGE, *place(slot, j, MESSAGE))
                    if has_pair(s - SCORE):
                        score(i - (SCORE - j + G - 1) // G, s - SCORE, its_slot, its_j)
                    if j == 5 and has_batch(i - 2) and (in_loop(i) or i >= 3):
                        less_1(i - 2)
                    if has_pair(s - SUM):
                        add(i - (SUM - j + G - 1) // G, s - SUM, place(slot, j, SUM)[1])
            over_batches(dve, step, lag=3)


def after_attention(nc, t, d, layer):
    with ExitStack() as ctx:
        sem = sem_maker(nc, ctx, f"o{layer}")
        loads = [weights(nc, ctx, f"wo{layer}", d.L2_gnn_Wo[layer]), vector(nc, ctx, f"ln_g{layer}", d.L2_gnn_ln_g[layer]),
                 vector(nc, ctx, f"ln_b{layer}", d.L2_gnn_ln_b[layer])]
        wo, g, bb = (x[0] for x in loads)

        def sb(name, shape):
            return ctx.enter_context(nc.sbuf_tensor(f"{name}{layer}", shape, F32))

        total = sb("total", [P, 2, H])
        share = sb("share", [P, 2, H])
        loaded = sem("loaded")
        total_ready = sem("total_ready")
        share_ready = sem("share_ready")
        mean_ready = sem("mean_ready")
        turned = sem("turned")
        turned_copied = sem("turned_copied")
        product_done = sem("product_done")
        norm = norm_sems(sem)
        scaled = sem("scaled")
        finished = sem("finished")
        block = ctx.enter_context(nc.Block())

        @block.vector
        def _(dve):
            dve.wait_ge(loaded, 48)

            def step(b, par):
                if started(b):
                    acc = t.acc[:, bass.ds(b * W, W)].rearrange("p (h e) -> p h e", h=H)
                    two_back(dve, share_ready, b)
                    dve.tensor_scalar(total[:, par, :], acc[:, :, DK], 1e-9, None, ALU.add).then_inc(total_ready, 1)
                    dve.wait_ge(total_ready, b + 1)
                    two_back(dve, mean_ready, b)
                    dve.reciprocal(share[:, par, :], total[:, par, :]).then_inc(share_ready, 1)
                    dve.wait_ge(share_ready, b + 1)
                    two_back(dve, turned, b)
                    dve.tensor_tensor(t.work[:, par, 0:D].rearrange("p (h e) -> p h e", h=H), acc[:, :, 0:DK],
                                      share[:, par, :].unsqueeze(2).to_broadcast([P, H, DK]), ALU.mult
                                      ).then_inc(mean_ready, 1)
                if started(b, 1):
                    o, q = b - 1, 1 - par
                    dve.wait_ge(product_done, o + 1)
                    two_back(dve, norm.normed, o)
                    dve.tensor_tensor(t.s2[:, q, :], t.ps[2 + q][:, 0:D], t.x[:, bass.ds(o * D, D)], ALU.add
                                      ).then_inc(norm.summed, 1)
                    norm_moments(dve, t, norm, o, q)
                if started(b, 2):
                    o = b - 2
                    two_back(dve, scaled, o)
                    norm_apply(dve, t, norm, o, par, t.s1[:, par, :])
                    dve.wait_ge(norm.normed, o + 1)
                    two_back(dve, finished, o)
                    dve.tensor_tensor(t.work[:, par, D:2 * D], t.s1[:, par, :], g[:, :], ALU.mult).then_inc(scaled, 1)
                    dve.wait_ge(scaled, o + 1)
                    dve.tensor_tensor(t.x[:, bass.ds(o * D, D)], t.work[:, par, D:2 * D], bb[:, :], ALU.add
                                      ).then_inc(finished, 1)
            over_bins(dve, step, lag=2)
            dve.memset(t.acc[:, :], 0.0)

        @block.tensor
        def _(pe):
            pe.wait_ge(loaded, 48)

            def step(b, par):
                if started(b):
                    pe.wait_ge(mean_ready, b + 1)
                    two_back(pe, turned_copied, b)
                    turn(pe, t, t.work[:, par, :], par, turned)
                if started(b, 1):
                    o, q = b - 1, 1 - par
                    pe.wait_ge(turned_copied, o + 1)
                    two_back(pe, norm.summed, o)
                    for c in range(2):
                        mm = pe.matmul(t.ps[2 + q][:, 0:D], t.turned[:, q, c * P:(c + 1) * P], wo[:, c, :],
                                       start=c == 0, stop=c == 1)
                    mm.then_inc(product_done, 1)
            over_bins(pe, step, lag=1)

        @block.scalar
        def _(act):
            def step(b, par):
                if started(b):
                    act.wait_ge(turned, b + 1)
                    two_back(act, product_done, b)
                    act.copy(t.turned[:, par, 0:D], t.ps[par][:, 0:D]).then_inc(turned_copied, 1)
                if started(b, 1):
                    norm_std(act, t, norm, b - 1, 1 - par)
            over_bins(act, step, lag=1)

        @block.sync
        def _(sp):
            load(sp, loads, loaded)


def mlp(nc, t, d):
    HC = HID // P
    with ExitStack() as ctx:
        sem = sem_maker(nc, ctx, "mlp")
        loads = [weights(nc, ctx, "mlp_w1", d.L2_gnn_w1), weights(nc, ctx, "mlp_w2", d.L2_gnn_w2),
                 vector(nc, ctx, "mlp_b2", d.L2_gnn_b2)]
        w1, w2, b2 = (x[0] for x in loads)
        b1 = ctx.enter_context(nc.sbuf_tensor("mlp_b1", [P, HC], F32))
        hidden = ctx.enter_context(nc.sbuf_tensor("hidden", [P, 2, HC, P], F32))
        before = ctx.enter_context(nc.sbuf_tensor("x_before", [P, 2, D], F32))
        loaded = sem("loaded")
        before_loaded = [sem(f"before_loaded{p}") for p in range(2)]
        input_ready = sem("input_ready")
        turned = sem("turned")
        turned_copied = sem("turned_copied")
        hidden_done = sem("hidden_done")
        hidden_ready = sem("hidden_ready")
        product_done = sem("product_done")
        biased = sem("biased")
        norm = norm_sems(sem)
        block = ctx.enter_context(nc.Block())

        @block.vector
        def _(dve):
            dve.wait_ge(loaded, 64)

            def step(b, par):
                if started(b):
                    two_back(dve, turned, b)
                    dve.tensor_scalar(t.work[:, par, 0:D], t.x[:, bass.ds(b * D, D)], 1.0, None,
                                      ALU.mult).then_inc(input_ready, 1)
                if started(b, 2):
                    o = b - 2
                    dve.wait_ge(product_done, o + 1)
                    two_back(dve, norm.summed, o)
                    dve.tensor_tensor(t.s1[:, par, :], t.ps[6 + par][:, 0:D], b2[:, :], ALU.add).then_inc(biased, 1)
                    dve.wait_ge(biased, o + 1)
                    dve.wait_ge(before_loaded[par], (o - par) * 8 + 16)
                    two_back(dve, norm.normed, o)
                    dve.tensor_tensor(t.s2[:, par, :], t.s1[:, par, :], before[:, par, :], ALU.add
                                      ).then_inc(norm.summed, 1)
                    norm_moments(dve, t, norm, o, par)
                if started(b, 3):
                    norm_apply(dve, t, norm, b - 3, 1 - par, t.x[:, bass.ds((b - 3) * D, D)])
            over_bins(dve, step, lag=3)

        @block.tensor
        def _(pe):
            pe.wait_ge(loaded, 64)

            def step(b, par):
                if started(b):
                    pe.wait_ge(input_ready, b + 1)
                    two_back(pe, turned_copied, b)
                    turn(pe, t, t.work[:, par, :], par, turned)
                if started(b, 1):
                    o, q = b - 1, 1 - par
                    pe.wait_ge(turned_copied, o + 1)
                    two_back(pe, hidden_ready, o)
                    for j in range(HC):
                        for c in range(2):
                            mm = pe.matmul(t.ps[2 + 2 * q + j // 4][:, (j % 4) * P:(j % 4 + 1) * P],
                                           w1[:, c, j * P:(j + 1) * P], t.turned[:, q, c * P:(c + 1) * P],
                                           start=c == 0, stop=c == 1)
                    mm.then_inc(hidden_done, 1)
                if started(b, 2):
                    o = b - 2
                    pe.wait_ge(hidden_ready, o + 1)
                    two_back(pe, biased, o)
                    for j in range(HC):
                        mm = pe.matmul(t.ps[6 + par][:, 0:D], hidden[:, par, j, :], w2[:, j, :],
                                       start=j == 0, stop=j == HC - 1)
                    mm.then_inc(product_done, 1)
            over_bins(pe, step, lag=2)

        @block.scalar
        def _(act):
            act.wait_ge(loaded, 64)

            def step(b, par):
                if started(b):
                    act.wait_ge(turned, b + 1)
                    two_back(act, hidden_done, b)
                    act.copy(t.turned[:, par, 0:D], t.ps[par][:, 0:D]).then_inc(turned_copied, 1)
                if started(b, 1):
                    o, q = b - 1, 1 - par
                    act.wait_ge(hidden_done, o + 1)
                    two_back(act, product_done, o)
                    for j in range(HC):
                        ins = act.activation(hidden[:, q, j, :], t.ps[2 + 2 * q + j // 4][:, (j % 4) * P:(j % 4 + 1) * P],
                                             ACT.Relu, bias=b1[:, j:j + 1])
                    ins.then_inc(hidden_ready, 1)
                if started(b, 2):
                    norm_std(act, t, norm, b - 2, par)
            over_bins(act, step, lag=2)

        @block.sync
        def _(sp):
            load(sp, loads, loaded)
            sp.dma_start(b1[:, :], d.b1T).then_inc(loaded, 16)

            def step(b, par):
                two_back(sp, norm.summed, b)
                sp.dma_start(before[:, par, :], d.x2[bass.ds(b * P, P), :]).then_inc(before_loaded[par], 16)
            over_bins(sp, step)


def project3(nc, t, d):
    with ExitStack() as ctx:
        sem = sem_maker(nc, ctx, "p3")
        loads = [weights(nc, ctx, "w1", d.w1T), vector(nc, ctx, "w1_b", d.L3_gnn_w1_b)]
        w1, b1 = (x[0] for x in loads)
        is_twin = ctx.enter_context(nc.sbuf_tensor("is_twin", [P, K], F32))
        detour = ctx.enter_context(nc.sbuf_tensor("detour", [P, K], F32))
        loaded = sem("loaded")
        input_ready = sem("input_ready")
        turned = sem("turned")
        turned_copied = sem("turned_copied")
        product_done = sem("product_done")
        kept = sem("kept")
        stored = sem("stored")
        chain = sem("target_chain")
        block = ctx.enter_context(nc.Block())

        @block.vector
        def _(dve):
            dve.wait_ge(loaded, 32)
            dve.tensor_scalar(is_twin[:, :], t.twins[:, :], 1.0, None, ALU.min)
            dve.tensor_scalar(detour[:, :], t.src_at[:, :], -1.0, t.spare[:, :], ALU.mult, ALU.add).then_inc(chain, 1)
            dve.wait_ge(chain, 1)
            dve.tensor_tensor(detour[:, :], detour[:, :], is_twin[:, :], ALU.mult).then_inc(chain, 1)
            dve.wait_ge(chain, 2)
            dve.tensor_tensor(t.target_i[:, :], detour[:, :], t.src_at[:, :], ALU.add)

            def step(b, par):
                if started(b):
                    two_back(dve, turned, b)
                    dve.tensor_scalar(t.work[:, par, 0:D], t.x[:, bass.ds(b * D, D)], 1.0, None,
                                      ALU.mult).then_inc(input_ready, 1)
                if started(b, 1):
                    o, q = b - 1, 1 - par
                    dve.wait_ge(product_done, o + 1)
                    dve.tensor_tensor(t.z[:, bass.ds(o * SUP, SUP)], t.ps[2 + q][:, 0:SUP], b1[:, :], ALU.add
                                      ).then_inc(kept, 1)
            over_bins(dve, step, lag=1)

        @block.tensor
        def _(pe):
            pe.wait_ge(loaded, 32)

            def step(b, par):
                if started(b):
                    pe.wait_ge(input_ready, b + 1)
                    two_back(pe, turned_copied, b)
                    turn(pe, t, t.work[:, par, :], par, turned)
                if started(b, 1):
                    o, q = b - 1, 1 - par
                    pe.wait_ge(turned_copied, o + 1)
                    two_back(pe, kept, o)
                    for c in range(2):
                        mm = pe.matmul(t.ps[2 + q][:, 0:SUP], t.turned[:, q, c * P:(c + 1) * P], w1[:, c, :],
                                       start=c == 0, stop=c == 1)
                    mm.then_inc(product_done, 1)
            over_bins(pe, step, lag=1)

        @block.scalar
        def _(act):
            def step(b, par):
                act.wait_ge(turned, b + 1)
                two_back(act, product_done, b)
                act.copy(t.turned[:, par, 0:D], t.ps[par][:, 0:D]).then_inc(turned_copied, 1)
            over_bins(act, step)

        @block.sync
        def _(sp):
            load(sp, loads, loaded)
            store_bins(sp, t, t.z, SUP, SUP, d.z, kept, stored)


def neighbour_sums(nc, t, d):
    LAG = 2 * G + G // 2
    BUFFERS = 2 * G
    assert LAG % COPIES == BUFFERS % COPIES == 0 and SLOTS * G % BUFFERS == 0
    with ExitStack() as ctx:
        sem = sem_maker(nc, ctx, "a3")

        def sb(name, shape):
            return ctx.enter_context(nc.sbuf_tensor(name, shape, F32))

        onehot_t = sb("node_edge", [P, 2, P])
        same = sb("same_source", [P, 2, P])
        ends = sb("z_at_destination", [P, 2, SUP])
        outgoing = sb("outgoing", [P, BUFFERS, SUP])
        column = sb("source_column", [P, 2, G])
        target = ctx.enter_context(nc.sbuf_tensor("target_now", [P, SLOTS, G], I32))
        index_copied = sem("index_copied")
        index_taken = sem("index_taken")
        gathered = [sem(f"gathered{s}") for s in range(SLOTS)]
        sent = [sem(f"sent{r}") for r in range(COPIES)]
        column_ready = sem("column_ready")
        onehot_ready = sem("onehot_ready")
        turned = sem("turned")
        turned_copied = sem("turned_copied")
        row_ready = sem("row_ready")
        same_ready = sem("same_ready")
        ends_done = sem("ends_done")
        ends_copied = sem("ends_copied")
        merged = sem("merged")
        outgoing_ready = sem("outgoing_ready")
        part_done = sem("part_done")
        added = sem("added")
        block = ctx.enter_context(nc.Block())

        def in_loop(i):
            return not isinstance(i, int)

        def has_pair(k):
            return in_loop(k) or 0 <= k < K

        def batch_of(i, j, lag):
            return i + (j - lag) // G

        @block.gpsimd
        def _(pool):
            def step(i, slot):
                if in_loop(i) or i < NBATCH:
                    if in_loop(i) or i >= SLOTS:
                        pool.wait_ge(part_done, (i - SLOTS + 1) * G)
                    pool.tensor_copy(t.index[:, slot, :], t.src_i[:, bass.ds(i * G, G)])
                    if in_loop(i) or i >= SLOTS:
                        for r in range(COPIES):
                            pool.wait_ge(sent[r], (i - SLOTS + 1) * (16 * G // COPIES))
                        pool.sem_inc(index_taken, 1)
                    pool.tensor_copy(target[:, slot, :], t.target_i[:, bass.ds(i * G, G)]).then_inc(index_copied, 1)
                    pool.wait_ge(index_copied, i + 1)
                    pool.sem_inc(index_taken, 1)
                for j in range(G):
                    if in_loop(i) or i < NBATCH:
                        pool.indirect_dma_start(t.rows[:, slot, j, 0:SUP], None, d.z,
                                                bass.IndirectOffsetOnAxis(t.index[:, slot, j:j + 1], 0)
                                                ).then_inc(gathered[slot], 16)
                    k = i * G + j - LAG
                    if has_pair(k):
                        r = j % COPIES
                        pool.wait_ge(outgoing_ready, k + 1)
                        pool.sem_inc(index_taken, 1)
                        if in_loop(k) or k >= COPIES:
                            pool.wait_ge(sent[r], i * (16 * G // COPIES) + 16 * ((j - LAG - r) // COPIES))
                            pool.sem_inc(index_taken, 1)
                        pool.indirect_dma_start(d.reversed[r], bass.IndirectOffsetOnAxis(
                            target[:, (slot * G + j - LAG) // G % SLOTS, (j - LAG) % G:(j - LAG) % G + 1], 0),
                            outgoing[:, (slot * G + j - LAG) % BUFFERS, :], None, compute_op=ALU.add).then_inc(sent[r], 16)
            over_batches(pool, step, lag=3)
            for r in range(COPIES):
                pool.wait_ge(sent[r], 16 * K // COPIES)

        @block.tensor
        def _(pe):
            def turn_both(i, k, slot, j):
                pe.wait_ge(onehot_ready, k + 1)
                two_back(pe, ends_copied, k)
                pe.transpose(t.ps[2 + j % 2][:, 0:P], t.onehot[:, j % 4, :], t.ident[:, :]).then_inc(turned, 1)
                pe.wait_ge(column_ready, i + 1)
                two_back(pe, same_ready, k)
                pe.matmul(t.ps[4 + j % 2][:, 0:P], column[:, slot % 2, j:j + 1].to_broadcast([P, P]),
                          t.ident[:, :], start=True, stop=True).then_inc(row_ready, 1)

            def take_ends(k, j):
                b = pe.value_load(t.bins[0:1, bass.ds(k, 1)], min_val=0, max_val=NB - 1)
                pe.wait_ge(turned_copied, k + 1)
                pe.matmul(t.ps[2 + j % 2][:, P:P + SUP], onehot_t[:, j % 2, :], t.z[:, bass.ds(b * SUP, SUP)],
                          start=True, stop=True).then_inc(ends_done, 1)

            def merge(k, j):
                pe.wait_ge(ends_copied, k + 1)
                pe.wait_ge(same_ready, k + 1)
                two_back(pe, outgoing_ready, k)
                pe.matmul(t.ps[6 + j % 2][:, 0:SUP], same[:, j % 2, :], ends[:, j % 2, :],
                          start=True, stop=True).then_inc(merged, 1)

            def part(k, slot, j):
                two_back(pe, added, k)
                pe.matmul(t.ps[j % 2][:, 0:SUP], t.onehot[:, j % 4, :], t.rows[:, slot, j, 0:SUP],
                          start=True, stop=True).then_inc(part_done, 1)

            def step(i, slot):
                for j in range(G):
                    s = i * G + j
                    before, its_slot = batch_of(i, j, 1), (slot * G + j - 1) // G % SLOTS
                    if has_pair(s - 1):
                        turn_both(before, s - 1, its_slot, (j - 1) % G)
                        if j == 1:
                            pe.wait_ge(gathered[slot], (i - slot) * (16 * G // SLOTS) + 16 * G)
                        part(s - 1, its_slot, (j - 1) % G)
                    if has_pair(s - 2):
                        take_ends(s - 2, (j - 2) % G)
                    if has_pair(s - 3):
                        merge(s - 3, (j - 3) % G)
            over_batches(pe, step, lag=1)

        @block.scalar
        def _(act):
            def step(i, slot):
                for j in range(G):
                    k = i * G + j - 1
                    if has_pair(k):
                        act.wait_ge(turned, k + 1)
                        two_back(act, ends_done, k)
                        act.copy(onehot_t[:, (j - 1) % 2, :], t.ps[2 + (j - 1) % 2][:, 0:P]).then_inc(turned_copied, 1)
                    k = i * G + j - 2
                    if has_pair(k):
                        act.wait_ge(ends_done, k + 1)
                        two_back(act, merged, k)
                        act.copy(ends[:, j % 2, :], t.ps[2 + j % 2][:, P:P + SUP]).then_inc(ends_copied, 1)
                    k = i * G + j - 3
                    if has_pair(k):
                        act.wait_ge(merged, k + 1)
                        r = (j - 3) % COPIES
                        if in_loop(k) or k >= BUFFERS:
                            act.wait_ge(sent[r], (k - BUFFERS - r) * (16 // COPIES) + 16)
                        act.copy(outgoing[:, (slot * G + j - 3) % BUFFERS, :], t.ps[6 + (j - 3) % 2][:, 0:SUP]
                                 ).then_inc(outgoing_ready, 1)
            over_batches(act, step, lag=1)

        @block.vector
        def _(dve):
            def add(k, j):
                b = dve.value_load(t.bins[0:1, bass.ds(k, 1)], min_val=0, max_val=NB - 1)
                dve.wait_ge(part_done, k + 1)
                acc = t.acc[:, bass.ds(b * W, SUP)]
                if in_loop(k) or k >= 1:
                    dve.wait_ge(added, k)
                dve.tensor_tensor(acc, t.ps[j % 2][:, 0:SUP], acc, ALU.add).then_inc(added, 1)

            def step(i, slot):
                if has_pair(i * G):
                    if in_loop(i) or i >= 2:
                        dve.wait_ge(same_ready, (i - 1) * G)
                    dve.tensor_copy(column[:, slot % 2, :], t.src_at[:, bass.ds(i * G, G)]).then_inc(column_ready, 1)
                for j in range(G):
                    k = i * G + j
                    if has_pair(k):
                        if in_loop(k) or k >= 4:
                            dve.wait_ge(part_done, k - 3)
                            dve.wait_ge(turned, k - 3)
                        dve.tensor_scalar(t.onehot[:, j % 4, :], t.node[:, :], t.dst_at[:, bass.ds(k, 1)], None,
                                          ALU.is_equal).then_inc(onehot_ready, 1)
                    k = i * G + j - 2
                    if has_pair(k):
                        its_slot, its_j = (slot * G + j - 2) // G % SLOTS, (j - 2) % G
                        if its_j == 0:
                            dve.wait_ge(column_ready, batch_of(i, j, 2) + 1)
                        dve.wait_ge(row_ready, k + 1)
                        two_back(dve, merged, k)
                        dve.tensor_scalar(same[:, j % 2, :], t.ps[4 + j % 2][:, 0:P],
                                          column[:, its_slot % 2, its_j:its_j + 1], None,
                                          ALU.is_equal).then_inc(same_ready, 1)
                        add(k, its_j)
            over_batches(dve, step, lag=1)


def dense3(nc, t, d):
    with ExitStack() as ctx:
        sem = sem_maker(nc, ctx, "d3")
        loads = [weights(nc, ctx, "w0", d.w0T), vector(nc, ctx, "w0_b", d.L3_gnn_w0_b)]
        w0, b0 = (x[0] for x in loads)
        back = ctx.enter_context(nc.sbuf_tensor("back", [P, 2, COPIES, SUP], F32))
        loaded = sem("loaded")
        back_loaded = [sem(f"back_loaded{p}") for p in range(2)]
        input_ready = sem("input_ready")
        turned = sem("turned")
        turned_copied = sem("turned_copied")
        product_done = sem("product_done")
        gathered = sem("sums_added")
        biased = sem("biased")
        joined = sem("joined")
        norm = norm_sems(sem)
        stored = sem("stored")
        block = ctx.enter_context(nc.Block())

        @block.vector
        def _(dve):
            dve.wait_ge(loaded, 32)

            def step(b, par):
                if started(b):
                    two_back(dve, turned, b)
                    dve.tensor_scalar(t.work[:, par, 0:D], t.x[:, bass.ds(b * D, D)], 1.0, None,
                                      ALU.mult).then_inc(input_ready, 1)
                    acc = t.acc[:, bass.ds(b * W, SUP)]
                    dve.wait_ge(back_loaded[par], (b - par) * (16 * COPIES // 2) + 16 * COPIES)
                    for r in range(COPIES):
                        dve.tensor_tensor(acc, acc, back[:, par, r, :], ALU.add).then_inc(gathered, 1)
                        dve.wait_ge(gathered, b * COPIES + r + 1)
                if started(b, 1):
                    o, q = b - 1, 1 - par
                    dve.wait_ge(product_done, o + 1)
                    two_back(dve, norm.summed, o)
                    dve.tensor_tensor(t.s1[:, q, :], t.ps[2 + q][:, 0:D], b0[:, :], ALU.add).then_inc(biased, 1)
                    dve.wait_ge(biased, o + 1)
                    dve.tensor_tensor(t.s1[:, q, 0:SUP], t.s1[:, q, 0:SUP], t.acc[:, bass.ds(o * W, SUP)],
                                      ALU.add).then_inc(joined, 1)
                    dve.wait_ge(joined, o + 1)
                    two_back(dve, norm.normed, o)
                    dve.tensor_tensor(t.s2[:, q, :], t.s1[:, q, :], t.x[:, bass.ds(o * D, D)], ALU.add
                                      ).then_inc(norm.summed, 1)
                    norm_moments(dve, t, norm, o, q)
                if started(b, 2):
                    norm_apply(dve, t, norm, b - 2, par, t.x[:, bass.ds((b - 2) * D, D)])
            over_bins(dve, step, lag=2)

        @block.tensor
        def _(pe):
            pe.wait_ge(loaded, 32)

            def step(b, par):
                if started(b):
                    pe.wait_ge(input_ready, b + 1)
                    two_back(pe, turned_copied, b)
                    turn(pe, t, t.work[:, par, :], par, turned)
                if started(b, 1):
                    o, q = b - 1, 1 - par
                    pe.wait_ge(turned_copied, o + 1)
                    two_back(pe, biased, o)
                    for c in range(2):
                        mm = pe.matmul(t.ps[2 + q][:, 0:D], t.turned[:, q, c * P:(c + 1) * P], w0[:, c, :],
                                       start=c == 0, stop=c == 1)
                    mm.then_inc(product_done, 1)
            over_bins(pe, step, lag=1)

        @block.scalar
        def _(act):
            def step(b, par):
                if started(b):
                    act.wait_ge(turned, b + 1)
                    two_back(act, product_done, b)
                    act.copy(t.turned[:, par, 0:D], t.ps[par][:, 0:D]).then_inc(turned_copied, 1)
                if started(b, 1):
                    norm_std(act, t, norm, b - 1, 1 - par)
            over_bins(act, step, lag=1)

        @block.sync
        def _(sp):
            load(sp, loads, loaded)

            def step(b, par):
                if started(b):
                    if not isinstance(b, int) or b >= 2:
                        sp.wait_ge(gathered, (b - 1) * COPIES)
                    for r in range(COPIES):
                        sp.dma_start(back[:, par, r, :], d.reversed[r][bass.ds(b * P, P), :]
                                     ).then_inc(back_loaded[par], 16)
                if started(b, 2):
                    o = b - 2
                    sp.wait_ge(norm.normed, o + 1)
                    rows = LAST if isinstance(b, int) and o == NB - 1 else P
                    sp.dma_start(d.out[bass.ds(o * P, rows), :], t.x[0:rows, bass.ds(o * D, D)]).then_inc(stored, 16)
            over_bins(sp, step, lag=2)
            sp.wait_ge(stored, 16 * NB)


def program(nc, d):
    with ExitStack() as ctx:
        t = Named()

        t.ps = [ctx.enter_context(nc.psum_tensor(f"bank{i}", [P, 512], F32)) for i in range(8)]

        def sb(name, shape, dt=F32):
            return ctx.enter_context(nc.sbuf_tensor(name, shape, dt))

        t.x = sb("x", [P, NB * D])
        t.acc = sb("acc", [P, NB * W])
        t.rows = sb("rows", [P, SLOTS, G, KV])
        t.onehot = sb("onehot", [P, 4, P])
        t.ident = sb("ident", [P, P])
        t.lower = sb("lower", [P, P])
        t.node = sb("node", [P, P])
        t.real = sb("real", [P, 2, P])
        t.eps = sb("eps", [P, 1])
        t.spare = sb("spare", [P, 1])
        t.dst_at = sb("dst_at", [P, K])
        t.src_at = sb("src_at", [P, K])
        t.src_i = sb("src_idx", [P, K], I32)
        t.bins = sb("bins", [1, K], I32)
        t.index = sb("index", [P, SLOTS, G], I32)
        t.degree = sb("degree", [P, 2, 1])
        t.inv_deg = sb("inv_deg", [P, NB])
        t.work = sb("work", [P, 2, 2 * D])
        t.turned = sb("turned", [P, 2, 2 * D])
        t.squares = sb("squares", [P, 2, 1])
        t.column = sb("column", [P, 2, G])
        t.twin_count = sb("twin_count", [P, 2, G])
        t.twins = sb("twins", [P, K])
        t.s1 = sb("s1", [P, 2, D])
        t.s2 = sb("s2", [P, 2, D])
        t.stats = sb("stats", [P, 2, 6])
        t.mv = sb("mv", [P, 2, 2])
        t.std = sb("std", [P, 2, 1])
        t.rstd = sb("rstd", [P, 2, 1])

        with ExitStack() as edges:
            t.dst_i, t.prev_i, t.src_now = (edges.enter_context(nc.sbuf_tensor(name, [P, CH, P], I32))
                                            for name in ("dst_now", "dst_before", "src_now"))
            t.ones = edges.enter_context(nc.sbuf_tensor("ones", [P, P], F32))
            t.unsorted = edges.enter_context(nc.sbuf_tensor("unsorted", [1, 1], I32))
            load_edges(nc, t, d)
            sort_edges(nc, t, d)
            build_tables(nc, t, d)
        aggregate(nc, t, d, "a0", d.x, D, 1)
        dense0(nc, t, d)
        aggregate(nc, t, d, "a1", d.x1, D, 0, find_twins=True)
        dense1(nc, t, d)
        with nc.sbuf_tensor("queries", [P, NB * D], F32) as t.q:
            for layer in range(2):
                project(nc, t, d, layer)
                attend(nc, t, d, layer)
                after_attention(nc, t, d, layer)
        mlp(nc, t, d)
        with nc.sbuf_tensor("supports", [P, NB * SUP], F32) as t.z, nc.sbuf_tensor("target", [P, K], I32) as t.target_i:
            project3(nc, t, d)
            neighbour_sums(nc, t, d)
        dense3(nc, t, d)


def kernel(**inputs):
    import numpy as np
    import concourse.bacc as bacc
    from concourse.bass_utils import run_bass_kernel_spmd as run

    nc = bacc.Bacc("TRN2", target_bir_lowering=False, num_devices=1)
    v = {name: np.asarray(a) for name, a in inputs.items()}
    arrays = {name: a for name, a in v.items()
              if name != "L2_gnn_b1" and (name.startswith("L2") or a.ndim == 1 and name[0] == "L")}
    arrays["x"] = np.concatenate([v["x"], np.zeros((NP - N, D), v["x"].dtype)])
    arrays["src"] = np.concatenate([v["src"], np.full(EC - E, NP - 1, v["src"].dtype)])
    arrays["dst"] = np.concatenate([np.full(1, -1, v["dst"].dtype), v["dst"], np.full(EC - E, NP - 1, v["dst"].dtype)])
    for name, w in (("W0T", "L0_gnn_W"), ("WlT", "L1_gnn_W_l"), ("WrT", "L1_gnn_W_r"), ("w0T", "L3_gnn_w0_w"),
                    ("w1T", "L3_gnn_w1_w")):
        arrays[name] = np.ascontiguousarray(v[w].T)
    arrays["b1T"] = np.ascontiguousarray(v["L2_gnn_b1"].reshape(-1, P).T)
    d = Named()

    def given(name):
        a = arrays[name]
        return nc.dram_tensor(f"in_{name}", a.shape, mybir.dt.from_np(a.dtype), kind="ExternalInput").ap()

    d.x, d.src, d.dst = given("x"), given("src"), given("dst")
    d.W0T, d.L0_gnn_b = given("W0T"), given("L0_gnn_b")
    d.WlT, d.WrT, d.L1_gnn_b_l = given("WlT"), given("WrT"), given("L1_gnn_b_l")
    d.L1_gnn_gamma, d.L1_gnn_beta = given("L1_gnn_gamma"), given("L1_gnn_beta")
    d.L2_gnn_Wq, d.L2_gnn_Wk, d.L2_gnn_Wv = given("L2_gnn_Wq"), given("L2_gnn_Wk"), given("L2_gnn_Wv")
    d.L2_gnn_Wo, d.L2_gnn_ln_g, d.L2_gnn_ln_b = given("L2_gnn_Wo"), given("L2_gnn_ln_g"), given("L2_gnn_ln_b")
    d.L2_gnn_w1, d.b1T, d.L2_gnn_w2, d.L2_gnn_b2 = given("L2_gnn_w1"), given("b1T"), given("L2_gnn_w2"), given("L2_gnn_b2")
    d.w0T, d.L3_gnn_w0_b, d.w1T, d.L3_gnn_w1_b = given("w0T"), given("L3_gnn_w0_b"), given("w1T"), given("L3_gnn_w1_b")

    def scratch(name, shape, dt=F32):
        return nc.dram_tensor(f"dram_{name}", shape, dt).ap()

    d.records = scratch("records", (1 + EC, 2), I32)
    d.keys = scratch("keys", (EC,))
    d.bias = scratch("segment_bias", (K * P,))
    d.reversed = [scratch(f"reversed{r}", (NP + P, SUP)) for r in range(COPIES)]
    d.x1 = scratch("x1", (NP, D))
    d.x2 = scratch("x2", (NP, D))
    d.kv = scratch("kv", (NP, KV))
    d.z = scratch("z", (NP, SUP))
    d.out = nc.dram_tensor("out", (N, D), F32, kind="ExternalOutput").ap()
    program(nc, d)
    got = run(nc, [{f"in_{name}": a for name, a in arrays.items()}], core_ids=[0])
    return got.results[0]["out"]
```

```python
from contextlib import ExitStack

import concourse.bass as bass
from concourse import mybir

F32 = mybir.dt.float32
I32 = mybir.dt.int32
ALU = mybir.AluOpType
ACT = mybir.ActivationFunctionType
AX_X = mybir.AxisListType.X

P = 128
N = 3125
E = 50000
D = 256
H, DK = 8, 32
HZ = DK + 1
W = H * HZ
KV = W + D
SCALE = DK ** -0.5
HID = 1024
SUP = 128
NB = -(-N // P)
NP = NB * P
NT = -(-E // P)
CH = -(-NT // P)
EC = CH * P * P
G = 8
SLOTS = 4
NBATCH = -(-(NT + NB - 1) // (G * SLOTS)) * SLOTS
K = NBATCH * G
LAST = N - (NB - 1) * P
BIG = 1e30
LN_EPS = 1e-5
COPIES = 4


class Named:
    pass


def over_batches(eng, step, lag=0):
    for i in range(SLOTS):
        step(i, i)
    with eng.Fori(1, NBATCH // SLOTS) as n:
        for slot in range(SLOTS):
            step(n * SLOTS + slot, slot)
    for i in range(NBATCH, NBATCH + lag):
        step(i, i % SLOTS)


def over_bins(eng, step, lag=0):
    for b in range(6):
        step(b, b % 2)
    with eng.Fori(3, (NB - 1) // 2) as n:
        for parity in range(2):
            step(n * 2 + parity, parity)
    for b in range((NB - 1) // 2 * 2, NB + lag):
        step(b, b % 2)


def sem_maker(nc, ctx, phase):
    made = []

    def sem(name):
        made.append(nc.alloc_semaphore(f"{phase}_{name}"))
        return made[-1]

    def clear():
        nc.clear_and_free_semaphores(made)
        nc.all_engine_barrier()

    ctx.callback(clear)
    return sem


def load_edges(nc, t, d):
    with ExitStack() as ctx:
        sem = sem_maker(nc, ctx, "le")
        falls = ctx.enter_context(nc.sbuf_tensor("falls", [P, CH, P], F32))
        fall_count = ctx.enter_context(nc.sbuf_tensor("fall_count", [P, 1], F32))
        loaded = sem("loaded")
        compared = sem("compared")
        counted = sem("counted")
        summed = sem("summed")
        ones_ready = sem("ones_ready")
        block = ctx.enter_context(nc.Block())

        @block.sync
        def _(sp):
            for tile, flat in ((t.dst_i, d.dst[1:1 + EC]), (t.prev_i, d.dst[0:EC]), (t.src_now, d.src)):
                sp.dma_start(tile[:, :, :], flat.rearrange("(c p e) -> p c e", c=CH, p=P)).then_inc(loaded, 16)
            sp.wait_ge(loaded, 48)

        @block.vector
        def _(dve):
            dve.memset(t.ones[:, :], 1.0).then_inc(ones_ready, 1)
            dve.wait_ge(loaded, 48)
            dve.tensor_tensor(falls[:, :, :], t.dst_i[:, :, :], t.prev_i[:, :, :], ALU.is_lt).then_inc(compared, 1)
            dve.wait_ge(compared, 1)
            dve.tensor_reduce(fall_count[:, :], falls[:, :, :], mybir.AxisListType.XY, ALU.add).then_inc(counted, 1)
            dve.wait_ge(summed, 1)
            dve.tensor_copy(t.unsorted[:, :], t.ps[0][0:1, 0:1])

        @block.tensor
        def _(pe):
            pe.wait_ge(ones_ready, 1)
            pe.wait_ge(counted, 1)
            pe.matmul(t.ps[0][:, 0:1], t.ones[:, :], fall_count[:, :], start=True, stop=True).then_inc(summed, 1)


def sort_edges(nc, t, d):
    CUT = 8
    PIECE = NT * P // CUT
    with ExitStack() as ctx:
        sem = sem_maker(nc, ctx, "sort")

        def sb(name, shape, dt=F32):
            return ctx.enter_context(nc.sbuf_tensor(name, shape, dt))

        records = sb("records", [P, CH, P, 2], I32)
        keys = sb("keys", [P, CH * P])
        rank = sb("rank", [P, CH * P])
        count = sb("count", [P, 1])
        tile_no = sb("key_tile_no", [P, CH])
        position = sb("position", [P, P])
        equal = sb("equal_keys", [P, P])
        lower = sb("equal_before", [P, P])
        head = sb("head", [1, 2], I32)
        place = sb("place", [P, 1], I32)
        record = sb("record", [P, 2], I32)
        flat = t.rows[:, :, :, :].rearrange("p a b c -> p (a b c)")
        piece = flat[:, 0:PIECE]
        smaller = flat[:, PIECE:2 * PIECE]

        numbered = sem("numbered")
        filled = sem("filled")
        keys_ready = sem("keys_ready")
        kept = sem("kept")
        piece_loaded = sem("piece_loaded")
        compared = sem("compared")
        ranked = sem("ranked")
        tied = sem("tied")
        staged = sem("staged")
        taken = sem("taken")
        sent = sem("sent")
        reloaded = sem("reloaded")
        split = sem("split")
        block = ctx.enter_context(nc.Block())

        @block.gpsimd
        def _(pool):
            f = dict(allow_small_or_imprecise_dtypes=True)
            pool.iota(tile_no[:, :], [[P, CH]], base=0, channel_multiplier=1, **f).then_inc(numbered, 1)
            pool.iota(position[:, :], [[1, P]], base=0, channel_multiplier=0, **f).then_inc(numbered, 1)
            unsorted = pool.value_load(t.unsorted[0:1, 0:1])
            with pool.If(unsorted > 0):
                pool.wait_ge(kept, 48)
                for c in range(CH):
                    tiles = min(P, NT - c * P)
                    with pool.Fori(0, P) as e:
                        pool.wait_ge(staged, (e + c * P) + 1)
                        pool.sem_inc(taken, 1)
                        pool.indirect_dma_start(d.records, bass.IndirectOffsetOnAxis(place[0:tiles, :], 0),
                                                record[0:tiles, :], None).then_inc(sent, 16)

        @block.sync
        def _(sp):
            unsorted = sp.value_load(t.unsorted[0:1, 0:1])
            with sp.If(unsorted > 0):
                sp.wait_ge(filled, 3)
                sp.dma_start(d.records[1:1 + EC, :].rearrange("(c p e) r -> p c (e r)", c=CH, p=P),
                             records[:, :, :, :].rearrange("p c e r -> p c (e r)")).then_inc(kept, 16)
                sp.dma_start(d.records[0:1, :], head[:, :]).then_inc(kept, 16)
                sp.wait_ge(keys_ready, 1)
                sp.dma_start(d.keys.rearrange("(c p e) -> p c e", c=CH, p=P),
                             keys[:, :].rearrange("p (c e) -> p c e", c=CH)).then_inc(kept, 16)
                sp.wait_ge(kept, 48)
                for q in range(CUT):
                    if q >= 1:
                        sp.wait_ge(compared, q * CH * P)
                    sp.dma_start(piece, d.keys[q * PIECE:(q + 1) * PIECE].partition_broadcast(P)
                                 ).then_inc(piece_loaded, 16)
                sp.wait_ge(sent, 16 * CH * P)
                for n, tile in enumerate((1, 0)):
                    if n:
                        sp.wait_ge(split, 2)
                    sp.dma_start(records[:, :, :, :].rearrange("p c e r -> p c (e r)"),
                                 d.records[tile:tile + EC, :].rearrange("(c p e) r -> p c (e r)", c=CH, p=P)
                                 ).then_inc(reloaded, 16)
                sp.wait_ge(reloaded, 32)

        @block.vector
        def _(dve):
            dve.wait_ge(numbered, 2)
            unsorted = dve.value_load(t.unsorted[0:1, 0:1])
            with dve.If(unsorted > 0):
                dve.tensor_copy(records[:, :, :, 0], t.dst_i[:, :, :]).then_inc(filled, 1)
                dve.tensor_copy(records[:, :, :, 1], t.src_now[:, :, :]).then_inc(filled, 1)
                dve.memset(head[:, :], -1).then_inc(filled, 1)
                dve.memset(rank[:, :], 1.0)
                for c in range(CH):
                    ins = dve.tensor_scalar(keys[:, c * P:(c + 1) * P], t.dst_i[:, c, :], float(CH * P),
                                            tile_no[:, c:c + 1], ALU.mult, ALU.add)
                ins.then_inc(keys_ready, 1)
                dve.wait_ge(keys_ready, 1)
                for q in range(CUT):
                    dve.wait_ge(piece_loaded, 16 * (q + 1))
                    with dve.Fori(0, CH * P) as e:
                        at = e + q * CH * P
                        dve.wait_ge(ranked, at)
                        dve.tensor_scalar(smaller, piece, keys[:, bass.ds(e, 1)], 0.0, ALU.is_lt, ALU.add,
                                          accum_out=count[:, :]).then_inc(compared, 1)
                        dve.wait_ge(compared, at + 1)
                        dve.tensor_tensor(rank[:, bass.ds(e, 1)], rank[:, bass.ds(e, 1)], count[:, :], ALU.add
                                          ).then_inc(ranked, 1)
                for c in range(CH):
                    with dve.Fori(0, P) as e:
                        at = e + c * P
                        dve.wait_ge(ranked, at + CUT * CH * P)
                        dve.tensor_scalar(equal[:, :], keys[:, c * P:(c + 1) * P], keys[:, bass.ds(at, 1)], None,
                                          ALU.is_equal).then_inc(tied, 1)
                        dve.wait_ge(tied, at * 2 + 1)
                        dve.scalar_tensor_tensor(out=lower[:, :], in0=position[:, :], scalar=position[:, bass.ds(e, 1)],
                                                 in1=equal[:, :], op0=ALU.is_lt, op1=ALU.mult,
                                                 accum_out=count[:, :]).then_inc(tied, 1)
                        dve.wait_ge(tied, at * 2 + 2)
                        dve.tensor_tensor(rank[:, bass.ds(at, 1)], rank[:, bass.ds(at, 1)], count[:, :], ALU.add
                                          ).then_inc(ranked, 1)
                dve.wait_ge(ranked, (CUT + 1) * CH * P)
                for c in range(CH):
                    with dve.Fori(0, P) as e:
                        at = e + c * P
                        dve.wait_ge(sent, at * 16)
                        dve.tensor_scalar(place[:, :], rank[:, bass.ds(at, 1)], 1.0, None, ALU.mult)
                        dve.tensor_scalar(record[:, 0:1], t.dst_i[:, c, bass.ds(e, 1)], 1.0, None, ALU.mult)
                        dve.tensor_scalar(record[:, 1:2], t.src_now[:, c, bass.ds(e, 1)], 1.0, None, ALU.mult
                                          ).then_inc(staged, 1)
                dve.wait_ge(reloaded, 16)
                dve.tensor_copy(t.dst_i[:, :, :], records[:, :, :, 0]).then_inc(split, 1)
                dve.tensor_copy(t.src_now[:, :, :], records[:, :, :, 1]).then_inc(split, 1)
                dve.wait_ge(reloaded, 32)
                dve.tensor_copy(t.prev_i[:, :, :], records[:, :, :, 0])


def build_tables(nc, t, d):
    with ExitStack() as ctx:
        sem = sem_maker(nc, ctx, "tab")

        def sb(name, shape, dt=F32):
            return ctx.enter_context(nc.sbuf_tensor(name, shape, dt))

        dst_f = sb("dst_f", [P, CH, P])
        src_f = sb("src_f", [P, CH, P])
        seg_start = sb("seg_start", [P, CH, P])
        ends_i = sb("ends_i", [P, 2, CH], I32)
        first = sb("first", [P, CH])
        last = sb("last", [P, CH])
        real_tile = sb("real_tile", [P, CH])
        pairs = sb("pairs", [P, CH])
        pairs_before = sb("pairs_before", [P, CH])
        begin = sb("begin", [P, CH])
        end = sb("end", [P, CH])
        shift = sb("shift", [P, CH])
        iota_k = sb("iota_k", [P, K])
        tile_no = sb("tile_no", [P, CH])
        upper = sb("upper", [P, P])
        at_or_after = sb("at_or_after", [P, CH, K])
        sel = sb("sel", [P, CH, K])
        bin_f = sb("bin_f", [P, K])
        no_pair = sb("no_pair", [P, K])
        base = sb("base", [P, K])
        bias_rows = sb("bias_rows", [P, CH, P])
        zeros = sb("zeros", [P, 2048])

        xloaded = sem("x_loaded")
        consts = sem("consts")
        chain = sem("vector_chain")
        pairs_ready = sem("pairs_ready")
        begin_ready = sem("begin_ready")
        sel_ready = sem("sel_ready")
        bins_done = sem("bins_done")
        tables_done = sem("tables_done")
        bias_done = sem("bias_done")
        bias_copied = sem("bias_copied")
        zeroed = sem("zeroed")
        stored = sem("stored")
        block = ctx.enter_context(nc.Block())

        @block.sync
        def _(sp):
            sp.dma_start(t.x[:, :].rearrange("p (b f) -> p b f", b=NB),
                         d.x.rearrange("(b p) f -> p b f", p=P)).then_inc(xloaded, 16)
            sp.wait_ge(zeroed, 1)
            for r in range(COPIES):
                for at in range(0, NP + P, 2048):
                    rows = min(2048, NP + P - at)
                    sp.dma_start(d.reversed[r][at:at + rows, :].rearrange("(p a) n -> p (a n)", p=P),
                                 zeros[:, 0:rows * SUP // P]).then_inc(stored, 16)
            sp.wait_ge(bias_copied, CH)
            for c in range(CH):
                n = min(P, K - c * P)
                sp.dma_start(d.bias[c * P * P:(c * P + n) * P].rearrange("(k e) -> k e", e=P),
                             bias_rows[0:n, c, :]).then_inc(stored, 16)
            sp.wait_ge(xloaded, 16)
            sp.wait_ge(stored, (COPIES * 2 + CH) * 16)

        @block.gpsimd
        def _(pool):
            f = dict(allow_small_or_imprecise_dtypes=True)
            pool.memset(t.ident[:, :], 0.0).then_inc(consts, 1)
            pool.iota(t.node[:, :], [[1, P]], base=0, channel_multiplier=0, **f).then_inc(consts, 1)
            pool.iota(iota_k[:, :], [[1, K]], base=0, channel_multiplier=0, **f).then_inc(consts, 1)
            pool.iota(tile_no[:, :], [[P, CH]], base=0, channel_multiplier=1, **f).then_inc(consts, 1)
            pool.iota(t.spare[:, :], [[0, 1]], base=NP, channel_multiplier=1, **f).then_inc(consts, 1)
            pool.wait_ge(consts, 5)
            pool.affine_select(out=t.ident[:, :], in_=t.ident[:, :], compare_op=ALU.not_equal, fill=1.0,
                               base=0, pattern=[[-1, P]], channel_multiplier=1).then_inc(consts, 1)
            pool.affine_select(out=upper[:, :], in_=t.ones[:, :], compare_op=ALU.is_gt, fill=0.0,
                               base=0, pattern=[[1, P]], channel_multiplier=-1).then_inc(consts, 1)
            pool.affine_select(out=t.lower[:, :], in_=t.ones[:, :], compare_op=ALU.is_gt, fill=0.0,
                               base=0, pattern=[[-1, P]], channel_multiplier=1).then_inc(consts, 1)
            pool.memset(t.real[:, 0, :], 1.0).then_inc(consts, 1)
            pool.affine_select(out=t.real[:, 1, :], in_=t.ones[:, :], compare_op=ALU.is_gt, fill=0.0,
                               base=LAST, pattern=[[0, P]], channel_multiplier=-1).then_inc(consts, 1)

        @block.vector
        def _(dve):
            n = [0]

            def done(ins):
                n[0] += 1
                ins.then_inc(chain, 1)
                dve.wait_ge(chain, n[0])

            dve.memset(zeros[:, :], 0.0).then_inc(zeroed, 1)
            dve.memset(t.eps[:, :], LN_EPS)
            for slot in range(SLOTS):
                for j in range(G):
                    dve.memset(t.rows[:, slot, j, D:D + 1], 1.0)
            dve.memset(t.acc[:, :], 0.0)
            dve.wait_ge(consts, 10)
            dve.tensor_copy(src_f[:, :, :], t.src_now[:, :, :])
            dve.tensor_copy(dst_f[:, :, :], t.dst_i[:, :, :])
            dve.tensor_tensor(seg_start[:, :, :], t.dst_i[:, :, :], t.prev_i[:, :, :], ALU.not_equal)
            dve.tensor_scalar(ends_i[:, 0, :], t.dst_i[:, :, 0], 7, None, ALU.arith_shift_right)
            done(dve.tensor_scalar(ends_i[:, 1, :], t.dst_i[:, :, P - 1], 7, None, ALU.arith_shift_right))
            dve.tensor_copy(first[:, :], ends_i[:, 0, :])
            dve.tensor_scalar(real_tile[:, :], tile_no[:, :], float(NT), None, ALU.is_lt)
            done(dve.tensor_scalar(last[:, :], ends_i[:, 1, :], 1.0, None, ALU.add))
            done(dve.tensor_tensor(pairs[:, :], last[:, :], first[:, :], ALU.subtract))
            done(dve.tensor_tensor(pairs[:, :], pairs[:, :], real_tile[:, :], ALU.mult))
            done(dve.memset(pairs_before[:, 0:1], 0.0))
            for c in range(1, CH):
                done(dve.tensor_tensor(pairs_before[:, c:c + 1], pairs_before[:, c - 1:c], pairs[:, c - 1:c], ALU.add))
            dve.tensor_copy(end[:, :], pairs[:, :]).then_inc(pairs_ready, 1)
            dve.wait_ge(begin_ready, 1)
            done(dve.tensor_copy(begin[:, :], t.ps[0][:, 0:CH]))
            dve.tensor_tensor(shift[:, :], first[:, :], begin[:, :], ALU.subtract)
            done(dve.tensor_tensor(end[:, :], begin[:, :], pairs[:, :], ALU.add))
            for c in range(CH):
                done(dve.tensor_scalar(at_or_after[:, c, :], iota_k[:, :], begin[:, c:c + 1], None, ALU.is_ge))
            for c in range(CH):
                dve.scalar_tensor_tensor(out=sel[:, c, :], in0=iota_k[:, :], scalar=end[:, c:c + 1],
                                         in1=at_or_after[:, c, :], op0=ALU.is_lt, op1=ALU.mult).then_inc(sel_ready, 1)
            dve.wait_ge(bins_done, 1)
            done(dve.tensor_tensor(base[:, :], t.ps[2][:, 0:K], iota_k[:, :], ALU.mult))
            done(dve.tensor_tensor(bin_f[:, :], t.ps[1][:, 0:K], base[:, :], ALU.add))
            dve.tensor_copy(t.bins[:, :], bin_f[0:1, :])
            dve.tensor_scalar(t.acc_at[:, :], bin_f[0:1, :], float(W), None, ALU.mult)
            dve.tensor_scalar(no_pair[:, :], t.ps[2][:, 0:K], -1.0, 1e6, ALU.add, ALU.mult)
            done(dve.tensor_scalar(base[:, :], bin_f[:, :], float(-P), None, ALU.mult))
            done(dve.tensor_tensor(base[:, :], base[:, :], no_pair[:, :], ALU.add))
            dve.wait_ge(tables_done, 1)
            dve.tensor_tensor(t.dst_at[:, :], t.ps[4][:, 0:K], base[:, :], ALU.add)
            dve.tensor_copy(t.src_i[:, :], t.ps[3][:, 0:K])
            dve.tensor_copy(t.src_at[:, :], t.ps[3][:, 0:K])
            for c in range(CH):
                m = min(P, K - c * P)
                dve.wait_ge(bias_done, c + 1)
                dve.tensor_scalar(bias_rows[0:m, c, :], t.ps[5 + c % 2][0:m, 0:P], -BIG, None,
                                  ALU.mult).then_inc(bias_copied, 1)

        @block.tensor
        def _(pe):
            pe.wait_ge(consts, 10)
            pe.wait_ge(pairs_ready, 1)
            pe.matmul(t.ps[0][:, 0:CH], upper[:, :], pairs[:, :], start=True, stop=False)
            pe.matmul(t.ps[0][:, 0:CH], t.ones[:, :], pairs_before[:, :], start=False, stop=True).then_inc(begin_ready, 1)
            pe.wait_ge(sel_ready, CH)
            for c in range(CH):
                pe.matmul(t.ps[1][:, 0:K], shift[:, c:c + 1].to_broadcast([P, P]), sel[:, c, :],
                          start=c == 0, stop=c == CH - 1)
            for c in range(CH):
                mm = pe.matmul(t.ps[2][:, 0:K], t.ones[:, :], sel[:, c, :], start=c == 0, stop=c == CH - 1)
            mm.then_inc(bins_done, 1)
            for out, table in ((t.ps[3], src_f), (t.ps[4], dst_f)):
                for c in range(CH):
                    mm = pe.matmul(out[:, 0:K], table[:, c, :], sel[:, c, :], start=c == 0, stop=c == CH - 1)
            mm.then_inc(tables_done, 1)
            for kc in range(CH):
                m = min(P, K - kc * P)
                if kc >= 2:
                    pe.wait_ge(bias_copied, kc - 1)
                for c in range(CH):
                    mm = pe.matmul(t.ps[5 + kc % 2][0:m, 0:P], sel[:, c, kc * P:kc * P + m], seg_start[:, c, :],
                                   start=c == 0, stop=c == CH - 1)
                mm.then_inc(bias_done, 1)


def aggregate(nc, t, d, phase, table, width, ones_column):
    cols = width + ones_column
    HG = G // 2
    with ExitStack() as ctx:
        sem = sem_maker(nc, ctx, phase)
        index_copied = sem("index_copied")
        index_taken = sem("index_taken")
        gathered = [sem(f"gathered{s}") for s in range(SLOTS)]
        onehot = ctx.enter_context(nc.sbuf_tensor(f"onehot_{phase}", [P, 2, HG, P], F32))
        onehot_free = sem("onehot_free")
        distance_ready = sem("distance_ready")
        onehot_ready = sem("onehot_ready")
        part_done = sem("part_done")
        added = sem("added")
        block = ctx.enter_context(nc.Block())

        @block.gpsimd
        def _(pool):
            def step(i, slot):
                if not isinstance(i, int) or i >= SLOTS:
                    pool.wait_ge(part_done, (i - SLOTS + 1) * G)
                pool.tensor_copy(t.index[:, slot, :], t.src_i[:, bass.ds(i * G, G)]).then_inc(index_copied, 1)
                pool.wait_ge(index_copied, i + 1)
                pool.sem_inc(index_taken, 1)
                for j in range(G):
                    pool.indirect_dma_start(t.rows[:, slot, j, 0:width], None, table,
                                            bass.IndirectOffsetOnAxis(t.index[:, slot, j:j + 1], 0)
                                            ).then_inc(gathered[slot], 16)
            over_batches(pool, step)

        @block.tensor
        def _(pe):
            def step(i, slot):
                pe.wait_ge(gathered[slot], (i - slot) * (16 * G // SLOTS) + 16 * G)
                for j in range(G):
                    k = i * G + j
                    if j % HG == 0:
                        pe.wait_ge(onehot_ready, 2 * i + j // HG + 1)
                    two_back(pe, added, k)
                    pe.matmul(t.ps[j % 2][:, 0:cols], onehot[:, j // HG, j % HG, :], t.rows[:, slot, j, 0:cols],
                              start=True, stop=True).then_inc(part_done, 1)
            over_batches(pe, step)

        @block.scalar
        def _(act):
            def step(i, slot):
                for half in range(2):
                    if not isinstance(i, int) or i >= 1:
                        act.wait_ge(part_done, (i - 1) * G + (half + 1) * HG)
                        act.sem_inc(onehot_free, 1)
                    for j in range(HG):
                        act.activation(onehot[:, half, j, :], t.node[:, :], ACT.Abs, scale=-1.0,
                                       bias=t.dst_at[:, bass.ds(i * G + half * HG + j, 1)]).then_inc(distance_ready, 1)
                    act.wait_ge(distance_ready, i * G + (half + 1) * HG)
                    four = onehot[:, half, :, :]
                    act.activation(four, four, ACT.Relu, scale=-1.0, bias=1.0).then_inc(onehot_ready, 1)
            over_batches(act, step)

        @block.vector
        def _(dve):
            def place(k):
                return dve.value_load(t.acc_at[0:1, bass.ds(k, 1)], min_val=0, max_val=(NB - 1) * W)

            def add(k, j, at):
                dve.wait_ge(part_done, k + 1)
                acc = t.acc[:, bass.ds(at, cols)]
                if not isinstance(k, int) or k >= 1:
                    dve.wait_ge(added, k)
                dve.tensor_tensor(acc, t.ps[j % 2][:, 0:cols], acc, ALU.add).then_inc(added, 1)

            def step(i, slot):
                for j in range(G):
                    k = i * G + j
                    if not isinstance(k, int) or k >= 2:
                        at = place(k - 2)
                        add(k - 2, j, at)
            over_batches(dve, step)
            add(K - 2, 0, place(K - 2))
            add(K - 1, 1, place(K - 1))


def weights(nc, ctx, name, dram):
    tile = ctx.enter_context(nc.sbuf_tensor(f"sb_{name}", [P, dram.shape[0] // P, dram.shape[1]], F32))
    return tile, tile[:, :, :], dram.rearrange("(c p) n -> p c n", p=P)


def vector(nc, ctx, name, dram):
    tile = ctx.enter_context(nc.sbuf_tensor(f"sb_{name}", [P, dram.shape[0]], F32))
    return tile, tile[:, :], dram.partition_broadcast(P)


def load(sp, loads, loaded):
    for _, tile, dram in loads:
        sp.dma_start(tile, dram).then_inc(loaded, 16)


def started(b, lag=0):
    return not isinstance(b, int) or 0 <= b - lag < NB


def two_back(eng, signal, b):
    if not isinstance(b, int) or b >= 2:
        eng.wait_ge(signal, b - 1)


def norm_sems(sem):
    norm = Named()
    norm.summed, norm.waited, norm.stats, norm.moments = sem("summed"), sem("waited"), sem("stats"), sem("moments")
    norm.std, norm.rstd, norm.normed = sem("std"), sem("rstd"), sem("normed")
    return norm


def norm_stats(dve, t, s, b, par):
    dve.wait_ge(s.summed, b + 1)
    dve.bn_stats(t.stats[:, par, :], t.s2[:, par, :]).then_inc(s.stats, 1)


def norm_moments(dve, t, s, b, par):
    dve.wait_ge(s.stats, b + 1)
    dve.sem_inc(s.waited, 1)
    dve.bn_aggr(t.mv[:, par, :], t.stats[:, par, :]).then_inc(s.moments, 1)


def norm_std(act, t, s, b, par):
    act.wait_ge(s.moments, b + 1)
    act.activation(t.std[:, par, :], t.mv[:, par, 1:2], ACT.Sqrt, bias=t.eps[:, :]).then_inc(s.std, 1)


def norm_rstd(dve, t, s, b, par):
    dve.wait_ge(s.std, b + 1)
    dve.reciprocal(t.rstd[:, par, :], t.std[:, par, :]).then_inc(s.rstd, 1)


def norm_apply(dve, t, s, b, par, out):
    dve.wait_ge(s.rstd, b + 1)
    dve.tensor_scalar(out, t.s2[:, par, :], t.mv[:, par, 0:1], t.rstd[:, par, :],
                      ALU.subtract, ALU.mult).then_inc(s.normed, 1)


def turn(pe, t, src, par, signal, blocks=2):
    for c in range(blocks):
        mm = pe.transpose(t.ps[par][:, c * P:(c + 1) * P], src[:, c * P:(c + 1) * P], t.ident[:, :])
    mm.then_inc(signal, 1)


def store_bins(sp, t, src, stride, width, dram, ready, stored):
    def step(b, par):
        sp.wait_ge(ready, b + 1)
        sp.dma_start(dram[bass.ds(b * P, P), :], src[:, bass.ds(b * stride, width)]).then_inc(stored, 16)
    over_bins(sp, step)
    sp.wait_ge(stored, 16 * NB)


def dense0(nc, t, d):
    with ExitStack() as ctx:
        sem = sem_maker(nc, ctx, "d0")
        loads = [weights(nc, ctx, "W0", d.W0T), vector(nc, ctx, "b0", d.L0_gnn_b)]
        W0, b0 = (x[0] for x in loads)
        loaded = sem("loaded")
        degree = sem("degree")
        inverse = sem("inverse")
        mean_ready = sem("mean_ready")
        turned = sem("turned")
        turned_copied = sem("turned_copied")
        product_done = sem("product_done")
        biased = sem("biased")
        norm = norm_sems(sem)
        stored = sem("stored")
        block = ctx.enter_context(nc.Block())

        @block.vector
        def _(dve):
            dve.wait_ge(loaded, 32)

            def step(b, par):
                o, q, a = b - 3, 1 - par, b - 4
                if started(b):
                    two_back(dve, turned, b)
                    dve.tensor_scalar(t.degree[:, par, :], t.acc[:, bass.ds(b * W + D, 1)], 1.0, None,
                                      ALU.max).then_inc(degree, 1)
                if started(o):
                    dve.wait_ge(product_done, o + 1)
                    dve.tensor_tensor(t.s1[:, q, :], t.ps[2 + q][:, 0:D], b0[:, :], ALU.add).then_inc(biased, 1)
                if started(b):
                    dve.wait_ge(degree, b + 1)
                    dve.reciprocal(t.inv_deg[:, bass.ds(b, 1)], t.degree[:, par, :]).then_inc(inverse, 1)
                if started(o):
                    dve.wait_ge(biased, o + 1)
                    dve.scalar_tensor_tensor(out=t.s2[:, q, :], in0=t.s1[:, q, :], scalar=0.0,
                                             in1=t.x[:, bass.ds(o * D, D)], op0=ALU.max, op1=ALU.add
                                             ).then_inc(norm.summed, 1)
                if started(b):
                    dve.wait_ge(inverse, b + 1)
                    dve.tensor_scalar(t.work[:, par, 0:D], t.acc[:, bass.ds(b * W, D)], t.inv_deg[:, bass.ds(b, 1)],
                                      None, ALU.mult).then_inc(mean_ready, 1)
                if started(a):
                    norm_rstd(dve, t, norm, a, par)
                if started(o):
                    norm_stats(dve, t, norm, o, q)
                if started(a):
                    norm_apply(dve, t, norm, a, par, t.x[:, bass.ds(a * D, D)])
                if started(o):
                    norm_moments(dve, t, norm, o, q)
            over_bins(dve, step, lag=4)

        @block.gpsimd
        def _(pool):
            pool.wait_ge(mean_ready, NB)
            pool.memset(t.acc[:, :], 0.0)

        @block.tensor
        def _(pe):
            pe.wait_ge(loaded, 32)

            def step(b, par):
                if started(b):
                    pe.wait_ge(mean_ready, b + 1)
                    two_back(pe, turned_copied, b)
                    turn(pe, t, t.work[:, par, :], par, turned)
                if started(b, 1):
                    o, q = b - 1, 1 - par
                    pe.wait_ge(turned_copied, o + 1)
                    if not isinstance(b, int) or o >= 2:
                        pe.wait_ge(biased, o - 1)
                    for c in range(2):
                        mm = pe.matmul(t.ps[2 + q][:, 0:D], t.turned[:, q, c * P:(c + 1) * P], W0[:, c, :],
                                       start=c == 0, stop=c == 1)
                    mm.then_inc(product_done, 1)
            over_bins(pe, step, lag=1)

        @block.scalar
        def _(act):
            def step(b, par):
                if started(b, 4):
                    norm_std(act, t, norm, b - 4, par)
                if started(b):
                    act.wait_ge(turned, b + 1)
                    two_back(act, product_done, b)
                    act.copy(t.turned[:, par, 0:D], t.ps[par][:, 0:D]).then_inc(turned_copied, 1)
            over_bins(act, step, lag=4)

        @block.sync
        def _(sp):
            load(sp, loads, loaded)
            store_bins(sp, t, t.x, D, D, d.x1, norm.normed, stored)


def dense1(nc, t, d):
    with ExitStack() as ctx:
        sem = sem_maker(nc, ctx, "d1")
        loads = [weights(nc, ctx, "Wl", d.WlT), weights(nc, ctx, "Wr", d.WrT), vector(nc, ctx, "bl", d.L1_gnn_b_l),
                 vector(nc, ctx, "gamma", d.L1_gnn_gamma), vector(nc, ctx, "beta", d.L1_gnn_beta)]
        Wl, Wr, bl, gamma, beta = (x[0] for x in loads)
        col_mean = ctx.enter_context(nc.sbuf_tensor("col_mean", [P, D], F32))
        col_var = ctx.enter_context(nc.sbuf_tensor("col_var", [P, D], F32))
        loaded = sem("loaded")
        inputs_ready = sem("inputs_ready")
        turned = sem("turned")
        turned_copied = sem("turned_copied")
        product_done = sem("product_done")
        biased = sem("biased")
        squares_ready = sem("squares_ready")
        length_ready = sem("length_ready")
        length_kept = sem("length_kept")
        inverse = sem("inverse")
        unit_ready = sem("unit_ready")
        columns_summed = sem("columns_summed")
        column_mean = sem("column_mean")
        centred = sem("centred")
        waited = sem("square_waited")
        squared = sem("squared")
        squares_summed = sem("squares_summed")
        column_var = sem("column_var")
        column_std = sem("column_std")
        gain = sem("gain")
        scaled = sem("scaled")
        shifted = sem("shifted")
        norm = norm_sems(sem)
        stored = sem("stored")
        block = ctx.enter_context(nc.Block())

        def row(b):
            return t.acc[:, bass.ds(b * W, D)]

        def column_sum(pe, bank, rows, b, signal):
            first = isinstance(b, int) and b == 0
            last = isinstance(b, int) and b == NB - 1
            pe.matmul(t.ps[bank][:, 0:D], t.real[:, int(last), :], rows, start=first, stop=last,
                      skip_group_check=True).then_inc(signal, 1)

        @block.vector
        def _(dve):
            dve.wait_ge(loaded, 80)

            def rows(b, par):
                if started(b):
                    two_back(dve, turned, b)
                    dve.tensor_scalar(t.work[:, par, 0:D], row(b), t.inv_deg[:, bass.ds(b, 1)], None, ALU.mult)
                    dve.tensor_scalar(t.work[:, par, D:2 * D], t.x[:, bass.ds(b * D, D)], 1.0, None,
                                      ALU.mult).then_inc(inputs_ready, 1)
                if started(b, 3):
                    o, q = b - 3, 1 - par
                    dve.wait_ge(product_done, o + 1)
                    two_back(dve, unit_ready, o)
                    dve.tensor_tensor(t.s1[:, q, :], t.ps[2 + q][:, 0:D], bl[:, :], ALU.add).then_inc(biased, 1)
                if started(b, 4):
                    o = b - 4
                    dve.wait_ge(length_ready, o + 1)
                    dve.tensor_scalar(t.rstd[:, par, :], t.std[:, par, :], 1e-12, None, ALU.max).then_inc(length_kept, 1)
                    dve.wait_ge(length_kept, o + 1)
                    dve.reciprocal(t.degree[:, par, :], t.rstd[:, par, :]).then_inc(inverse, 1)
                    dve.wait_ge(inverse, o + 1)
                    dve.tensor_scalar(row(o), t.s1[:, par, :], t.degree[:, par, :], None, ALU.mult).then_inc(unit_ready, 1)
            over_bins(dve, rows, lag=4)
            dve.wait_ge(columns_summed, NB)
            dve.tensor_scalar(col_mean[:, :], t.ps[4][:, 0:D], 1.0 / N, None, ALU.mult).then_inc(column_mean, 1)
            dve.wait_ge(column_mean, 1)

            def centre(b, par):
                dve.tensor_tensor(row(b), row(b), col_mean[:, :], ALU.subtract).then_inc(centred, 1)
            over_bins(dve, centre)
            dve.wait_ge(squares_summed, NB)
            dve.tensor_scalar(col_var[:, :], t.ps[5][:, 0:D], 1.0 / N, None, ALU.mult).then_inc(column_var, 1)
            dve.wait_ge(column_std, 1)
            dve.reciprocal(col_var[:, :], col_mean[:, :]).then_inc(gain, 1)
            dve.wait_ge(gain, 1)
            dve.tensor_tensor(col_mean[:, :], col_var[:, :], gamma[:, :], ALU.mult).then_inc(gain, 1)
            dve.wait_ge(gain, 2)

            def finish_rows(b, par):
                if started(b):
                    dve.tensor_tensor(t.s1[:, par, :], row(b), col_mean[:, :], ALU.mult).then_inc(scaled, 1)
                if started(b, 1):
                    norm_rstd(dve, t, norm, b - 1, 1 - par)
                if started(b):
                    dve.wait_ge(scaled, b + 1)
                    dve.tensor_tensor(t.work[:, par, 0:D], t.s1[:, par, :], beta[:, :], ALU.add).then_inc(shifted, 1)
                if started(b, 1):
                    norm_apply(dve, t, norm, b - 1, 1 - par, t.x[:, bass.ds((b - 1) * D, D)])
                if started(b):
                    dve.wait_ge(shifted, b + 1)
                    dve.scalar_tensor_tensor(out=t.s2[:, par, :], in0=t.work[:, par, 0:D], scalar=0.0,
                                             in1=t.x[:, bass.ds(b * D, D)], op0=ALU.max, op1=ALU.add
                                             ).then_inc(norm.summed, 1)
                    norm_stats(dve, t, norm, b, par)
                    norm_moments(dve, t, norm, b, par)
            over_bins(dve, finish_rows, lag=1)

        @block.tensor
        def _(pe):
            pe.wait_ge(loaded, 80)

            def rows(b, par):
                if started(b):
                    pe.wait_ge(inputs_ready, b + 1)
                    two_back(pe, turned_copied, b)
                    turn(pe, t, t.work[:, par, :], par, turned, 4)
                if started(b, 1):
                    o, q = b - 1, 1 - par
                    pe.wait_ge(turned_copied, o + 1)
                    if not isinstance(b, int) or o >= 2:
                        pe.wait_ge(biased, o - 1)
                    for c in range(4):
                        mm = pe.matmul(t.ps[2 + q][:, 0:D], t.turned[:, q, c * P:(c + 1) * P],
                                       (Wl, Wr)[c // 2][:, c % 2, :], start=c == 0, stop=c == 3)
                    mm.then_inc(product_done, 1)
                if started(b, 3):
                    pe.wait_ge(unit_ready, b - 2)
                    column_sum(pe, 4, row(b - 3), b - 3, columns_summed)
            over_bins(pe, rows, lag=3)

            def squares(b, par):
                pe.wait_ge(squared, b + 1)
                column_sum(pe, 5, t.s2[:, par, :], b, squares_summed)
            over_bins(pe, squares)

        @block.scalar
        def _(act):
            def rows(b, par):
                if started(b, 4):
                    o = b - 4
                    act.wait_ge(biased, o + 1)
                    act.activation(t.s2[:, par, :], t.s1[:, par, :], ACT.Square,
                                   accum_out=t.squares[:, par, :]).then_inc(squares_ready, 1)
                    act.wait_ge(squares_ready, o + 1)
                    act.sqrt(t.std[:, par, :], t.squares[:, par, :]).then_inc(length_ready, 1)
                if started(b):
                    act.wait_ge(turned, b + 1)
                    two_back(act, product_done, b)
                    act.copy(t.turned[:, par, :], t.ps[par][:, 0:2 * D]).then_inc(turned_copied, 1)
            over_bins(act, rows, lag=4)

            def squares(b, par):
                act.wait_ge(centred, b + 1)
                two_back(act, squares_summed, b)
                act.sem_inc(waited, 1)
                act.activation(t.s2[:, par, :], row(b), ACT.Square).then_inc(squared, 1)
            over_bins(act, squares)
            act.wait_ge(column_var, 1)
            act.activation(col_mean[:, :], col_var[:, :], ACT.Sqrt, bias=t.eps[:, :]).then_inc(column_std, 1)

            def finish_rows(b, par):
                norm_std(act, t, norm, b, par)
            over_bins(act, finish_rows)

        @block.sync
        def _(sp):
            load(sp, loads, loaded)
            store_bins(sp, t, t.x, D, D, d.x2, norm.normed, stored)


def project(nc, t, d, layer):
    with ExitStack() as ctx:
        sem = sem_maker(nc, ctx, f"p{layer}")
        loads = [weights(nc, ctx, f"{w}{layer}", dram[layer])
                 for w, dram in (("wq", d.L2_gnn_Wq), ("wk", d.L2_gnn_Wk), ("wv", d.L2_gnn_Wv))]
        wq, wk, wv = (x[0] for x in loads)
        kv = ctx.enter_context(nc.sbuf_tensor(f"kv_out{layer}", [P, 2, KV], F32))
        loaded = sem("weights_loaded")
        gap_ready = sem("gap_ready")
        input_ready = sem("input_ready")
        turned = sem("turned")
        turned_copied = sem("turned_copied")
        query_done = sem("query_done")
        kv_done = sem("kv_done")
        query_kept = sem("query_kept")
        kv_copied = sem("kv_copied")
        stored = [sem(f"stored{p}") for p in range(2)]
        block = ctx.enter_context(nc.Block())

        @block.vector
        def _(dve):
            dve.memset(kv[:, :, D:W], 0.0).then_inc(gap_ready, 1)

            def step(b, par):
                if started(b):
                    two_back(dve, turned, b)
                    dve.tensor_scalar(t.work[:, par, 0:D], t.x[:, bass.ds(b * D, D)], 1.0, None,
                                      ALU.mult).then_inc(input_ready, 1)
                if started(b, 1):
                    o, q = b - 1, 1 - par
                    dve.wait_ge(query_done, o + 1)
                    dve.tensor_scalar(t.q[:, bass.ds(o * D, D)], t.ps[2 + q][:, 0:D], 1.0, None,
                                      ALU.mult).then_inc(query_kept, 1)
            over_bins(dve, step, lag=1)

        @block.gpsimd
        def _(pool):
            pool.memset(t.acc[:, :], 0.0)

        @block.tensor
        def _(pe):
            pe.wait_ge(loaded, 48)

            def step(b, par):
                if started(b):
                    pe.wait_ge(input_ready, b + 1)
                    two_back(pe, turned_copied, b)
                    turn(pe, t, t.work[:, par, :], par, turned)
                if started(b, 1):
                    o, q = b - 1, 1 - par
                    pe.wait_ge(turned_copied, o + 1)
                    two_back(pe, query_kept, o)
                    for c in range(2):
                        mm = pe.matmul(t.ps[2 + q][:, 0:D], t.turned[:, q, c * P:(c + 1) * P], wq[:, c, :],
                                       start=c == 0, stop=c == 1)
                    mm.then_inc(query_done, 1)
                    two_back(pe, kv_copied, o)
                    for n, w in enumerate((wk, wv)):
                        for c in range(2):
                            mm = pe.matmul(t.ps[4 + q][:, n * D:(n + 1) * D], t.turned[:, q, c * P:(c + 1) * P],
                                           w[:, c, :], start=c == 0, stop=c == 1)
                    mm.then_inc(kv_done, 1)
            over_bins(pe, step, lag=1)

        @block.scalar
        def _(act):
            act.wait_ge(gap_ready, 1)

            def step(b, par):
                if started(b):
                    act.wait_ge(turned, b + 1)
                    two_back(act, kv_done, b)
                    act.copy(t.turned[:, par, 0:D], t.ps[par][:, 0:D]).then_inc(turned_copied, 1)
                if started(b, 1):
                    o, q = b - 1, 1 - par
                    act.wait_ge(kv_done, o + 1)
                    if not isinstance(o, int) or o >= 2:
                        act.wait_ge(stored[q], (o - q) * 8)
                    act.copy(kv[:, q, 0:D], t.ps[4 + q][:, 0:D])
                    act.copy(kv[:, q, W:KV], t.ps[4 + q][:, D:2 * D]).then_inc(kv_copied, 1)
            over_bins(act, step, lag=1)

        @block.sync
        def _(sp):
            load(sp, loads, loaded)

            def step(b, par):
                sp.wait_ge(kv_copied, b + 1)
                sp.dma_start(d.kv[bass.ds(b * P, P), :], kv[:, par, :]).then_inc(stored[par], 16)
            over_bins(sp, step)
            sp.wait_ge(stored[0], 16 * (NB - NB // 2))
            sp.wait_ge(stored[1], 16 * (NB // 2))


def attend(nc, t, d, layer):
    QUERY, PRODUCT, SCORE, MESSAGE, PART, SUM = G, G + 2, G + 3, 2 * G + 6, 2 * G + 7, 3 * G
    HG = G // 2
    with ExitStack() as ctx:
        sem = sem_maker(nc, ctx, f"at{layer}")

        def sb(name, shape):
            return ctx.enter_context(nc.sbuf_tensor(f"{name}{layer}", shape, F32))

        onehot = sb("edge_node", [P, SLOTS, G, P])
        onehot_t = sb("node_edge", [P, 2, HG, P])
        product = t.s1
        scores = sb("scores", [P, 2, G * H])
        below = sb("below", [P, 2, G * H])
        fresh = sb("fresh", [H, 2, G * P + 1])
        run_max = sb("run_max", [H, 2, G * P])
        seg_max = t.work[0:H, :, :].rearrange("p a b -> p (a b)")
        first_max = sb("first_max", [1, H])
        drop = sb("drop", [1, H])
        shrink = sb("shrink", [1, H])
        shrink_less_1 = sb("shrink_less_1", [1, H])

        index_copied = sem("index_copied")
        index_taken = sem("index_taken")
        gathered = [sem(f"gathered{s}") for s in range(SLOTS)]
        fresh_loaded = [sem(f"fresh_loaded{p}") for p in range(2)]
        distance_ready = sem("distance_ready")
        distance_free = sem("distance_free")
        onehot_ready = sem("onehot_ready")
        onehot_turned = sem("onehot_turned")
        onehot_t_copied = sem("onehot_t_copied")
        query_done = sem("query_done")
        product_ready = sem("product_ready")
        score_ready = sem("score_ready")
        score_turned = sem("score_turned")
        run_max_ready = sem("run_max_ready")
        seg_max_ready = sem("seg_max_ready")
        max_turned = sem("max_turned")
        below_ready = sem("below_ready")
        weight_ready = sem("weight_ready")
        first_kept = sem("first_kept")
        drop_ready = sem("drop_ready")
        shrink_ready = sem("shrink_ready")
        shrink_used = sem("shrink_used")
        spread_done = sem("spread_done")
        message_ready = sem("message_ready")
        rescaled = sem("rescaled")
        waited = sem("waited")
        part_done = sem("part_done")
        added = sem("added")
        block = ctx.enter_context(nc.Block())

        turned_bank = t.ps[0]
        score_bank = t.ps[5]
        weight = t.ps[6][:, 0:G * H]
        max_cols = t.ps[7][:, 0:G * H]
        old_max = t.ps[7][0:1, G * H:G * H + H]
        spread = t.ps[7][:, 256:256 + H]

        def in_loop(i):
            return not isinstance(i, int)

        def has_pair(k):
            return in_loop(k) or 0 <= k < K

        def has_batch(b):
            return in_loop(b) or 0 <= b < NBATCH

        def batch_of(i, j, lag):
            return i + (j - lag) // G

        def place(slot, j, lag):
            n = (slot * G + j - lag) % (SLOTS * G)
            return n // G, n % G

        @block.sync
        def _(sp):
            def step(i, slot):
                if in_loop(i) or i >= 2:
                    sp.wait_ge(seg_max_ready, i - 1)
                sp.dma_start(fresh[:, slot % 2, 0:G * P],
                             d.bias[bass.ds(i * G * P, G * P)].partition_broadcast(H)
                             ).then_inc(fresh_loaded[slot % 2], 16)
            over_batches(sp, step)

        @block.gpsimd
        def _(pool):
            def step(i, slot):
                if in_loop(i) or i >= SLOTS:
                    pool.wait_ge(part_done, (i - SLOTS + 1) * G)
                pool.tensor_copy(t.index[:, slot, :], t.src_i[:, bass.ds(i * G, G)]).then_inc(index_copied, 1)
                pool.wait_ge(index_copied, i + 1)
                pool.sem_inc(index_taken, 1)
                for j in range(G):
                    pool.indirect_dma_start(t.rows[:, slot, j, :], None, d.kv,
                                            bass.IndirectOffsetOnAxis(t.index[:, slot, j:j + 1], 0)
                                            ).then_inc(gathered[slot], 16)
            over_batches(pool, step)

        @block.tensor
        def _(pe):
            def turn_onehots(b, slot, half):
                pe.wait_ge(onehot_ready, 2 * b + half + 1)
                if in_loop(b) or 2 * b + half >= 1:
                    pe.wait_ge(onehot_t_copied, 2 * b + half)
                for j in range(HG):
                    mm = pe.transpose(turned_bank[:, j * P:(j + 1) * P], onehot[:, slot, half * HG + j, :],
                                      t.ident[:, :])
                mm.then_inc(onehot_turned, 1)

            def query(b, k, j):
                bin_ = pe.value_load(t.bins[0:1, bass.ds(k, 1)], min_val=0, max_val=NB - 1)
                if j % HG == 0:
                    pe.wait_ge(onehot_t_copied, 2 * b + j // HG + 1)
                if j % 2 == 0 and (in_loop(b) or k >= 4):
                    pe.wait_ge(product_ready, b * (G // 2) + j // 2 - 1)
                pe.matmul(t.ps[1 + j // 2 % 2][:, j % 2 * D:(j % 2 + 1) * D], onehot_t[:, j // HG, j % HG, :], t.q[:, bass.ds(bin_ * D, D)],
                          start=True, stop=True).then_inc(query_done, 1)

            def turn_scores(b, par, half):
                pe.wait_ge(score_ready, b * (G // 2) + (half + 1) * (HG // 2))
                if in_loop(b) or 2 * b + half >= 1:
                    pe.wait_ge(run_max_ready, 2 * b + half)
                for j in range(HG):
                    col = (half * HG + j) * H
                    mm = pe.transpose(score_bank[0:H, j * P:(j + 1) * P], scores[:, par, col:col + H], t.ident[:, :])
                mm.then_inc(score_turned, 1)

            def turn_max(b, par):
                pe.wait_ge(seg_max_ready, b + 1)
                if in_loop(b) or b >= 1:
                    pe.wait_ge(below_ready, b)
                if in_loop(b) or b >= 2:
                    pe.wait_ge(rescaled, b - 1)
                pe.sem_inc(waited, 1)
                for j in range(G):
                    mm = pe.transpose(max_cols[:, j * H:(j + 1) * H], seg_max[:, j * P:(j + 1) * P],
                                      t.ident[0:H, 0:H])
                if in_loop(b) or b >= 1:
                    mm = pe.transpose(old_max, run_max[:, 1 - par, G * P - 1:G * P], t.ident[0:H, 0:H])
                mm.then_inc(max_turned, 1)

            def spread_shrink(b, slot):
                pe.wait_ge(shrink_used, b)
                pe.matmul(spread, onehot[0:1, slot, 0, :], shrink_less_1[:, :], start=True,
                          stop=True).then_inc(spread_done, 1)

            def part(b, k, slot, j):
                if j % 2 == 0:
                    pe.wait_ge(message_ready, b * (G // 2) + j // 2 + 1)
                two_back(pe, added, k)
                pe.matmul(t.ps[3 + j % 2][:, 0:W], onehot[:, slot, j, :], t.rows[:, slot, j, 0:W],
                          start=True, stop=True).then_inc(part_done, 1)

            def step(i, slot):
                for j in range(G):
                    s = i * G + j
                    if j == 0 and has_batch(i - 1):
                        turn_onehots(i - 1, (slot - 1) % SLOTS, 1)
                    if j == HG and has_batch(i):
                        turn_onehots(i, slot, 0)
                    if has_pair(s - QUERY):
                        query(i - 1, s - QUERY, j)
                    if j == 2 and has_batch(i - 2):
                        turn_scores(i - 2, slot % 2, 1)
                    if j == HG + 2 and has_batch(i - 1):
                        turn_scores(i - 1, 1 - slot % 2, 0)
                    if j == 4 and has_batch(i - 2):
                        turn_max(i - 2, slot % 2)
                    if j == 7 and has_batch(i - 2) and (in_loop(i) or i >= 3):
                        spread_shrink(i - 2, (slot - 2) % SLOTS)
                    if has_pair(s - PART):
                        part(batch_of(i, j, PART), s - PART, *place(slot, j, PART))
            over_batches(pe, step, lag=3)

        @block.scalar
        def _(act):
            def find_onehot(i, k, slot, j):
                half = j // HG
                if j % HG == 0 and (in_loop(i) or i >= SLOTS):
                    act.wait_ge(part_done, k + HG - SLOTS * G)
                    act.sem_inc(distance_free, 1)
                act.activation(onehot[:, slot, j, :], t.node[:, :], ACT.Abs, scale=-1.0,
                               bias=t.dst_at[:, bass.ds(k, 1)]).then_inc(distance_ready, 1)
                if j % HG == HG - 1:
                    act.wait_ge(distance_ready, k + 1)
                    four = onehot[:, slot, half * HG:(half + 1) * HG, :]
                    act.activation(four, four, ACT.Relu, scale=-1.0, bias=1.0).then_inc(onehot_ready, 1)

            def copy_turned(b, half):
                act.wait_ge(onehot_turned, 2 * b + half + 1)
                if in_loop(b) or b >= 1:
                    act.wait_ge(query_done, (b - 1) * G + (half + 1) * HG)
                act.copy(onehot_t[:, half, :, :], turned_bank[:, :].rearrange("p (j n) -> p j n", j=HG)
                         ).then_inc(onehot_t_copied, 1)

            def find_weights(b, slot):
                par = slot % 2
                act.wait_ge(below_ready, b + 1)
                if in_loop(b) or b >= 1:
                    act.wait_ge(message_ready, b * (G // 2))
                act.activation(weight, below[:, par, :], ACT.Exp, scale=SCALE).then_inc(weight_ready, 1)
                z = t.rows[:, slot, :, 0:W].rearrange("p j (h e) -> p j h e", h=H)[:, :, :, DK]
                act.activation(z, below[:, par, :].rearrange("p (j h) -> p j h", j=G), ACT.Exp,
                               scale=SCALE).then_inc(weight_ready, 1)
                if in_loop(b) or b >= 1:
                    act.wait_ge(drop_ready, b)
                    if in_loop(b) or b >= 2:
                        act.wait_ge(shrink_used, b - 1)
                    act.activation(shrink[:, :], drop[:, :], ACT.Exp, scale=SCALE).then_inc(shrink_ready, 1)

            def step(i, slot):
                for j in range(G):
                    if j == 1 and has_batch(i - 1):
                        copy_turned(i - 1, 1)
                    if j == HG + 1 and has_batch(i):
                        copy_turned(i, 0)
                    if j == 5 and has_batch(i - 2):
                        find_weights(i - 2, (slot - 2) % SLOTS)
                    if has_batch(i):
                        find_onehot(i, i * G + j, slot, j)
            over_batches(act, step, lag=3)

        @block.vector
        def _(dve):
            for par in range(2):
                dve.memset(fresh[:, par, G * P:G * P + 1], 0.0)

            def multiply(b, k, slot, j):
                if j == 0:
                    dve.wait_ge(gathered[slot], (b - slot) * (16 * G // SLOTS) + 16 * G)
                dve.wait_ge(query_done, k + 2)
                if in_loop(b) or k >= 2:
                    dve.wait_ge(score_ready, b * (G // 2) + j // 2)
                queries = t.ps[1 + j // 2 % 2][:, :].rearrange("p (a n) -> p a n", a=2)
                dve.tensor_tensor(product[:, :, :], queries, t.rows[:, slot, j:j + 2, 0:D],
                                  ALU.mult).then_inc(product_ready, 1)

            def score(b, slot, j):
                dve.wait_ge(product_ready, b * (G // 2) + j // 2 + 1)
                if j == 0 and (in_loop(b) or b >= 2):
                    dve.wait_ge(below_ready, b - 1)
                dve.tensor_reduce(scores[:, slot % 2, j * H:(j + 2) * H],
                                  product[:, :, :].rearrange("p a (h e) -> p (a h) e", h=H), AX_X, ALU.add
                                  ).then_inc(score_ready, 1)

            half = G * P // 2

            def first_scan(b, par):
                dve.wait_ge(fresh_loaded[par], (b - par) * 8 + 16)
                dve.wait_ge(score_turned, 2 * b + 1)
                if in_loop(b) or b >= 1:
                    dve.wait_ge(max_turned, b)
                    dve.wait_ge(seg_max_ready, b)
                start = run_max[:, 1 - par, G * P - 1:G * P] if in_loop(b) or b >= 1 else -BIG
                dve.tensor_tensor_scan(run_max[:, par, 0:half], fresh[:, par, 0:half], score_bank[0:H, :], start,
                                       ALU.add, ALU.max).then_inc(run_max_ready, 1)

            def scans(b, par):
                dve.wait_ge(score_turned, 2 * b + 2)
                dve.wait_ge(run_max_ready, b * 2 + 1)
                dve.tensor_tensor_scan(run_max[:, par, half:2 * half], fresh[:, par, half:2 * half], score_bank[0:H, :],
                                       run_max[:, par, half - 1:half], ALU.add, ALU.max).then_inc(run_max_ready, 1)
                dve.wait_ge(run_max_ready, b * 2 + 2)
                dve.tensor_tensor_scan(seg_max[:, ::-1], fresh[:, par, 1:G * P + 1][:, ::-1],
                                       run_max[:, par, ::-1], -BIG, ALU.add, ALU.max).then_inc(seg_max_ready, 1)

            def compare(b, par):
                dve.wait_ge(max_turned, b + 1)
                if in_loop(b) or b >= 2:
                    dve.wait_ge(weight_ready, 2 * (b - 1))
                dve.tensor_tensor(below[:, par, :], scores[:, par, :], max_cols, ALU.subtract).then_inc(below_ready, 1)
                if in_loop(b) or b >= 1:
                    if in_loop(b) or b >= 2:
                        dve.wait_ge(drop_ready, b - 1)
                    dve.tensor_copy(first_max[:, :], max_cols[0:1, 0:H]).then_inc(first_kept, 1)

            def find_drop(b):
                dve.wait_ge(first_kept, b)
                if in_loop(b) or b >= 2:
                    dve.wait_ge(shrink_ready, b - 1)
                dve.tensor_tensor(drop[:, :], old_max, first_max[:, :], ALU.subtract).then_inc(drop_ready, 1)

            def less_1(b):
                dve.wait_ge(shrink_ready, b)
                if in_loop(b) or b >= 2:
                    dve.wait_ge(spread_done, b - 1)
                dve.tensor_scalar(shrink_less_1[:, :], shrink[:, :], 1.0, -1.0, ALU.min, ALU.add).then_inc(shrink_used, 1)

            def message(b, slot, j):
                if j == 0:
                    dve.wait_ge(weight_ready, 2 * (b + 1))
                pairs = t.rows[:, slot, j:j + 2, :]
                out = pairs[:, :, 0:W].rearrange("p a (h e) -> p a h e", h=H)[:, :, :, 0:DK]
                values = pairs[:, :, W:KV].rearrange("p a (h e) -> p a h e", h=H)
                w = weight[:, j * H:(j + 2) * H].rearrange("p (a h) -> p a h", a=2).unsqueeze(3)
                dve.tensor_tensor(out, values, w.to_broadcast([P, 2, H, DK]), ALU.mult).then_inc(message_ready, 1)

            def rescale(b, k, at):
                dve.wait_ge(spread_done, b)
                dve.wait_ge(added, k)
                heads = t.acc[:, bass.ds(at, W)].rearrange("p (h e) -> p h e", h=H)
                dve.scalar_tensor_tensor(out=heads, in0=spread.unsqueeze(2).to_broadcast([P, H, HZ]), scalar=1.0,
                                         in1=heads, op0=ALU.add, op1=ALU.mult).then_inc(rescaled, 1)

            def add(b, k, j, at):
                acc = t.acc[:, bass.ds(at, W)]
                if j == 0 and (in_loop(b) or b >= 1):
                    dve.wait_ge(rescaled, b)
                elif in_loop(k) or k >= 1:
                    dve.wait_ge(added, k)
                dve.wait_ge(part_done, k + 1)
                dve.tensor_tensor(acc, t.ps[3 + j % 2][:, 0:W], acc, ALU.add).then_inc(added, 1)

            def step(i, slot):
                for j in range(G):
                    s = i * G + j
                    if j == HG + 3 and has_batch(i - 1):
                        first_scan(i - 1, 1 - slot % 2)
                    if j == 3 and has_batch(i - 2):
                        scans(i - 2, slot % 2)
                    if j == 5 and has_batch(i - 2):
                        compare(i - 2, slot % 2)
                    if j % 2 == 0 and has_pair(s - PRODUCT):
                        multiply(batch_of(i, j, PRODUCT), s - PRODUCT, *place(slot, j, PRODUCT))
                    if has_pair(s - SUM):
                        at = dve.value_load(t.acc_at[0:1, bass.ds(s - SUM, 1)], min_val=0, max_val=(NB - 1) * W)
                    if j == SUM % G and has_pair(s - SUM) and (in_loop(i) or i >= 4):
                        rescale(batch_of(i, j, SUM), s - SUM, at)
                    if j % 2 == 0 and has_pair(s - MESSAGE):
                        message(batch_of(i, j, MESSAGE), *place(slot, j, MESSAGE))
                    if j % 2 == 1 and has_pair(s - SCORE):
                        score(batch_of(i, j, SCORE), *place(slot, j, SCORE))
                    if j == 5 and has_batch(i - 2) and (in_loop(i) or i >= 3):
                        find_drop(i - 2)
                    if j == 6 and has_batch(i - 2) and (in_loop(i) or i >= 3):
                        less_1(i - 2)
                    if has_pair(s - SUM):
                        add(batch_of(i, j, SUM), s - SUM, place(slot, j, SUM)[1], at)
            over_batches(dve, step, lag=3)


def after_attention(nc, t, d, layer):
    with ExitStack() as ctx:
        sem = sem_maker(nc, ctx, f"o{layer}")
        loads = [weights(nc, ctx, f"wo{layer}", d.L2_gnn_Wo[layer]), vector(nc, ctx, f"ln_g{layer}", d.L2_gnn_ln_g[layer]),
                 vector(nc, ctx, f"ln_b{layer}", d.L2_gnn_ln_b[layer])]
        wo, g, bb = (x[0] for x in loads)

        def sb(name, shape):
            return ctx.enter_context(nc.sbuf_tensor(f"{name}{layer}", shape, F32))

        total = sb("total", [P, 2, H])
        share = sb("share", [P, 2, H])
        loaded = sem("loaded")
        total_ready = sem("total_ready")
        share_ready = sem("share_ready")
        mean_ready = sem("mean_ready")
        turned = sem("turned")
        turned_copied = sem("turned_copied")
        product_done = sem("product_done")
        norm = norm_sems(sem)
        scaled = sem("scaled")
        finished = sem("finished")
        block = ctx.enter_context(nc.Block())

        @block.vector
        def _(dve):
            dve.wait_ge(loaded, 48)

            def step(b, par):
                o, q, a = b - 3, 1 - par, b - 4
                if started(b):
                    acc = t.acc[:, bass.ds(b * W, W)].rearrange("p (h e) -> p h e", h=H)
                    two_back(dve, share_ready, b)
                    dve.tensor_scalar(total[:, par, :], acc[:, :, DK], 1e-9, None, ALU.add).then_inc(total_ready, 1)
                if started(o):
                    dve.wait_ge(product_done, o + 1)
                    two_back(dve, norm.normed, o)
                    dve.tensor_tensor(t.s2[:, q, :], t.ps[2 + q][:, 0:D], t.x[:, bass.ds(o * D, D)], ALU.add
                                      ).then_inc(norm.summed, 1)
                if started(b):
                    dve.wait_ge(total_ready, b + 1)
                    two_back(dve, mean_ready, b)
                    dve.reciprocal(share[:, par, :], total[:, par, :]).then_inc(share_ready, 1)
                if started(o):
                    norm_stats(dve, t, norm, o, q)
                if started(b):
                    dve.wait_ge(share_ready, b + 1)
                    two_back(dve, turned, b)
                    dve.tensor_tensor(t.work[:, par, 0:D].rearrange("p (h e) -> p h e", h=H), acc[:, :, 0:DK],
                                      share[:, par, :].unsqueeze(2).to_broadcast([P, H, DK]), ALU.mult
                                      ).then_inc(mean_ready, 1)
                if started(a):
                    norm_rstd(dve, t, norm, a, par)
                if started(o):
                    norm_moments(dve, t, norm, o, q)
                if started(a):
                    two_back(dve, scaled, a)
                    norm_apply(dve, t, norm, a, par, t.s1[:, par, :])
                    dve.wait_ge(norm.normed, a + 1)
                    two_back(dve, finished, a)
                    dve.tensor_tensor(t.work[:, par, D:2 * D], t.s1[:, par, :], g[:, :], ALU.mult).then_inc(scaled, 1)
                    dve.wait_ge(scaled, a + 1)
                    dve.tensor_tensor(t.x[:, bass.ds(a * D, D)], t.work[:, par, D:2 * D], bb[:, :], ALU.add
                                      ).then_inc(finished, 1)
            over_bins(dve, step, lag=4)

        @block.tensor
        def _(pe):
            pe.wait_ge(loaded, 48)

            def step(b, par):
                if started(b):
                    pe.wait_ge(mean_ready, b + 1)
                    two_back(pe, turned_copied, b)
                    turn(pe, t, t.work[:, par, :], par, turned)
                if started(b, 1):
                    o, q = b - 1, 1 - par
                    pe.wait_ge(turned_copied, o + 1)
                    two_back(pe, norm.summed, o)
                    for c in range(2):
                        mm = pe.matmul(t.ps[2 + q][:, 0:D], t.turned[:, q, c * P:(c + 1) * P], wo[:, c, :],
                                       start=c == 0, stop=c == 1)
                    mm.then_inc(product_done, 1)
            over_bins(pe, step, lag=1)

        @block.scalar
        def _(act):
            def step(b, par):
                if started(b, 4):
                    norm_std(act, t, norm, b - 4, par)
                if started(b):
                    act.wait_ge(turned, b + 1)
                    two_back(act, product_done, b)
                    act.copy(t.turned[:, par, 0:D], t.ps[par][:, 0:D]).then_inc(turned_copied, 1)
            over_bins(act, step, lag=4)

        @block.sync
        def _(sp):
            load(sp, loads, loaded)


def mlp(nc, t, d):
    HC = HID // P
    with ExitStack() as ctx:
        sem = sem_maker(nc, ctx, "mlp")
        loads = [weights(nc, ctx, "mlp_w1", d.L2_gnn_w1), weights(nc, ctx, "mlp_w2", d.L2_gnn_w2),
                 vector(nc, ctx, "mlp_b2", d.L2_gnn_b2)]
        w1, w2, b2 = (x[0] for x in loads)
        b1 = ctx.enter_context(nc.sbuf_tensor("mlp_b1", [P, HC], F32))
        hidden = ctx.enter_context(nc.sbuf_tensor("hidden", [P, 2, HC, P], F32))
        before = ctx.enter_context(nc.sbuf_tensor("x_before", [P, 2, D], F32))
        loaded = sem("loaded")
        before_loaded = [sem(f"before_loaded{p}") for p in range(2)]
        input_ready = sem("input_ready")
        turned = sem("turned")
        turned_copied = sem("turned_copied")
        hidden_done = sem("hidden_done")
        hidden_ready = sem("hidden_ready")
        product_done = sem("product_done")
        biased = sem("biased")
        norm = norm_sems(sem)
        block = ctx.enter_context(nc.Block())

        @block.vector
        def _(dve):
            dve.wait_ge(loaded, 64)

            def step(b, par):
                if started(b):
                    two_back(dve, turned, b)
                    dve.tensor_scalar(t.work[:, par, 0:D], t.x[:, bass.ds(b * D, D)], 1.0, None,
                                      ALU.mult).then_inc(input_ready, 1)
                if started(b, 3):
                    o, q = b - 3, 1 - par
                    dve.wait_ge(product_done, o + 1)
                    two_back(dve, norm.summed, o)
                    dve.tensor_tensor(t.s1[:, q, :], t.ps[6 + q][:, 0:D], b2[:, :], ALU.add).then_inc(biased, 1)
                    dve.wait_ge(biased, o + 1)
                    dve.wait_ge(before_loaded[q], (o - q) * 8 + 16)
                    two_back(dve, norm.normed, o)
                    dve.tensor_tensor(t.s2[:, q, :], t.s1[:, q, :], before[:, q, :], ALU.add
                                      ).then_inc(norm.summed, 1)
                    norm_stats(dve, t, norm, o, q)
                if started(b, 4):
                    norm_rstd(dve, t, norm, b - 4, par)
                if started(b, 3):
                    norm_moments(dve, t, norm, b - 3, 1 - par)
                if started(b, 4):
                    norm_apply(dve, t, norm, b - 4, par, t.x[:, bass.ds((b - 4) * D, D)])
            over_bins(dve, step, lag=4)

        @block.gpsimd
        def _(pool):
            pool.memset(t.acc[:, :], 0.0)

        @block.tensor
        def _(pe):
            pe.wait_ge(loaded, 64)

            def step(b, par):
                if started(b):
                    pe.wait_ge(input_ready, b + 1)
                    two_back(pe, turned_copied, b)
                    turn(pe, t, t.work[:, par, :], par, turned)
                if started(b, 1):
                    o, q = b - 1, 1 - par
                    pe.wait_ge(turned_copied, o + 1)
                    two_back(pe, hidden_ready, o)
                    for j in range(HC):
                        for c in range(2):
                            mm = pe.matmul(t.ps[2 + 2 * q + j // 4][:, (j % 4) * P:(j % 4 + 1) * P],
                                           w1[:, c, j * P:(j + 1) * P], t.turned[:, q, c * P:(c + 1) * P],
                                           start=c == 0, stop=c == 1)
                    mm.then_inc(hidden_done, 1)
                if started(b, 2):
                    o = b - 2
                    pe.wait_ge(hidden_ready, o + 1)
                    two_back(pe, biased, o)
                    for j in range(HC):
                        mm = pe.matmul(t.ps[6 + par][:, 0:D], hidden[:, par, j, :], w2[:, j, :],
                                       start=j == 0, stop=j == HC - 1)
                    mm.then_inc(product_done, 1)
            over_bins(pe, step, lag=2)

        @block.scalar
        def _(act):
            act.wait_ge(loaded, 64)

            def step(b, par):
                if started(b):
                    act.wait_ge(turned, b + 1)
                    two_back(act, hidden_done, b)
                    act.copy(t.turned[:, par, 0:D], t.ps[par][:, 0:D]).then_inc(turned_copied, 1)
                if started(b, 1):
                    o, q = b - 1, 1 - par
                    act.wait_ge(hidden_done, o + 1)
                    two_back(act, product_done, o)
                    for j in range(HC):
                        ins = act.activation(hidden[:, q, j, :], t.ps[2 + 2 * q + j // 4][:, (j % 4) * P:(j % 4 + 1) * P],
                                             ACT.Relu, bias=b1[:, j:j + 1])
                    ins.then_inc(hidden_ready, 1)
                if started(b, 3):
                    norm_std(act, t, norm, b - 3, 1 - par)
            over_bins(act, step, lag=3)

        @block.sync
        def _(sp):
            load(sp, loads, loaded)
            sp.dma_start(b1[:, :], d.b1T).then_inc(loaded, 16)

            def step(b, par):
                two_back(sp, norm.summed, b)
                sp.dma_start(before[:, par, :], d.x2[bass.ds(b * P, P), :]).then_inc(before_loaded[par], 16)
            over_bins(sp, step)


def project3(nc, t, d):
    with ExitStack() as ctx:
        sem = sem_maker(nc, ctx, "p3")
        loads = [weights(nc, ctx, "w1", d.w1T), vector(nc, ctx, "w1_b", d.L3_gnn_w1_b)]
        w1, b1 = (x[0] for x in loads)
        loaded = sem("loaded")
        input_ready = sem("input_ready")
        turned = sem("turned")
        turned_copied = sem("turned_copied")
        product_done = sem("product_done")
        kept = sem("kept")
        stored = sem("stored")
        block = ctx.enter_context(nc.Block())

        @block.vector
        def _(dve):
            dve.wait_ge(loaded, 32)

            def step(b, par):
                if started(b):
                    two_back(dve, turned, b)
                    dve.tensor_scalar(t.work[:, par, 0:D], t.x[:, bass.ds(b * D, D)], 1.0, None,
                                      ALU.mult).then_inc(input_ready, 1)
                if started(b, 3):
                    o, q = b - 3, 1 - par
                    dve.wait_ge(product_done, o + 1)
                    dve.tensor_tensor(t.z[:, bass.ds(o * SUP, SUP)], t.ps[2 + q][:, 0:SUP], b1[:, :], ALU.add
                                      ).then_inc(kept, 1)
            over_bins(dve, step, lag=3)

        @block.tensor
        def _(pe):
            pe.wait_ge(loaded, 32)

            def step(b, par):
                if started(b):
                    pe.wait_ge(input_ready, b + 1)
                    two_back(pe, turned_copied, b)
                    turn(pe, t, t.work[:, par, :], par, turned)
                if started(b, 1):
                    o, q = b - 1, 1 - par
                    pe.wait_ge(turned_copied, o + 1)
                    two_back(pe, kept, o)
                    for c in range(2):
                        mm = pe.matmul(t.ps[2 + q][:, 0:SUP], t.turned[:, q, c * P:(c + 1) * P], w1[:, c, :],
                                       start=c == 0, stop=c == 1)
                    mm.then_inc(product_done, 1)
            over_bins(pe, step, lag=1)

        @block.scalar
        def _(act):
            def step(b, par):
                act.wait_ge(turned, b + 1)
                two_back(act, product_done, b)
                act.copy(t.turned[:, par, 0:D], t.ps[par][:, 0:D]).then_inc(turned_copied, 1)
            over_bins(act, step)

        @block.sync
        def _(sp):
            load(sp, loads, loaded)
            store_bins(sp, t, t.z, SUP, SUP, d.z, kept, stored)


def neighbour_sums(nc, t, d):
    LAG = 2 * G + G // 2
    BUFFERS = 2 * G
    assert LAG % COPIES == BUFFERS % COPIES == 0 and SLOTS * G % BUFFERS == 0
    with ExitStack() as ctx:
        sem = sem_maker(nc, ctx, "a3")

        def sb(name, shape):
            return ctx.enter_context(nc.sbuf_tensor(name, shape, F32))

        onehot_t = sb("node_edge", [P, 2, P])
        same = sb("same_source", [P, 2, P])
        ends = sb("z_at_destination", [P, 2, SUP])
        outgoing = sb("outgoing", [P, BUFFERS, SUP])
        column = sb("source_column", [P, 2, G])
        twin_count = sb("twin_count", [P, 2, G])
        detour = sb("detour", [P, 2, G])
        step_aside = sb("step_aside", [P, 2, G])
        target = ctx.enter_context(nc.sbuf_tensor("target_now", [P, SLOTS, G], I32))
        index_copied = sem("index_copied")
        index_taken = sem("index_taken")
        gathered = [sem(f"gathered{s}") for s in range(SLOTS)]
        sent = [sem(f"sent{r}") for r in range(COPIES)]
        column_ready = sem("column_ready")
        onehot_ready = sem("onehot_ready")
        turned = sem("turned")
        turned_copied = sem("turned_copied")
        row_ready = sem("row_ready")
        same_ready = sem("same_ready")
        twins_counted = sem("twins_counted")
        detour_ready = sem("detour_ready")
        aside_ready = sem("aside_ready")
        target_ready = sem("target_ready")
        ends_done = sem("ends_done")
        ends_copied = sem("ends_copied")
        merged = sem("merged")
        outgoing_ready = sem("outgoing_ready")
        part_done = sem("part_done")
        added = sem("added")
        block = ctx.enter_context(nc.Block())

        def in_loop(i):
            return not isinstance(i, int)

        def has_pair(k):
            return in_loop(k) or 0 <= k < K

        def batch_of(i, j, lag):
            return i + (j - lag) // G

        @block.gpsimd
        def _(pool):
            def step(i, slot):
                if in_loop(i) or i < NBATCH:
                    if in_loop(i) or i >= SLOTS:
                        pool.wait_ge(part_done, (i - SLOTS + 1) * G)
                    pool.tensor_copy(t.index[:, slot, :], t.src_i[:, bass.ds(i * G, G)]).then_inc(index_copied, 1)
                    pool.wait_ge(index_copied, i + 1)
                    pool.sem_inc(index_taken, 1)
                for j in range(G):
                    if in_loop(i) or i < NBATCH:
                        pool.indirect_dma_start(t.rows[:, slot, j, 0:SUP], None, d.z,
                                                bass.IndirectOffsetOnAxis(t.index[:, slot, j:j + 1], 0)
                                                ).then_inc(gathered[slot], 16)
                    k = i * G + j - LAG
                    if has_pair(k):
                        r = j % COPIES
                        if (j - LAG) % G == 0:
                            pool.wait_ge(target_ready, batch_of(i, j, LAG) + 1)
                        pool.wait_ge(outgoing_ready, k + 1)
                        pool.sem_inc(index_taken, 1)
                        if in_loop(k) or k >= COPIES:
                            pool.wait_ge(sent[r], i * (16 * G // COPIES) + 16 * ((j - LAG - r) // COPIES))
                            pool.sem_inc(index_taken, 1)
                        pool.indirect_dma_start(d.reversed[r], bass.IndirectOffsetOnAxis(
                            target[:, (slot * G + j - LAG) // G % SLOTS, (j - LAG) % G:(j - LAG) % G + 1], 0),
                            outgoing[:, (slot * G + j - LAG) % BUFFERS, :], None, compute_op=ALU.add).then_inc(sent[r], 16)
            over_batches(pool, step, lag=3)
            for r in range(COPIES):
                pool.wait_ge(sent[r], 16 * K // COPIES)

        @block.tensor
        def _(pe):
            def turn_both(i, k, slot, j):
                pe.wait_ge(onehot_ready, k + 1)
                two_back(pe, ends_copied, k)
                pe.transpose(t.ps[2 + j % 2][:, 0:P], t.onehot[:, j % 4, :], t.ident[:, :]).then_inc(turned, 1)
                pe.wait_ge(column_ready, i + 1)
                two_back(pe, twins_counted, k)
                pe.matmul(t.ps[4 + j % 2][:, 0:P], column[:, slot % 2, j:j + 1].to_broadcast([P, P]),
                          t.ident[:, :], start=True, stop=True).then_inc(row_ready, 1)

            def take_ends(k, j):
                b = pe.value_load(t.bins[0:1, bass.ds(k, 1)], min_val=0, max_val=NB - 1)
                pe.wait_ge(turned_copied, k + 1)
                pe.matmul(t.ps[2 + j % 2][:, P:P + SUP], onehot_t[:, j % 2, :], t.z[:, bass.ds(b * SUP, SUP)],
                          start=True, stop=True).then_inc(ends_done, 1)

            def merge(k, j):
                pe.wait_ge(ends_copied, k + 1)
                pe.wait_ge(same_ready, k + 1)
                two_back(pe, outgoing_ready, k)
                pe.matmul(t.ps[6 + j % 2][:, 0:SUP], same[:, j % 2, :], ends[:, j % 2, :],
                          start=True, stop=True).then_inc(merged, 1)

            def part(k, slot, j):
                two_back(pe, added, k)
                pe.matmul(t.ps[j % 2][:, 0:SUP], t.onehot[:, j % 4, :], t.rows[:, slot, j, 0:SUP],
                          start=True, stop=True).then_inc(part_done, 1)

            def step(i, slot):
                for j in range(G):
                    s = i * G + j
                    before, its_slot = batch_of(i, j, 1), (slot * G + j - 1) // G % SLOTS
                    if has_pair(s - 1):
                        turn_both(before, s - 1, its_slot, (j - 1) % G)
                        if j == 1:
                            pe.wait_ge(gathered[slot], (i - slot) * (16 * G // SLOTS) + 16 * G)
                        part(s - 1, its_slot, (j - 1) % G)
                    if has_pair(s - 2):
                        take_ends(s - 2, (j - 2) % G)
                    if has_pair(s - 3):
                        merge(s - 3, (j - 3) % G)
            over_batches(pe, step, lag=1)

        @block.scalar
        def _(act):
            def step(i, slot):
                for j in range(G):
                    k = i * G + j - 1
                    if has_pair(k):
                        act.wait_ge(turned, k + 1)
                        two_back(act, ends_done, k)
                        act.copy(onehot_t[:, (j - 1) % 2, :], t.ps[2 + (j - 1) % 2][:, 0:P]).then_inc(turned_copied, 1)
                    k = i * G + j - 2
                    if has_pair(k):
                        act.wait_ge(ends_done, k + 1)
                        two_back(act, merged, k)
                        act.copy(ends[:, j % 2, :], t.ps[2 + j % 2][:, P:P + SUP]).then_inc(ends_copied, 1)
                    k = i * G + j - 3
                    if has_pair(k):
                        act.wait_ge(merged, k + 1)
                        r = (j - 3) % COPIES
                        if in_loop(k) or k >= BUFFERS:
                            act.wait_ge(sent[r], (k - BUFFERS - r) * (16 // COPIES) + 16)
                        act.copy(outgoing[:, (slot * G + j - 3) % BUFFERS, :], t.ps[6 + (j - 3) % 2][:, 0:SUP]
                                 ).then_inc(outgoing_ready, 1)
            over_batches(act, step, lag=1)

        @block.vector
        def _(dve):
            def add(k, j):
                at = dve.value_load(t.acc_at[0:1, bass.ds(k, 1)], min_val=0, max_val=(NB - 1) * W)
                dve.wait_ge(part_done, k + 1)
                acc = t.acc[:, bass.ds(at, SUP)]
                if in_loop(k) or k >= 1:
                    dve.wait_ge(added, k)
                dve.tensor_tensor(acc, t.ps[j % 2][:, 0:SUP], acc, ALU.add).then_inc(added, 1)

            def count_twins(k, j, slot, its_j):
                dve.scalar_tensor_tensor(out=t.work[:, j % 2, 0:P], in0=t.ps[4 + j % 2][:, 0:P],
                                         scalar=column[:, slot % 2, its_j:its_j + 1], in1=t.lower[:, :],
                                         op0=ALU.is_equal, op1=ALU.mult,
                                         accum_out=twin_count[:, slot % 2, its_j:its_j + 1]).then_inc(twins_counted, 1)

            def find_targets(b, slot):
                par = slot % 2
                dve.wait_ge(column_ready, b + 1)
                dve.tensor_scalar(detour[:, par, :], column[:, par, :], -1.0, t.spare[:, :],
                                  ALU.mult, ALU.add).then_inc(detour_ready, 1)
                dve.wait_ge(detour_ready, b + 1)
                dve.wait_ge(twins_counted, (b + 1) * G)
                dve.scalar_tensor_tensor(out=step_aside[:, par, :], in0=twin_count[:, par, :], scalar=1.0,
                                         in1=detour[:, par, :], op0=ALU.min, op1=ALU.mult).then_inc(aside_ready, 1)
                dve.wait_ge(aside_ready, b + 1)
                if in_loop(b) or b >= SLOTS:
                    for r in range(COPIES):
                        dve.wait_ge(sent[r], (b - SLOTS + 1) * (16 * G // COPIES))
                dve.tensor_tensor(target[:, slot, :], step_aside[:, par, :], column[:, par, :], ALU.add
                                  ).then_inc(target_ready, 1)

            def step(i, slot):
                if has_pair(i * G):
                    if in_loop(i) or i >= 2:
                        dve.wait_ge(target_ready, i - 1)
                    dve.tensor_copy(column[:, slot % 2, :], t.src_at[:, bass.ds(i * G, G)]).then_inc(column_ready, 1)
                for j in range(G):
                    k = i * G + j
                    if has_pair(k):
                        if in_loop(k) or k >= 4:
                            dve.wait_ge(part_done, k - 3)
                            dve.wait_ge(turned, k - 3)
                        dve.tensor_scalar(t.onehot[:, j % 4, :], t.node[:, :], t.dst_at[:, bass.ds(k, 1)], None,
                                          ALU.is_equal).then_inc(onehot_ready, 1)
                    k = i * G + j - 2
                    if has_pair(k):
                        its_slot, its_j = (slot * G + j - 2) // G % SLOTS, (j - 2) % G
                        if its_j == 0:
                            dve.wait_ge(column_ready, batch_of(i, j, 2) + 1)
                        dve.wait_ge(row_ready, k + 1)
                        two_back(dve, merged, k)
                        dve.tensor_scalar(same[:, j % 2, :], t.ps[4 + j % 2][:, 0:P],
                                          column[:, its_slot % 2, its_j:its_j + 1], None,
                                          ALU.is_equal).then_inc(same_ready, 1)
                        count_twins(k, j, its_slot, its_j)
                        add(k, its_j)
                    if j == 2 and has_pair(i * G - 1):
                        find_targets(i - 1, (slot - 1) % SLOTS)
            over_batches(dve, step, lag=1)


def dense3(nc, t, d):
    with ExitStack() as ctx:
        sem = sem_maker(nc, ctx, "d3")
        loads = [weights(nc, ctx, "w0", d.w0T), vector(nc, ctx, "w0_b", d.L3_gnn_w0_b)]
        w0, b0 = (x[0] for x in loads)
        back = ctx.enter_context(nc.sbuf_tensor("back", [P, 2, COPIES, SUP], F32))
        loaded = sem("loaded")
        back_loaded = [sem(f"back_loaded{p}") for p in range(2)]
        input_ready = sem("input_ready")
        turned = sem("turned")
        turned_copied = sem("turned_copied")
        product_done = sem("product_done")
        biased = sem("biased")
        norm = norm_sems(sem)
        stored = sem("stored")
        block = ctx.enter_context(nc.Block())

        @block.vector
        def _(dve):
            dve.wait_ge(loaded, 32)

            def step(b, par):
                o, q, a = b - 3, 1 - par, b - 4
                if started(b):
                    two_back(dve, turned, b)
                    dve.tensor_scalar(t.work[:, par, 0:D], t.x[:, bass.ds(b * D, D)], 1.0, None,
                                      ALU.mult).then_inc(input_ready, 1)
                if started(o):
                    dve.wait_ge(product_done, o + 1)
                    two_back(dve, norm.summed, o)
                    dve.tensor_tensor(t.s1[:, q, :], t.ps[2 + q][:, 0:D], b0[:, :], ALU.add).then_inc(biased, 1)
                if started(o):
                    dve.wait_ge(biased, o + 1)
                    two_back(dve, norm.normed, o)
                    dve.tensor_tensor(t.s2[:, q, :], t.s1[:, q, :], t.x[:, bass.ds(o * D, D)], ALU.add
                                      ).then_inc(norm.summed, 1)
                if started(a):
                    norm_rstd(dve, t, norm, a, par)
                if started(o):
                    norm_stats(dve, t, norm, o, q)
                if started(a):
                    norm_apply(dve, t, norm, a, par, t.x[:, bass.ds(a * D, D)])
                if started(o):
                    norm_moments(dve, t, norm, o, q)
            over_bins(dve, step, lag=4)

        @block.tensor
        def _(pe):
            pe.wait_ge(loaded, 32)

            def step(b, par):
                if started(b):
                    pe.wait_ge(input_ready, b + 1)
                    two_back(pe, turned_copied, b)
                    turn(pe, t, t.work[:, par, :], par, turned)
                if started(b, 1):
                    o, q = b - 1, 1 - par
                    pe.wait_ge(turned_copied, o + 1)
                    two_back(pe, biased, o)
                    for c in range(2):
                        mm = pe.matmul(t.ps[2 + q][:, 0:D], t.turned[:, q, c * P:(c + 1) * P], w0[:, c, :],
                                       start=c == 0, stop=False, skip_group_check=True)
                    pe.wait_ge(back_loaded[q], (o - q) * (16 * COPIES // 2) + 16 * COPIES)
                    sums = [back[:, q, r, :] for r in range(COPIES)] + [t.acc[:, bass.ds(o * W, SUP)]]
                    for n, rows in enumerate(sums):
                        mm = pe.matmul(t.ps[2 + q][:, 0:SUP], t.ident[:, :], rows, start=False, stop=n == COPIES,
                                       skip_group_check=True)
                    mm.then_inc(product_done, 1)
            over_bins(pe, step, lag=1)

        @block.scalar
        def _(act):
            def step(b, par):
                if started(b, 4):
                    norm_std(act, t, norm, b - 4, par)
                if started(b):
                    act.wait_ge(turned, b + 1)
                    two_back(act, product_done, b)
                    act.copy(t.turned[:, par, 0:D], t.ps[par][:, 0:D]).then_inc(turned_copied, 1)
                if started(b, 4):
                    o = b - 4
                    act.wait_ge(norm.normed, o + 1)
                    rows = LAST if isinstance(b, int) and o == NB - 1 else P
                    act.dma_start(d.out[bass.ds(o * P, rows), :], t.x[0:rows, bass.ds(o * D, D)]).then_inc(stored, 16)
            over_bins(act, step, lag=4)
            act.wait_ge(stored, 16 * NB)

        @block.sync
        def _(sp):
            load(sp, loads, loaded)

            def step(b, par):
                two_back(sp, product_done, b)
                for r in range(COPIES):
                    sp.dma_start(back[:, par, r, :], d.reversed[r][bass.ds(b * P, P), :]
                                 ).then_inc(back_loaded[par], 16)
            over_bins(sp, step)


def program(nc, d):
    with ExitStack() as ctx:
        t = Named()

        t.ps = [ctx.enter_context(nc.psum_tensor(f"bank{i}", [P, 512], F32)) for i in range(8)]

        def sb(name, shape, dt=F32):
            return ctx.enter_context(nc.sbuf_tensor(name, shape, dt))

        t.x = sb("x", [P, NB * D])
        t.acc = sb("acc", [P, NB * W])
        t.rows = sb("rows", [P, SLOTS, G, KV])
        t.onehot = sb("onehot", [P, 4, P])
        t.ident = sb("ident", [P, P])
        t.lower = sb("lower", [P, P])
        t.node = sb("node", [P, P])
        t.real = sb("real", [P, 2, P])
        t.eps = sb("eps", [P, 1])
        t.spare = sb("spare", [P, 1])
        t.dst_at = sb("dst_at", [P, K])
        t.src_at = sb("src_at", [P, K])
        t.src_i = sb("src_idx", [P, K], I32)
        t.bins = sb("bins", [1, K], I32)
        t.acc_at = sb("acc_at", [1, K], I32)
        t.index = sb("index", [P, SLOTS, G], I32)
        t.degree = sb("degree", [P, 2, 1])
        t.inv_deg = sb("inv_deg", [P, NB])
        t.work = sb("work", [P, 2, 2 * D])
        t.turned = sb("turned", [P, 2, 2 * D])
        t.squares = sb("squares", [P, 2, 1])
        t.s1 = sb("s1", [P, 2, D])
        t.s2 = sb("s2", [P, 2, D])
        t.stats = sb("stats", [P, 2, 6])
        t.mv = sb("mv", [P, 2, 2])
        t.std = sb("std", [P, 2, 1])
        t.rstd = sb("rstd", [P, 2, 1])

        with ExitStack() as edges:
            t.dst_i, t.prev_i, t.src_now = (edges.enter_context(nc.sbuf_tensor(name, [P, CH, P], I32))
                                            for name in ("dst_now", "dst_before", "src_now"))
            t.ones = edges.enter_context(nc.sbuf_tensor("ones", [P, P], F32))
            t.unsorted = edges.enter_context(nc.sbuf_tensor("unsorted", [1, 1], I32))
            load_edges(nc, t, d)
            sort_edges(nc, t, d)
            build_tables(nc, t, d)
        aggregate(nc, t, d, "a0", d.x, D, 1)
        dense0(nc, t, d)
        aggregate(nc, t, d, "a1", d.x1, D, 0)
        dense1(nc, t, d)
        with nc.sbuf_tensor("queries", [P, NB * D], F32) as t.q:
            for layer in range(2):
                project(nc, t, d, layer)
                attend(nc, t, d, layer)
                after_attention(nc, t, d, layer)
        mlp(nc, t, d)
        with nc.sbuf_tensor("supports", [P, NB * SUP], F32) as t.z:
            project3(nc, t, d)
            neighbour_sums(nc, t, d)
        dense3(nc, t, d)


def kernel(**inputs):
    import numpy as np
    import concourse.bacc as bacc
    from concourse.bass_utils import run_bass_kernel_spmd as run

    nc = bacc.Bacc("TRN2", target_bir_lowering=False, num_devices=1)
    v = {name: np.asarray(a) for name, a in inputs.items()}
    arrays = {name: a for name, a in v.items()
              if name != "L2_gnn_b1" and (name.startswith("L2") or a.ndim == 1 and name[0] == "L")}
    arrays["x"] = np.concatenate([v["x"], np.zeros((NP - N, D), v["x"].dtype)])
    arrays["src"] = np.concatenate([v["src"], np.full(EC - E, NP - 1, v["src"].dtype)])
    arrays["dst"] = np.concatenate([np.full(1, -1, v["dst"].dtype), v["dst"], np.full(EC - E, NP - 1, v["dst"].dtype)])
    for name, w in (("W0T", "L0_gnn_W"), ("WlT", "L1_gnn_W_l"), ("WrT", "L1_gnn_W_r"), ("w0T", "L3_gnn_w0_w"),
                    ("w1T", "L3_gnn_w1_w")):
        arrays[name] = np.ascontiguousarray(v[w].T)
    arrays["b1T"] = np.ascontiguousarray(v["L2_gnn_b1"].reshape(-1, P).T)
    d = Named()

    def given(name):
        a = arrays[name]
        return nc.dram_tensor(f"in_{name}", a.shape, mybir.dt.from_np(a.dtype), kind="ExternalInput").ap()

    d.x, d.src, d.dst = given("x"), given("src"), given("dst")
    d.W0T, d.L0_gnn_b = given("W0T"), given("L0_gnn_b")
    d.WlT, d.WrT, d.L1_gnn_b_l = given("WlT"), given("WrT"), given("L1_gnn_b_l")
    d.L1_gnn_gamma, d.L1_gnn_beta = given("L1_gnn_gamma"), given("L1_gnn_beta")
    d.L2_gnn_Wq, d.L2_gnn_Wk, d.L2_gnn_Wv = given("L2_gnn_Wq"), given("L2_gnn_Wk"), given("L2_gnn_Wv")
    d.L2_gnn_Wo, d.L2_gnn_ln_g, d.L2_gnn_ln_b = given("L2_gnn_Wo"), given("L2_gnn_ln_g"), given("L2_gnn_ln_b")
    d.L2_gnn_w1, d.b1T, d.L2_gnn_w2, d.L2_gnn_b2 = given("L2_gnn_w1"), given("b1T"), given("L2_gnn_w2"), given("L2_gnn_b2")
    d.w0T, d.L3_gnn_w0_b, d.w1T, d.L3_gnn_w1_b = given("w0T"), given("L3_gnn_w0_b"), given("w1T"), given("L3_gnn_w1_b")

    def scratch(name, shape, dt=F32):
        return nc.dram_tensor(f"dram_{name}", shape, dt).ap()

    d.records = scratch("records", (1 + EC, 2), I32)
    d.keys = scratch("keys", (EC,))
    d.bias = scratch("segment_bias", (K * P,))
    d.reversed = [scratch(f"reversed{r}", (NP + P, SUP)) for r in range(COPIES)]
    d.x1 = scratch("x1", (NP, D))
    d.x2 = scratch("x2", (NP, D))
    d.kv = scratch("kv", (NP, KV))
    d.z = scratch("z", (NP, SUP))
    d.out = nc.dram_tensor("out", (N, D), F32, kind="ExternalOutput").ap()
    program(nc, d)
    got = run(nc, [{f"in_{name}": a for name, a in arrays.items()}], core_ids=[0])
    return got.results[0]["out"]
```
